# Optimizing a Trainium2 kernel written in Bass

```python
import numpy as np
import jax
import jax.numpy as jnp

def _softmax(x, axis=-1):
    return jax.nn.softmax(x, axis=axis)

def _gelu(x):
    return jax.nn.gelu(x, approximate=True)

def _silu(x):
    return jax.nn.silu(x)

def _sigmoid(x):
    return jax.nn.sigmoid(x)

def _layernorm(x, axis=-1, eps=1e-05):
    m = jnp.mean(x, axis=axis, keepdims=True)
    v = jnp.var(x, axis=axis, keepdims=True)
    return (x - m) / jnp.sqrt(v + eps)

def _scatter_add(tgt, idx, src, axis=0):
    return tgt.at[idx].add(src)

def _segment_sum(src, seg, n):
    return jax.ops.segment_sum(src, seg, n)
kernel_name = 'mk_gps_d1_gnn_r8_156441'

def setup_inputs(seed: int=0):
    np.random.seed(seed)
    _w = jnp.asarray

    def _rec_inputs():
        import jax
        import jax.numpy as jnp
        _gk = jax.random.key(seed)
        x = -0.0003713 + 1 * jax.random.normal(jax.random.fold_in(_gk, 1), (6250, 256), jnp.float32)
        _s = jax.random.randint(jax.random.fold_in(_gk, 2), (100000,), 0, 6250, jnp.int32)
        _d = jax.random.randint(jax.random.fold_in(_gk, 3), (100000,), 0, 6250, jnp.int32)
        _loop = jnp.arange(6250, dtype=jnp.int32)
        src = jnp.concatenate([_s, _d, _loop])
        dst = jnp.concatenate([_d, _s, _loop])
        _o = jnp.argsort(dst, stable=True)
        src = src[_o]
        dst = dst[_o]
        return (x, src, dst)
    x, src, dst = _rec_inputs()

    def _L0_gnn_setup():
        import jax, jax.numpy as jnp
        import numpy as np
        N, E, H, D = (6250, 100000, 4, 64)
        IN_DIM = H * D
        NEG_SLOPE = 0.2
        key = jax.random.key(seed)
        k = jax.random.split(key, 7)
        h = jax.random.normal(k[0], (N, IN_DIM), dtype=jnp.float32)
        W = jax.random.normal(k[1], (IN_DIM, H * D), dtype=jnp.float32) * (1.0 / np.sqrt(IN_DIM))
        attn_l = jax.random.normal(k[2], (H, D), dtype=jnp.float32) * 0.1
        attn_r = jax.random.normal(k[3], (H, D), dtype=jnp.float32) * 0.1
        bias = jnp.zeros((H * D,), dtype=jnp.float32)
        src = jax.random.randint(k[4], (E,), 0, N, dtype=jnp.int32)
        dst = jax.random.randint(k[5], (E,), 0, N, dtype=jnp.int32)
        return {'h': h, 'W': W, 'attn_l': attn_l, 'attn_r': attn_r, 'bias': bias, 'src': src, 'dst': dst}
    _L0_gnn_all = _L0_gnn_setup()
    _L0_gnn_in = {k: v for k, v in _L0_gnn_all.items() if k in ('W', 'attn_l', 'attn_r', 'bias')}
    del _L0_gnn_all

    def _L0_mix_setup():
        import jax, jax.numpy as jnp
        import numpy as np
        D_MODEL = 256
        NHEAD = 8
        D_HEAD = D_MODEL // NHEAD
        DIM_FF = 1024
        B, L = (4, 2048)
        LN_EPS = 1e-05

        def _layernorm(x, g, b):
            mu = jnp.mean(x, axis=-1, keepdims=True)
            var = jnp.mean((x - mu) ** 2, axis=-1, keepdims=True)
            return (x - mu) * jax.lax.rsqrt(var + LN_EPS) * g + b

        def _phi(x):
            return jnp.where(x > 0, x + 1.0, jnp.exp(x))
        key = jax.random.key(seed)
        ks = jax.random.split(key, 16)
        s_in = 1.0 / np.sqrt(D_MODEL)
        s_ff = 1.0 / np.sqrt(DIM_FF)
        inp = {'x': jax.random.normal(ks[0], (B, L, D_MODEL), dtype=jnp.float32), 'Wq': jax.random.normal(ks[1], (D_MODEL, D_MODEL), dtype=jnp.float32) * s_in, 'bq': jnp.zeros((D_MODEL,), jnp.float32), 'Wk': jax.random.normal(ks[2], (D_MODEL, D_MODEL), dtype=jnp.float32) * s_in, 'bk': jnp.zeros((D_MODEL,), jnp.float32), 'Wv': jax.random.normal(ks[3], (D_MODEL, D_MODEL), dtype=jnp.float32) * s_in, 'bv': jnp.zeros((D_MODEL,), jnp.float32), 'Wo': jax.random.normal(ks[4], (D_MODEL, D_MODEL), dtype=jnp.float32) * s_in, 'bo': jnp.zeros((D_MODEL,), jnp.float32), 'W1': jax.random.normal(ks[5], (D_MODEL, DIM_FF), dtype=jnp.float32) * s_in, 'b1': jnp.zeros((DIM_FF,), jnp.float32), 'W2': jax.random.normal(ks[6], (DIM_FF, D_MODEL), dtype=jnp.float32) * s_ff, 'b2': jnp.zeros((D_MODEL,), jnp.float32), 'ln1_g': jnp.ones((D_MODEL,), jnp.float32), 'ln1_b': jnp.zeros((D_MODEL,), jnp.float32), 'ln2_g': jnp.ones((D_MODEL,), jnp.float32), 'ln2_b': jnp.zeros((D_MODEL,), jnp.float32)}
        return inp
    _L0_mix_all = _L0_mix_setup()
    _L0_mix_in = {k: v for k, v in _L0_mix_all.items() if k in ('Wq', 'bq', 'Wk', 'bk', 'Wv', 'bv', 'Wo', 'bo', 'W1', 'b1', 'W2', 'b2', 'ln1_g', 'ln1_b', 'ln2_g', 'ln2_b')}
    del _L0_mix_all

    def _L0_ffn_setup():
        import jax, jax.numpy as jnp
        import numpy as np
        E, D, H, TOP_K = (6, 256, 256, 2)
        ROUTER_H = D // 2
        key = jax.random.key(seed)
        ks = jax.random.split(key, 12)
        s = 1.0 / np.sqrt(D)
        sh = 1.0 / np.sqrt(H)
        sr = 1.0 / np.sqrt(ROUTER_H)
        return {'features': jax.random.normal(ks[0], (8, 512, D), dtype=jnp.float32), 'router_w1': jax.random.uniform(ks[1], (D, ROUTER_H), jnp.float32, -s, s), 'router_b1': jnp.zeros((ROUTER_H,), jnp.float32), 'router_w2': jax.random.uniform(ks[2], (ROUTER_H, E), jnp.float32, -sr, sr), 'router_b2': jnp.zeros((E,), jnp.float32), 'expert_w1': jax.random.uniform(ks[3], (E, D, H), jnp.float32, -s, s), 'expert_b1': jnp.zeros((E, H), jnp.float32), 'expert_w2': jax.random.uniform(ks[4], (E, H, H), jnp.float32, -sh, sh), 'expert_b2': jnp.zeros((E, H), jnp.float32), 'expert_w3': jax.random.uniform(ks[5], (E, H, D), jnp.float32, -sh, sh), 'expert_b3': jnp.zeros((E, D), jnp.float32)}
    _L0_ffn_all = _L0_ffn_setup()
    _L0_ffn_in = {k: v for k, v in _L0_ffn_all.items() if k in ('router_w1', 'router_b1', 'router_w2', 'router_b2', 'expert_w1', 'expert_b1', 'expert_w2', 'expert_b2', 'expert_w3', 'expert_b3')}
    del _L0_ffn_all
    return {'x': x, 'src': src, 'dst': dst, 'L0_gnn_W': _L0_gnn_in['W'], 'L0_gnn_attn_l': _L0_gnn_in['attn_l'], 'L0_gnn_attn_r': _L0_gnn_in['attn_r'], 'L0_gnn_bias': _L0_gnn_in['bias'], 'L0_mix_Wq': _L0_mix_in['Wq'], 'L0_mix_bq': _L0_mix_in['bq'], 'L0_mix_Wk': _L0_mix_in['Wk'], 'L0_mix_bk': _L0_mix_in['bk'], 'L0_mix_Wv': _L0_mix_in['Wv'], 'L0_mix_bv': _L0_mix_in['bv'], 'L0_mix_Wo': _L0_mix_in['Wo'], 'L0_mix_bo': _L0_mix_in['bo'], 'L0_mix_W1': _L0_mix_in['W1'], 'L0_mix_b1': _L0_mix_in['b1'], 'L0_mix_W2': _L0_mix_in['W2'], 'L0_mix_b2': _L0_mix_in['b2'], 'L0_mix_ln1_g': _L0_mix_in['ln1_g'], 'L0_mix_ln1_b': _L0_mix_in['ln1_b'], 'L0_mix_ln2_g': _L0_mix_in['ln2_g'], 'L0_mix_ln2_b': _L0_mix_in['ln2_b'], 'L0_ffn_router_w1': _L0_ffn_in['router_w1'], 'L0_ffn_router_b1': _L0_ffn_in['router_b1'], 'L0_ffn_router_w2': _L0_ffn_in['router_w2'], 'L0_ffn_router_b2': _L0_ffn_in['router_b2'], 'L0_ffn_expert_w1': _L0_ffn_in['expert_w1'], 'L0_ffn_expert_b1': _L0_ffn_in['expert_b1'], 'L0_ffn_expert_w2': _L0_ffn_in['expert_w2'], 'L0_ffn_expert_b2': _L0_ffn_in['expert_b2'], 'L0_ffn_expert_w3': _L0_ffn_in['expert_w3'], 'L0_ffn_expert_b3': _L0_ffn_in['expert_b3']}

def reference(x, src, dst, L0_gnn_W, L0_gnn_attn_l, L0_gnn_attn_r, L0_gnn_bias, L0_mix_Wq, L0_mix_bq, L0_mix_Wk, L0_mix_bk, L0_mix_Wv, L0_mix_bv, L0_mix_Wo, L0_mix_bo, L0_mix_W1, L0_mix_b1, L0_mix_W2, L0_mix_b2, L0_mix_ln1_g, L0_mix_ln1_b, L0_mix_ln2_g, L0_mix_ln2_b, L0_ffn_router_w1, L0_ffn_router_b1, L0_ffn_router_w2, L0_ffn_router_b2, L0_ffn_expert_w1, L0_ffn_expert_b1, L0_ffn_expert_w2, L0_ffn_expert_b2, L0_ffn_expert_w3, L0_ffn_expert_b3):
    import jax
    import jax.numpy as jnp

    def _L0_gnn_ref(h, W, attn_l, attn_r, bias, src, dst):
        import jax, jax.numpy as jnp
        import numpy as np
        N, E, H, D = (6250, 100000, 4, 64)
        IN_DIM = H * D
        NEG_SLOPE = 0.2
        feat = (h @ W).reshape(N, H, D)
        el = jnp.einsum('nhd,hd->nh', feat, attn_l)
        er = jnp.einsum('nhd,hd->nh', feat, attn_r)
        e = jax.nn.leaky_relu(el[src] + er[dst], NEG_SLOPE)
        emax = jax.ops.segment_max(e, dst, num_segments=N)
        ex = jnp.exp(e - emax[dst])
        denom = jax.ops.segment_sum(ex, dst, num_segments=N)
        alpha = ex / denom[dst]
        msg = feat[src] * alpha[..., None]
        rst = jax.ops.segment_sum(msg, dst, num_segments=N)
        rst = rst + bias.reshape(1, H, D)
        out = jax.nn.elu(rst.reshape(N, H * D))
        return h + out

    def _L0_mix_ref(x, Wq, bq, Wk, bk, Wv, bv, Wo, bo, W1, b1, W2, b2, ln1_g, ln1_b, ln2_g, ln2_b):
        import jax, jax.numpy as jnp
        import numpy as np
        D_MODEL = 256
        NHEAD = 8
        D_HEAD = D_MODEL // NHEAD
        DIM_FF = 1024
        B, L = (4, 2048)
        LN_EPS = 1e-05

        def _layernorm(x, g, b):
            mu = jnp.mean(x, axis=-1, keepdims=True)
            var = jnp.mean((x - mu) ** 2, axis=-1, keepdims=True)
            return (x - mu) * jax.lax.rsqrt(var + LN_EPS) * g + b

        def _phi(x):
            return jnp.where(x > 0, x + 1.0, jnp.exp(x))
        Bq, Lq, _ = x.shape
        q = (x @ Wq + bq).reshape(Bq, Lq, NHEAD, D_HEAD)
        k = (x @ Wk + bk).reshape(Bq, Lq, NHEAD, D_HEAD)
        v = (x @ Wv + bv).reshape(Bq, Lq, NHEAD, D_HEAD)
        q_phi = _phi(q)
        k_phi = _phi(k)
        kv = jnp.einsum('blhd,blhe->bhde', k_phi, v)
        k_sum = k_phi.sum(axis=1)
        z = 1.0 / (jnp.einsum('blhd,bhd->blh', q_phi, k_sum) + 1e-06)
        out = jnp.einsum('blhd,bhde,blh->blhe', q_phi, kv, z)
        out = out.reshape(Bq, Lq, D_MODEL) @ Wo + bo
        x = _layernorm(x + out, ln1_g, ln1_b)
        ff = jax.nn.relu(x @ W1 + b1) @ W2 + b2
        x = _layernorm(x + ff, ln2_g, ln2_b)
        return x

    def _L0_ffn_ref(features, router_w1, router_b1, router_w2, router_b2, expert_w1, expert_b1, expert_w2, expert_b2, expert_w3, expert_b3):
        import jax, jax.numpy as jnp
        import numpy as np
        E, D, H, TOP_K = (6, 256, 256, 2)
        ROUTER_H = D // 2
        rh = jax.nn.relu(features @ router_w1 + router_b1)
        expert_logits = jax.nn.softmax(rh @ router_w2 + router_b2, axis=-1)
        top_w, top_i = jax.lax.top_k(expert_logits, TOP_K)
        routing_weights = jax.nn.softmax(top_w, axis=-1)
        h1 = jax.nn.relu(jnp.einsum('bsd,edh->bseh', features, expert_w1) + expert_b1)
        h2 = jax.nn.relu(jnp.einsum('bseh,ehf->bsef', h1, expert_w2) + expert_b2)
        expert_out = jnp.einsum('bsef,efo->bseo', h2, expert_w3) + expert_b3
        sel = jnp.take_along_axis(expert_out, top_i[:, :, :, None], axis=2)
        combined = jnp.sum(sel * routing_weights[..., None], axis=2)
        return combined
    xn = _layernorm(x, axis=-1)
    x = x + _L0_gnn_ref(xn, L0_gnn_W, L0_gnn_attn_l, L0_gnn_attn_r, L0_gnn_bias, src, dst) + _L0_mix_ref(xn[None], L0_mix_Wq, L0_mix_bq, L0_mix_Wk, L0_mix_bk, L0_mix_Wv, L0_mix_bv, L0_mix_Wo, L0_mix_bo, L0_mix_W1, L0_mix_b1, L0_mix_W2, L0_mix_b2, L0_mix_ln1_g, L0_mix_ln1_b, L0_mix_ln2_g, L0_mix_ln2_b)[0]
    x = x + _L0_ffn_ref(_layernorm(x, axis=-1)[None], L0_ffn_router_w1, L0_ffn_router_b1, L0_ffn_router_w2, L0_ffn_router_b2, L0_ffn_expert_w1, L0_ffn_expert_b1, L0_ffn_expert_w2, L0_ffn_expert_b2, L0_ffn_expert_w3, L0_ffn_expert_b3)[0]
    return x

_drawn_inputs = setup_inputs


def setup_inputs(seed=0):
    import zlib

    import numpy as np

    out = dict(_drawn_inputs(seed))
    spreads = {'L0_gnn_bias': (0.0, 0.1),
     'L0_mix_bq': (0.0, 0.8),
     'L0_mix_bk': (0.0, 0.8),
     'L0_mix_bv': (0.0, 0.1),
     'L0_mix_bo': (0.0, 0.1),
     'L0_mix_b1': (0.0, 0.381),
     'L0_mix_b2': (0.0, 0.275),
     'L0_mix_ln1_g': (1.0, 0.2),
     'L0_mix_ln1_b': (0.0, 0.1),
     'L0_mix_ln2_g': (1.0, 0.2),
     'L0_mix_ln2_b': (0.0, 0.1),
     'L0_ffn_router_b1': (0.0, 0.609),
     'L0_ffn_router_b2': (0.0, 0.397),
     'L0_ffn_expert_b1': (0.0, 0.8),
     'L0_ffn_expert_b2': (0.0, 0.8),
     'L0_ffn_expert_b3': (0.0, 0.317)}
    factors = {'L0_gnn_attn_r': 4.18,
     'L0_mix_Wq': 8.0,
     'L0_mix_Wk': 8.0,
     'L0_mix_Wv': 8.0,
     'L0_ffn_expert_w1': 3.24,
     'L0_ffn_expert_w2': 2.769}
    for name, (base, spread) in spreads.items():
        noise = np.random.default_rng([zlib.crc32(name.encode()), seed]).standard_normal(out[name].shape)
        drawn = base * np.exp(spread * noise) if base else spread * noise
        out[name] = jnp.asarray(drawn.astype(out[name].dtype))
    for name, factor in factors.items():
        out[name] = (out[name] * factor).astype(out[name].dtype)
    return out
```

```python
from contextlib import ExitStack

import concourse.bass as bass
from concourse import mybir

N, D, E, H, HD = 6250, 256, 206250, 4, 64
P = 125
NT = N // P
TE = 128
PAIR = 2
NP = -(-E // (TE * PAIR))
EPAD = NP * PAIR * TE
BATCH = 4
BODY = 4
SLOTS = BATCH * BODY
SB = BATCH // PAIR
ROUNDS = -(-(NP + NT) * PAIR // SLOTS)
CH = -(-(ROUNDS * SLOTS // PAIR + 4) // 128)
ROW = D + H
NCB = NT + 1
MH, MD = 8, 32
FF = 1024
RH = 128
NE = 6
MT = 2
NJ = NT // MT
EPS = 1e-5
AU = 5
HALF = NP // 2
KV_ROUNDS = NT // 2
SITES = ["g0", "g1", "g2", "g3", "aggr", "norm0", "norm1", "rows", "max0", "max1", "index0", "index1"]
WLOADS = 27
TAB_LINKS = 2 + 1 + 2 * CH + 6 + 8
ATT_LINKS = 2
assert N == NT * P and NP == 2 * HALF and NT % AU == 0 and KV_ROUNDS + NT - 1 <= ROUNDS


class Chain:

    def __init__(self, engine, semaphore):
        self.engine, self.semaphore, self.base, self.n = engine, semaphore, 0, 0

    def start(self, base):
        self.base, self.n = base, 0

    def __call__(self, instruction):
        self.n += 1
        instruction.then_inc(self.semaphore, 1)
        self.engine.wait_ge(self.semaphore, self.base + self.n)


def gps_layer(nc, x, src, dst, gW, attn_l, attn_r, gbias, Wq, bq, Wk, bk, Wv, bv, Wo, bo, W1, b1, W2, b2,
              g1, be1, g2, be2, rw1, rb1, rw2, rb2, ew1, eb1, ew2, eb2, ew3, eb3, out):
    fp32, bf16, i32, u32 = mybir.dt.float32, mybir.dt.bfloat16, mybir.dt.int32, mybir.dt.uint32
    ALU = mybir.AluOpType
    ACT = mybir.ActivationFunctionType
    AX = mybir.AxisListType.X
    ds = bass.ds

    feat_d = nc.dram_tensor("feat_d", (N, ROW), fp32, kind="Internal").ap()
    xn_d = nc.dram_tensor("xn_d", (N, D), fp32, kind="Internal").ap()
    xT_d = nc.dram_tensor("xT_d", (NT * 128, 2 * P), fp32, kind="Internal").ap()
    base_d = nc.dram_tensor("base_d", (N, D), fp32, kind="Internal").ap()
    blk_d = nc.dram_tensor("blk_d", (1, CH * 128), i32, kind="Internal").ap()
    src2 = src.rearrange("(t e) -> t e", e=PAIR * TE)
    dst2 = dst.rearrange("(t e) -> t e", e=PAIR * TE)

    ctx, tables, early, mixer, experts = ExitStack(), ExitStack(), ExitStack(), ExitStack(), ExitStack()
    with ctx:
        def sb(name, shape, dt=fp32, where=ctx):
            return where.enter_context(nc.sbuf_tensor(name, shape, dt))

        def sem(name):
            return ctx.enter_context(nc.semaphore(name))

        ident = sb("ident", [128, 128])
        ones = sb("ones", [128, 128])
        zero = sb("zero", [128, ROW])
        iota = sb("iota", [128, P])
        eps = sb("eps", [128, 1])
        wext = sb("wext", [128, 2, D + 2 * H])
        wkv = sb("wkv", [128, 2, 2 * D])
        wq = sb("wq", [128, 2, D])
        wo = sb("wo", [128, 2, D])
        w1 = sb("w1", [128, 2, FF])
        w2 = sb("w2", [128, 8, D])
        r1 = sb("r1", [128, 2, RH])
        r2 = sb("r2", [128, NE])
        x1 = sb("x1", [128, NE, 2, D])
        x2 = sb("x2", [128, NE, 2, D])
        x3 = sb("x3", [128, NE, 2, D])
        e3b = sb("e3b", [NE, D])
        rows = sb("rows", [128, 9, D])
        BK, BV, BO, B2, G1, E1, G2, E2, GB = range(9)
        rb2r = sb("rb2r", [128, NE])
        bqc = sb("bqc", [128, 2])
        b1c = sb("b1c", [128, 8])
        rb1c = sb("rb1c", [128, 1])
        eb1c = sb("eb1c", [128, NE, 2])
        eb2c = sb("eb2c", [128, NE, 2])
        srct = sb("srct", [128, CH * 128, PAIR], i32)
        dstt = sb("dstt", [128, CH * 128, PAIR])
        blk = sb("blk", [1, CH * 128 + SB], i32)
        nodes = sb("nodes", [P, NCB, 2 * H])
        nodep = sb("nodep", [P, 3, NCB * 2 * H], bf16)
        acc = sb("acc", [P, NCB * ROW])
        turn = sb("turn", [1, len(SITES)])
        kvbd = sb("kvbd", [128, 2, 128 + H])
        first = sb("first", [1, NP], i32, tables)
        pos = sb("pos", [1, 2, NP], fp32, tables)
        step = sb("step", [128, CH], fp32, tables)
        below = sb("below", [128, HALF], fp32, tables)
        sg = sb("sg", [128, 2, PAIR * TE], i32, tables)
        dg = sb("dg", [128, 2, PAIR * TE], i32, tables)
        sf = sb("sf", [128, PAIR * TE], fp32, tables)
        df = sb("df", [128, PAIR * TE], fp32, tables)
        lr = sb("lr", [128, 2, D], fp32, tables)
        prod = sb("prod", [128, 2, D], fp32, tables)
        tables.close()
        G = sb("G", [128, SLOTS, ROW])
        idx = sb("idx", [128, SLOTS], i32)
        S = sb("S", [128, 2, BATCH, P])
        ST = sb("ST", [128, 2, BATCH * TE], bf16)
        arg = sb("arg", [128, 3, BATCH, H])
        xin = sb("xin", [P, AU, D], fp32, early)
        xn = sb("xn", [P, AU, D], fp32, early)
        xT = sb("xT", [128, AU, 2 * P], fp32, early)
        fe = sb("fe", [P, AU, ROW + H], fp32, early)
        stat = sb("stat", [P, AU, 6], fp32, early)
        mv = sb("mv", [P, AU, 2], fp32, early)
        rstd = sb("rstd", [P, 2, AU], fp32, early)
        count = sb("count", [128, 2, CH], fp32, early)
        tpair = sb("tpair", [128, 4, CH], fp32, early)
        tpi = sb("tpi", [128, 2, CH], i32, early)
        ntmp = sb("ntmp", [P, 2, NCB * 2 * H], fp32, early)
        gmax = sb("gmax", [128, 16], fp32, early)
        early.close()
        kb = sb("kb", [P, 2, D], fp32, mixer)
        ke = sb("ke", [P, 2, D], fp32, mixer)
        vb = sb("vb", [P, 2, 2, 128 + 1], fp32, mixer)
        xm = sb("xm", [128, 2, 2 * P], fp32, mixer)
        xr = sb("xr", [P, 2, D], fp32, mixer)
        xx = sb("xx", [P, D], fp32, mixer)
        qb = sb("qb", [128, 2, P], fp32, mixer)
        qe = sb("qe", [128, 2, P], fp32, mixer)
        at = sb("at", [P, D], fp32, mixer)
        aT = sb("aT", [128, 2, P], fp32, mixer)
        res = sb("res", [P, 2, D], fp32, mixer)
        y = sb("y", [P, D], fp32, mixer)
        yT = sb("yT", [128, 2, P], fp32, mixer)
        hT = sb("hT", [128, 8, P], fp32, mixer)
        ob = sb("ob", [P, D], fp32, mixer)
        zs = sb("zs", [P, 64], fp32, mixer)
        mixer.close()
        mb = sb("mb", [P, MT, D], fp32, experts)
        mx = sb("mx", [P, 2, MT, D], fp32, experts)
        mf = sb("mf", [P, MT, D], fp32, experts)
        me = sb("me", [P, MT, D], fp32, experts)
        mfT = sb("mfT", [128, 2, 2, MT * P], fp32, experts)
        mrh = sb("mrh", [128, MT * P], fp32, experts)
        mw = sb("mw", [P, MT, 16, 8], fp32, experts)
        mi = sb("mi", [P, MT, 8], u32, experts)
        wt = sb("wt", [P, 2, MT, NE], fp32, experts)
        wtT = sb("wtT", [NE, MT, P], fp32, experts)
        h1 = sb("h1", [128, 2, 2, MT * P], fp32, experts)
        h2 = sb("h2", [128, 2, 2, MT * P], fp32, experts)
        experts.close()

        bank = [ctx.enter_context(nc.psum_tensor(f"bank{i}", [128, 512], fp32)) for i in range(8)]

        s_turn = [sem(f"s_turn_{name}") for name in SITES]
        s_const = sem("s_const")
        s_vconst = sem("s_vconst")
        s_wload = sem("s_wload")
        s_gload = sem("s_gload")
        s_first = sem("s_first")
        s_tab = sem("s_tab")
        s_pos = sem("s_pos")
        s_tpe = sem("s_tpe")
        s_tix = sem("s_tix")
        s_tg = [sem(f"s_tg{i}") for i in range(2)]
        s_tf = sem("s_tf")
        s_tt = sem("s_tt")
        s_tc = sem("s_tc")
        s_blk = sem("s_blk")
        s_xin = [sem(f"s_xin{i}") for i in range(AU)]
        s_mv = sem("s_mv")
        s_sd = sem("s_sd")
        s_xn = sem("s_xn")
        s_xns = [sem(f"s_xns{i}") for i in range(AU)]
        s_ach = sem("s_ach")
        s_xt = sem("s_xt")
        s_xte = sem("s_xte")
        s_xts = [sem(f"s_xts{i}") for i in range(AU)]
        s_f = sem("s_f")
        s_fe = sem("s_fe")
        s_nd = sem("s_nd")
        s_nch = sem("s_nch")
        s_gm = sem("s_gm")
        s_nt = sem("s_nt")
        s_idx = [sem(f"s_idx{i}") for i in range(BODY)]
        s_g = [sem(f"s_g{i}") for i in range(BODY)]
        s_S = sem("s_S")
        s_st = sem("s_st")
        s_ste = sem("s_ste")
        s_er = sem("s_er")
        s_zch = sem("s_zch")
        s_arg = sem("s_arg")
        s_w = sem("s_w")
        s_msg = sem("s_msg")
        s_sum = sem("s_sum")
        s_acc = sem("s_acc")
        s_kx = [sem(f"s_kx{i}") for i in range(2)]
        s_kmm = [sem(f"s_kmm{i}") for i in range(2)]
        s_kb = sem("s_kb")
        s_km = sem("s_km")
        s_ke = sem("s_ke")
        s_kp = sem("s_kp")
        s_ka = [sem(f"s_ka{i}") for i in range(2)]
        s_kch = sem("s_kch")
        s_kv = sem("s_kv")
        s_kbd = sem("s_kbd")
        s_xm = sem("s_xm")
        s_xr = sem("s_xr")
        s_pq = sem("s_pq")
        s_qb = sem("s_qb")
        s_qm = sem("s_qm")
        s_qe = sem("s_qe")
        s_qp = sem("s_qp")
        s_pa = sem("s_pa")
        s_at = sem("s_at")
        s_pT = sem("s_pT")
        s_aT = sem("s_aT")
        s_po = sem("s_po")
        s_res = sem("s_res")
        s_mv1 = sem("s_mv1")
        s_sd1 = sem("s_sd1")
        s_y = sem("s_y")
        s_fy = sem("s_fy")
        s_yT = sem("s_yT")
        s_fh = sem("s_fh")
        s_h = sem("s_h")
        s_fw = sem("s_fw")
        s_r2 = sem("s_r2")
        s_mv2 = sem("s_mv2")
        s_sd2 = sem("s_sd2")
        s_o = sem("s_o")
        s_os = sem("s_os")
        s_lch = sem("s_lch")
        s_rch = sem("s_rch")
        s_r2ch = sem("s_r2ch")
        s_mch = sem("s_mch")
        m_b = sem("m_b")
        m_em = sem("m_em")
        m_ee = sem("m_ee")
        m_x = sem("m_x")
        m_mv = sem("m_mv")
        m_sd = sem("m_sd")
        m_f = sem("m_f")
        m_fT = sem("m_fT")
        m_fe = sem("m_fe")
        m_r = sem("m_r")
        m_rr = sem("m_rr")
        m_l = sem("m_l")
        m_lm = sem("m_lm")
        m_le = sem("m_le")
        m_d = sem("m_d")
        m_de = sem("m_de")
        m_wt = sem("m_wt")
        m_wT = sem("m_wT")
        m_we = sem("m_we")
        m_bb = sem("m_bb")
        m_c = sem("m_c")
        m_s = sem("m_s")
        m_h1 = sem("m_h1")
        m_h1r = sem("m_h1r")
        m_h2 = sem("m_h2")
        m_h2r = sem("m_h2r")
        m_o = sem("m_o")
        m_oa = sem("m_oa")
        m_st = sem("m_st")
        m_ch = sem("m_ch")

        block = ctx.enter_context(nc.Block())

        def settle(engine, site, times):
            n, done = SITES.index(site), s_turn[SITES.index(site)]
            if site[0] == "g":
                engine.wait_ge(done, times)
                engine.tensor_tensor(turn[0:1, n:n + 1], zero[0:1, 0:1], zero[0:1, 1:2], ALU.add).then_inc(done, 1)
            else:
                engine.wait_ge(done, times)
                engine.memset(turn[0:1, n:n + 1], 0.0).then_inc(done, 1)

        @block.sync
        def _(sp):
            with nc.allow_non_contiguous_dma("first destination of each pair, biases by partition"):
                sp.dma_start(first[:, :], dst2[:, 0:1].rearrange("t e -> e t")).then_inc(s_first, 16)
            gl = [(wext[:, :, 0:D], gW.rearrange("(c p) n -> p c n", p=128)),
                  (lr[:, 0, :], attn_l.rearrange("h d -> (h d)").partition_broadcast(128)),
                  (lr[:, 1, :], attn_r.rearrange("h d -> (h d)").partition_broadcast(128))]
            for to, of in gl:
                sp.dma_start(to, of).then_inc(s_gload, 16)

            def load_x(t, u):
                sp.dma_start(xin[:, u, :], x[ds(t * P, P), :]).then_inc(s_xin[u], 16)

            for u in range(AU):
                load_x(u, u)
            sp.wait_ge(s_tix, 1)
            with nc.allow_non_contiguous_dma("steps from partitions to a row"):
                sp.dma_start(blk_d[0, :].rearrange("(c p) -> p c", p=128), tpi[:, 1, :]).then_inc(s_blk, 16)
            sp.wait_ge(s_blk, 16)
            sp.dma_start(blk[:, SB:], blk_d[:, :]).then_inc(s_blk, 16)

            def store_xn(i, u):
                sp.wait_ge(s_xn, i * AU + u + 1)
                sp.dma_start(xn_d[ds((i * AU + u) * P, P), :], xn[:, u, :]).then_inc(s_xns[u], 16)

            with sp.Fori(0, NT // AU - 1) as i:
                for u in range(AU):
                    store_xn(i, u)
                    load_x((i + 1) * AU + u, u)
            for u in range(AU):
                store_xn(NT // AU - 1, u)

            wl = [(wkv[:, :, 0:D], Wk.rearrange("(c p) n -> p c n", p=128)),
                  (wkv[:, :, D:2 * D], Wv.rearrange("(c p) n -> p c n", p=128))]
            wl += [(rows[:, n, :], v.partition_broadcast(128)) for n, v in
                   enumerate([bk, bv, bo, b2, g1, be1, g2, be2, gbias])]
            wl += [(wq[:, :, :], Wq.rearrange("(c p) n -> p c n", p=128)),
                   (wo[:, :, :], Wo.rearrange("(c p) n -> p c n", p=128)),
                   (w1[:, :, :], W1.rearrange("(c p) n -> p c n", p=128)),
                   (w2[:, :, :], W2.rearrange("(c p) n -> p c n", p=128)),
                   (r1[:, :, :], rw1.rearrange("(c p) n -> p c n", p=128)),
                   (r2[:, :], rw2), (e3b[:, :], eb3),
                   (rb2r[:, :], rb2.partition_broadcast(128)),
                   (x1[:, :, :, :], ew1.rearrange("e (c p) n -> p e c n", p=128)),
                   (x2[:, :, :, :], ew2.rearrange("e (c p) n -> p e c n", p=128)),
                   (x3[:, :, :, :], ew3.rearrange("e (c p) n -> p e c n", p=128))]
            nl = [(bqc[:, :], bq.rearrange("(c p) -> p c", p=128)),
                  (b1c[:, :], b1.rearrange("(c p) -> p c", p=128)),
                  (rb1c[:, :], rb1.rearrange("(c p) -> p c", p=128)),
                  (eb1c[:, :, :], eb1.rearrange("e (c p) -> p e c", p=128)),
                  (eb2c[:, :, :], eb2.rearrange("e (c p) -> p e c", p=128))]
            assert len(wl) + len(nl) == WLOADS
            for to, of in wl:
                sp.dma_start(to, of).then_inc(s_wload, 16)
            with nc.allow_non_contiguous_dma("biases by partition"):
                for to, of in nl:
                    sp.dma_start(to, of).then_inc(s_wload, 16)

            for u in range(AU):
                sp.wait_ge(s_xts[u], 32 * (NT // AU))
                sp.wait_ge(s_xns[u], 16 * (NT // AU))
            sp.wait_ge(s_nt, 1)
            with sp.Fori(0, KV_ROUNDS) as i:
                for u in range(2):
                    sp.wait_ge(s_kmm[u], i)
                    sp.dma_start(xm[:, u, :], xT_d[ds((i * 2 + u) * 128, 128), :]).then_inc(s_kx[u], 16)
            sp.wait_ge(s_kmm[0], KV_ROUNDS)

            def load_xm(m):
                sp.wait_ge(s_pq, m)
                sp.dma_start(xm[:, 0, :], xT_d[ds(m * 128, 128), :]).then_inc(s_xm, 16)

            def load_xr(m):
                sp.wait_ge(s_res, m)
                sp.dma_start(xr[:, 0, :], xn_d[ds(m * P, P), :]).then_inc(s_xr, 16)
                sp.dma_start(xr[:, 1, :], x[ds(m * P, P), :]).then_inc(s_xr, 16)

            def store_base(m):
                sp.wait_ge(s_o, m + 1)
                sp.dma_start(base_d[ds(m * P, P), :], ob[:, :]).then_inc(s_os, 16)

            load_xm(0)
            load_xr(0)
            load_xm(1)
            load_xr(1)
            with sp.Fori(0, NT - 2) as i:
                load_xm(i + 2)
                store_base(i)
                load_xr(i + 2)
            store_base(NT - 2)
            store_base(NT - 1)
            sp.wait_ge(s_os, 16 * NT)

            def load_base(j):
                sp.wait_ge(m_x, j)
                sp.dma_start(mb[:, :, :], base_d[ds(j * MT * P, MT * P), :].rearrange("(s p) n -> p s n", p=P)
                             ).then_inc(m_b, 16)

            def store_out(j):
                sp.wait_ge(m_oa, MT * NE * (j + 1))
                sp.dma_start(out[ds(j * MT * P, MT * P), :].rearrange("(s p) n -> p s n", p=P), mx[:, 1, :, :]
                             ).then_inc(m_st, 16)

            load_base(0)
            load_base(1)
            with sp.Fori(0, NJ - 2) as j:
                store_out(j)
                load_base(j + 2)
            store_out(NJ - 2)
            store_out(NJ - 1)
            sp.wait_ge(m_st, 16 * NJ)

        @block.gpsimd
        def _(pool):
            pool.memset(ident[:, :], 0.0).then_inc(s_const, 1)
            pool.wait_ge(s_const, 1)
            pool.affine_select(out=ident[:, :], in_=ident[:, :], compare_op=ALU.not_equal, fill=1.0, base=0,
                               pattern=[[-1, 128]], channel_multiplier=1).then_inc(s_const, 1)
            pool.iota(iota[:, :], [[1, P]], base=0, channel_multiplier=0,
                      allow_small_or_imprecise_dtypes=True).then_inc(s_const, 1)
            pool.iota(pos[:, 1, :], [[1, NP]], base=0, channel_multiplier=0,
                      allow_small_or_imprecise_dtypes=True).then_inc(s_const, 1)
            pool.iota(step[:, :], [[128, CH]], base=0, channel_multiplier=1,
                      allow_small_or_imprecise_dtypes=True).then_inc(s_const, 1)
            pool.wait_ge(s_tix, 1)
            for c in range(CH):
                if c >= 2:
                    pool.wait_ge(s_tf, c - 1)
                at_pair = bass.IndirectOffsetOnAxis(ap=tpi[:, 0, c:c + 1], axis=0)
                pool.indirect_dma_start(sg[:, c % 2, :], None, src2, at_pair).then_inc(s_tg[c % 2], 16)
                pool.indirect_dma_start(dg[:, c % 2, :], None, dst2, at_pair).then_inc(s_tg[c % 2], 16)
            pool.wait_ge(s_vconst, 1)
            for u in range(AU):
                pool.wait_ge(s_xts[u], 32 * (NT // AU))

            def gather(bt, k):
                pool.wait_ge(s_idx[bt], k + 1)
                settle(pool, f"g{bt}", k)
                for j in range(bt * BATCH, (bt + 1) * BATCH):
                    pool.indirect_dma_start(G[:, j, :], None, feat_d,
                                            bass.IndirectOffsetOnAxis(ap=idx[:, j:j + 1], axis=0)
                                            ).then_inc(s_g[bt], 16)

            for bt in range(BODY):
                gather(bt, 0)
            with pool.Fori(0, ROUNDS - 1) as k:
                for bt in range(BODY):
                    pool.wait_ge(s_sum, SB * (k * BODY + bt + 2))
                    gather(bt, k + 1)

        @block.scalar
        def _(act):
            with act.Fori(0, NT // AU) as i:
                act.wait_ge(s_mv, i + 1)
                act.activation(rstd[:, 0, :], mv[:, :, 1], ACT.Sqrt, bias=eps[0:P, :]).then_inc(s_sd, 1)
                for u in range(AU):
                    t = i * AU + u
                    act.wait_ge(s_xt, t + 1)
                    act.wait_ge(s_xts[u], i * 32)
                    if u == 0:
                        act.wait_ge(s_f, i * AU)
                    act.activation(xT[:, u, :], bank[4 + u % 2][:, 0:2 * P], ACT.Copy).then_inc(s_xte, 1)
                    act.wait_ge(s_xte, t + 1)
                    act.dma_start(xT_d[ds(t * 128, 128), :], xT[:, u, :]).then_inc(s_xts[u], 16)
                    act.wait_ge(s_f, t + 1)
                    act.wait_ge(s_nd, i * AU)
                    act.activation(fe[:, u, :], bank[6 + u % 2][0:P, 0:ROW + H], ACT.Copy).then_inc(s_fe, 1)
                    act.wait_ge(s_fe, t + 1)
                    act.dma_start(feat_d[ds(t * P, P), :], fe[:, u, 0:ROW]).then_inc(s_xts[u], 16)

            def indices(bt, k):
                act.activation(idx[:, bt * BATCH:(bt + 1) * BATCH],
                               srct[:, ds(k * (SLOTS // PAIR) + bt * SB, SB), :].rearrange("p s u -> p (s u)"),
                               ACT.Copy).then_inc(s_idx[bt], 1)

            def transposes_out(n, par):
                act.wait_ge(s_st, n + 1)
                act.activation(ST[0:P, par, :], bank[0][0:P, :], ACT.Copy).then_inc(s_ste, 1)

            act.wait_ge(s_tc, CH)
            for bt in range(BODY):
                indices(bt, 0)
            transposes_out(0, 0)

            def edges(k, bt):
                n = k * BODY + bt
                act.wait_ge(s_arg, n + 1)
                act.activation(G[:, bt * BATCH:(bt + 1) * BATCH, D:ROW], arg[:, 2, :, :], ACT.Exp
                               ).then_inc(s_w, 1)
                act.wait_ge(s_er, n)
                transposes_out(n + 1, (bt + 1) % 2)
                indices(bt, k + 1)

            def keys(i, u):
                act.wait_ge(s_km, i * 2 + u + 1)
                act.activation(ke[:, u, :], ke[:, u, :], ACT.Exp).then_inc(s_ke, 1)

            with act.Fori(0, KV_ROUNDS) as i:
                for bt in range(BODY):
                    edges(i, bt)
                    if bt < 2:
                        keys(i, bt)

            act.wait_ge(s_wload, 16 * WLOADS)

            def queries_in(m):
                act.wait_ge(s_pq, m + 1)
                act.wait_ge(s_pa, m)
                for c in range(2):
                    last = act.activation(qb[:, c, :], bank[5][:, c * P:(c + 1) * P], ACT.Identity,
                                          bias=bqc[:, c:c + 1])
                last.then_inc(s_qb, 1)
                act.wait_ge(s_qm, m + 1)
                act.activation(qe[:, :, :], qe[:, :, :], ACT.Exp).then_inc(s_qe, 1)

            def attention_T(m):
                act.wait_ge(s_pT, m + 1)
                act.wait_ge(s_po, m)
                act.activation(aT[:, :, :].rearrange("p c n -> p (c n)"), bank[4][:, 0:2 * P], ACT.Copy
                               ).then_inc(s_aT, 1)

            def deviation(mean_var, done, m, column):
                act.wait_ge(mean_var, m + 1)
                act.activation(zs[:, column + 2:column + 3], zs[:, column + 1:column + 2], ACT.Sqrt,
                               bias=eps[0:P, :]).then_inc(done, 1)

            def norm_T(m):
                act.wait_ge(s_fy, m + 1)
                act.wait_ge(s_fh, m * 2)
                act.activation(yT[:, :, :].rearrange("p c n -> p (c n)"), bank[4][:, 0:2 * P], ACT.Copy
                               ).then_inc(s_yT, 1)

            def hidden(m, half):
                act.wait_ge(s_fh, m * 2 + half + 1)
                if half == 0:
                    act.wait_ge(s_fw, m)
                for c in range(4):
                    ch = half * 4 + c
                    last = act.activation(hT[:, ch, :], bank[6 + half][:, c * P:(c + 1) * P], ACT.Relu,
                                          bias=b1c[:, ch:ch + 1])
                last.then_inc(s_h, 1)

            queries_in(0)
            attention_T(0)
            deviation(s_mv1, s_sd1, 0, 16)
            with act.Fori(0, NT - 1) as i:
                edges(i + KV_ROUNDS, 0)
                norm_T(i)
                queries_in(i + 1)
                edges(i + KV_ROUNDS, 1)
                hidden(i, 0)
                edges(i + KV_ROUNDS, 2)
                hidden(i, 1)
                attention_T(i + 1)
                edges(i + KV_ROUNDS, 3)
                deviation(s_mv2, s_sd2, i, 24)
                deviation(s_mv1, s_sd1, i + 1, 16)
            norm_T(NT - 1)
            hidden(NT - 1, 0)
            hidden(NT - 1, 1)
            deviation(s_mv2, s_sd2, NT - 1, 24)
            with act.Fori(KV_ROUNDS + NT - 1, ROUNDS) as k:
                for bt in range(BODY):
                    edges(k, bt)

            def elu_exp(j, s):
                act.wait_ge(m_em, j * MT + s + 1)
                act.activation(me[:, s, :], me[:, s, :], ACT.Exp).then_inc(m_ee, 1)

            def row_deviations(j):
                act.wait_ge(m_mv, j + 1)
                act.activation(mw[:, :, 1, 0:1], mw[:, :, 0, 1:2], ACT.Sqrt, bias=eps[0:P, :]).then_inc(m_sd, 1)

            def rows_T(j):
                act.wait_ge(m_fT, j + 1)
                act.wait_ge(m_c, j)
                act.activation(mfT[:, 0, :, :].rearrange("p c n -> p (c n)"), bank[0][:, 0:2 * MT * P],
                               ACT.Copy).then_inc(m_fe, 1)

            def router_hidden(j):
                act.wait_ge(m_r, j + 1)
                act.activation(mrh[:, :], bank[1][:, 0:MT * P], ACT.Relu, bias=rb1c[:, :]).then_inc(m_rr, 1)

            def router_exps(j):
                act.wait_ge(m_lm, j + 1)
                act.activation(mw[:, :, 3, 0:NE], mw[:, :, 2, 0:NE], ACT.Exp).then_inc(m_le, 1)
                act.wait_ge(m_d, j + 1)
                act.activation(mw[:, :, 8, 0:1], mw[:, :, 7, 0:1], ACT.Exp).then_inc(m_de, 1)

            def weights_T(j):
                act.wait_ge(m_wT, j + 1)
                act.wait_ge(m_bb, j)
                act.activation(wtT[:, :, :], bank[2][0:NE, 128:128 + MT * P].rearrange("p (s n) -> p s n", s=MT),
                               ACT.Copy).then_inc(m_we, 1)

            def place(j):
                act.wait_ge(m_fe, j + 1)
                act.wait_ge(m_h1, j * NE)
                act.activation(mfT[:, 1, :, :], mfT[:, 0, :, :], ACT.Copy).then_inc(m_c, 1)

            def relus(j, e, which):
                done, to, at_bank, bias, done_r, read = (
                    (m_h1, h1, 3, eb1c, m_h1r, m_h2) if which == 1 else (m_h2, h2, 4, eb2c, m_h2r, m_o))
                act.wait_ge(done, j * NE + e + 1)
                for c in range(2):
                    last = act.activation(to[:, e % 2, c, :], bank[at_bank][:, c * MT * P:(c + 1) * MT * P],
                                          ACT.Relu, bias=bias[:, e, c:c + 1])
                last.then_inc(done_r, 1)

            def tile_of_experts(j, ahead):
                place(j)
                relus(j, 0, 1)
                for e in range(NE):
                    if e + 1 < NE:
                        relus(j, e + 1, 1)
                    relus(j, e, 2)
                    if ahead:
                        if e == 0:
                            for s in range(MT):
                                elu_exp(j + 1, s)
                        if e == 1:
                            row_deviations(j + 1)
                        if e == 2:
                            rows_T(j + 1)
                        if e == 3:
                            router_hidden(j + 1)
                        if e == 4:
                            router_exps(j + 1)
                        if e == 5:
                            weights_T(j + 1)

            for s in range(MT):
                elu_exp(0, s)
            row_deviations(0)
            rows_T(0)
            router_hidden(0)
            router_exps(0)
            weights_T(0)
            with act.Fori(0, NJ - 1) as j:
                tile_of_experts(j, True)
            tile_of_experts(NJ - 1, False)

        @block.vector
        def _(dve):
            dve.memset(ones[:, :], 1.0)
            dve.memset(zero[:, :], 0.0)
            dve.memset(eps[:, :], EPS)
            dve.memset(nodes[:, :, :], 0.0)
            dve.memset(blk[:, 0:SB], 0)
            dve.memset(kvbd[:, :, :], 0.0)
            dve.memset(acc[:, :], 0.0).then_inc(s_vconst, 1)

            tab = Chain(dve, s_tab)
            dve.wait_ge(s_first, 16)
            tab(dve.tensor_copy(pos[:, 0, :], first[:, :]))
            tab(dve.tensor_scalar(pos[:, 0, :], pos[:, 0, :], 0.5, 1.0 / P, ALU.add, ALU.mult))
            tab(dve.tensor_scalar(first[:, :], pos[:, 0, :], -0.5, None, ALU.add))
            dve.wait_ge(s_const, 5)
            dve.tensor_tensor(pos[:, 0, :], first[:, :], pos[:, 1, :], ALU.add).then_inc(s_pos, 1)
            dve.wait_ge(s_tpe, 1)
            for c in range(CH):
                for b in range(2):
                    tab(dve.tensor_scalar(below[:, :], bank[b][:, 0:HALF], step[:, c:c + 1], 0.0,
                                          ALU.is_le, ALU.add, accum_out=count[:, b, c:c + 1]))
            tab(dve.scalar_tensor_tensor(out=tpair[:, 0, :], in0=count[:, 0, :], scalar=-1.0, in1=count[:, 1, :],
                                         op0=ALU.add, op1=ALU.add))
            tab(dve.tensor_scalar(tpair[:, 0, :], tpair[:, 0, :], 0.0, None, ALU.max))
            tab(dve.tensor_tensor(tpair[:, 1, :], step[:, :], tpair[:, 0, :], ALU.subtract))
            tab(dve.tensor_scalar(tpair[:, 1, :], tpair[:, 1, :], float(NT), None, ALU.min))
            tab(dve.tensor_scalar(tpair[:, 2, :], tpair[:, 1, :], float(P), None, ALU.mult))
            tab(dve.tensor_copy(tpi[:, 0, :], tpair[:, 0, :]))
            dve.tensor_copy(tpi[:, 1, :], tpair[:, 1, :]).then_inc(s_tix, 1)
            dve.wait_ge(s_gload, 48)
            for c in range(2):
                for a in range(2):
                    tab(dve.tensor_tensor(prod[:, a, :], wext[:, c, 0:D], lr[:, a, :], ALU.mult))
                    tab(dve.tensor_reduce(wext[:, c, D + a * H:D + (a + 1) * H],
                                          prod[:, a, :].rearrange("p (h d) -> p h d", h=H), AX, ALU.add))
            assert tab.n == TAB_LINKS
            for c in range(CH):
                dve.wait_ge(s_tg[c % 2], 32 * (c // 2 + 1))
                if c >= 1:
                    dve.wait_ge(s_tt, c)
                dve.tensor_copy(sf[:, :], sg[:, c % 2, :])
                dve.tensor_scalar(df[:, :], dg[:, c % 2, :], tpair[:, 2, c:c + 1], None, ALU.subtract
                                  ).then_inc(s_tf, 1)
                dve.wait_ge(s_tt, c + 1)
                dve.tensor_copy(srct[:, c * 128:(c + 1) * 128, :].rearrange("p s u -> p u s"),
                                bank[2 + c % 2][:, 0:PAIR * 128].rearrange("p (u s) -> p u s", u=PAIR))
                dve.tensor_copy(dstt[:, c * 128:(c + 1) * 128, :].rearrange("p s u -> p u s"),
                                bank[2 + c % 2][:, PAIR * 128:2 * PAIR * 128].rearrange("p (u s) -> p u s", u=PAIR)
                                ).then_inc(s_tc, 1)

            ch = Chain(dve, s_ach)
            with dve.Fori(0, NT // AU) as i:
                ch.start(i * (AU + 1))
                for u in range(AU):
                    dve.wait_ge(s_xin[u], (i + 1) * 16)
                    last = dve.bn_stats(stat[:, u, :], xin[:, u, :])
                    ch(last)
                settle(dve, "aggr", i)
                for u in range(AU):
                    last = dve.bn_aggr(mv[:, u, :], stat[:, u, :])
                last.then_inc(s_mv, 1)
                dve.wait_ge(s_sd, i + 1)
                ch(dve.reciprocal(rstd[:, 1, :], rstd[:, 0, :]))
                for u in range(AU):
                    dve.wait_ge(s_xns[u], i * 16)
                    dve.wait_ge(s_xt, i * AU + u)
                    dve.tensor_scalar(xn[:, u, :], xin[:, u, :], mv[:, u, 0:1], rstd[:, 1, u:u + 1],
                                      ALU.subtract, ALU.mult).then_inc(s_xn, 1)
                for u in range(AU):
                    dve.wait_ge(s_fe, i * AU + u + 1)
                    dve.tensor_copy(nodes[:, ds(i * AU + u, 1), :], fe[:, u:u + 1, D:ROW + H]).then_inc(s_nd, 1)

            nch = Chain(dve, s_nch)
            dve.wait_ge(s_nd, NT)
            nch(dve.tensor_reduce(gmax[0:P, 0:H], nodes[:, 0:NT, 0:H].rearrange("p t h -> p h t"), AX, ALU.max))
            dve.memset(gmax[0:P, 4:5], 0.0).then_inc(s_gm, 1)
            dve.wait_ge(s_gm, 2)
            nch(dve.tensor_reduce(gmax[0:H, 5:6], bank[2][0:H, 0:P], AX, ALU.max))
            dve.tensor_scalar(gmax[0:H, 8:8 + H], ident[0:H, 0:H], gmax[0:H, 5:6], None, ALU.mult).then_inc(s_gm, 1)
            dve.wait_ge(s_gm, 4)
            nch(dve.tensor_copy(gmax[0:P, 12:16], bank[2][0:P, 256:256 + H]))
            one = ntmp[:, 0, :].rearrange("p (t h) -> p t h", h=2 * H)
            two = ntmp[:, 1, :].rearrange("p (t h) -> p t h", h=2 * H)
            nch(dve.tensor_tensor(one[:, :, 0:H], nodes[:, :, H:2 * H],
                                  gmax[0:P, 12:16].unsqueeze(1).to_broadcast([P, NCB, H]), ALU.add))
            nch(dve.tensor_copy(nodes[:, :, 0:H], nodes[:, :, H:2 * H]))
            nch(dve.scalar_tensor_tensor(out=nodes[:, :, H:2 * H], in0=one[:, :, 0:H], scalar=0.2,
                                         in1=one[:, :, 0:H], op0=ALU.mult, op1=ALU.max))
            flat = nodes[:, :, :].rearrange("p t h -> p (t h)")
            nch(dve.tensor_copy(nodep[:, 0, :], flat))
            nch(dve.tensor_tensor(ntmp[:, 0, :], flat, nodep[:, 0, :], ALU.subtract))
            nch(dve.tensor_copy(nodep[:, 1, :], ntmp[:, 0, :]))
            nch(dve.tensor_tensor(ntmp[:, 1, :], ntmp[:, 0, :], nodep[:, 1, :], ALU.subtract))
            for u in range(AU):
                dve.wait_ge(s_xns[u], 16 * (NT // AU))
                dve.wait_ge(s_xts[u], 32 * (NT // AU))
            dve.tensor_copy(nodep[:, 2, :], ntmp[:, 1, :]).then_inc(s_nt, 1)
            dve.wait_ge(s_nt, 1)

            def one_hots(n, par, bt_in_table):
                columns = dstt[:, ds(bt_in_table * SB, SB), :].rearrange("p s u -> p (s u)")
                dve.tensor_tensor(S[:, par, :, :], iota[:, :].unsqueeze(1).to_broadcast([128, BATCH, P]),
                                  columns.unsqueeze(2).to_broadcast([128, BATCH, P]), ALU.is_equal
                                  ).then_inc(s_S, 1)

            def add_sums(n):
                for q in range(SB):
                    b = dve.value_load(blk[0:1, ds(n * SB + q, 1)], min_val=0, max_val=NT)
                    dve.wait_ge(s_sum, n * SB + q + 1)
                    dve.wait_ge(s_acc, n * SB + q)
                    dve.tensor_tensor(acc[:, ds(b * ROW, ROW)], bank[2 + q][0:P, 0:ROW],
                                      acc[:, ds(b * ROW, ROW)], ALU.add).then_inc(s_acc, 1)

            zch = Chain(dve, s_zch)

            def edges(k, bt):
                n = k * BODY + bt
                slots = G[:, bt * BATCH:(bt + 1) * BATCH, :]
                dve.wait_ge(s_g[bt], (k + 1) * (16 * BATCH))
                dve.wait_ge(s_er, n + 1)
                er = bank[1][:, 0:BATCH * 2 * H].rearrange("p (j h) -> p j h", j=BATCH)
                zch.start(n * 2)
                zch(dve.tensor_tensor(arg[:, 0, :, :], slots[:, :, D:ROW], er[:, :, 0:H], ALU.add))
                zch(dve.scalar_tensor_tensor(out=arg[:, 1, :, :], in0=arg[:, 0, :, :], scalar=0.2,
                                             in1=arg[:, 0, :, :], op0=ALU.mult, op1=ALU.max))
                dve.tensor_tensor(arg[:, 2, :, :], arg[:, 1, :, :], er[:, :, H:2 * H], ALU.subtract
                                  ).then_inc(s_arg, 1)
                dve.wait_ge(s_sum, n * SB + SB)
                one_hots(n + 1, (bt + 1) % 2, n + 1)
                add_sums(n)
                dve.wait_ge(s_w, n + 1)
                features = slots[:, :, 0:D].rearrange("p j (h d) -> p j h d", h=H)
                dve.tensor_tensor(features, features,
                                  slots[:, :, D:ROW].unsqueeze(3).to_broadcast([128, BATCH, H, HD]), ALU.mult
                                  ).then_inc(s_msg, 1)

            dve.wait_ge(s_blk, 32)
            dve.wait_ge(s_tc, CH)
            one_hots(0, 0, 0)
            dve.memset(vb[:, :, :, 128:129], 1.0)

            kch = Chain(dve, s_kch)
            dve.wait_ge(s_wload, 16 * WLOADS)

            def keys_in(i, u):
                m = i * 2 + u
                dve.wait_ge(s_kmm[u], i + 1)
                dve.wait_ge(s_ka[u], i)
                kch.start(m)
                dve.tensor_tensor(vb[:, u, :, 0:128], bank[4][0:P, D:2 * D].rearrange("p (c n) -> p c n", c=2),
                                  rows[0:P, BV, :].rearrange("p (c n) -> p c n", c=2), ALU.add)
                kch(dve.tensor_tensor(kb[:, u, :], bank[4][0:P, 0:D], rows[0:P, BK, :], ALU.add))
                dve.tensor_scalar(ke[:, u, :], kb[:, u, :], 0.0, None, ALU.min).then_inc(s_km, 1)

            def keys_phi(i, u):
                dve.wait_ge(s_ke, i * 2 + u + 1)
                dve.scalar_tensor_tensor(out=kb[:, u, :], in0=kb[:, u, :], scalar=0.0, in1=ke[:, u, :],
                                         op0=ALU.max, op1=ALU.add).then_inc(s_kp, 1)

            with dve.Fori(0, KV_ROUNDS) as i:
                edges(i, 0)
                keys_in(i, 0)
                edges(i, 1)
                keys_phi(i, 0)
                keys_in(i, 1)
                edges(i, 2)
                keys_phi(i, 1)
                edges(i, 3)
            dve.wait_ge(s_kv, 1)
            for c in range(2):
                for h in range(4):
                    hp = slice(32 * h, 32 * h + 32)
                    dve.tensor_copy(kvbd[hp, c, 32 * h:32 * h + 32], bank[5 + c][hp, 32 * h:32 * h + 32])
                    last = dve.tensor_copy(kvbd[hp, c, 128 + h:129 + h], bank[5 + c][hp, 128:129])
            last.then_inc(s_kbd, 1)

            mch = Chain(dve, s_mch)

            def queries_phi(m):
                dve.wait_ge(s_qb, m + 1)
                dve.tensor_scalar(qe[:, :, :], qb[:, :, :], 0.0, None, ALU.min).then_inc(s_qm, 1)
                dve.wait_ge(s_qe, m + 1)
                dve.scalar_tensor_tensor(out=qb[:, :, :], in0=qb[:, :, :], scalar=0.0, in1=qe[:, :, :],
                                         op0=ALU.max, op1=ALU.add).then_inc(s_qp, 1)

            def attention(m):
                dve.wait_ge(s_pa, m + 1)
                dve.wait_ge(s_pT, m)
                both = bank[5][0:P, 0:2 * (128 + H)].rearrange("p (c n) -> p c n", c=2)
                z = zs[:, 0:2 * H]
                mch.start(m * ATT_LINKS)
                mch(dve.tensor_scalar(z.rearrange("p (c h) -> p c h", c=2), both[:, :, 128:128 + H], 1e-6, None,
                                      ALU.add))
                mch(dve.reciprocal(z, z))
                dve.tensor_tensor(at[:, :].rearrange("p (c h d) -> p c h d", c=2, h=H),
                                  both[:, :, 0:128].rearrange("p c (h d) -> p c h d", h=H),
                                  z.rearrange("p (c h) -> p c h", c=2).unsqueeze(3).to_broadcast([P, 2, H, MD]),
                                  ALU.mult).then_inc(s_at, 1)

            nln = Chain(dve, s_lch)

            def norm(r, m, k, column, mean_var, deviated, gain, shift, to):
                nln.start((m * 2 + k) * 4)
                nln(dve.bn_stats(zs[:, 32:38], r))
                settle(dve, f"norm{k}", m)
                dve.bn_aggr(zs[:, column:column + 2], zs[:, 32:38]).then_inc(mean_var, 1)
                dve.wait_ge(deviated, m + 1)
                nln(dve.reciprocal(zs[:, column + 3:column + 4], zs[:, column + 2:column + 3]))
                nln(dve.tensor_scalar(r, r, zs[:, column:column + 1], zs[:, column + 3:column + 4],
                                      ALU.subtract, ALU.mult))
                nln(dve.tensor_tensor(r, r, rows[0:P, gain, :], ALU.mult))
                return dve.tensor_tensor(to, r, rows[0:P, shift, :], ALU.add)

            rch = Chain(dve, s_rch)

            def first_half(m):
                dve.wait_ge(s_po, m + 1)
                dve.wait_ge(s_xr, (m + 1) * 32)
                rch.start(m * 2)
                rch(dve.tensor_tensor(res[:, 0, :], bank[5][0:P, 0:D], xr[:, 0, :], ALU.add))
                dve.tensor_tensor(xx[:, :], xr[:, 0, :], xr[:, 1, :], ALU.add).then_inc(s_res, 1)
                rch(dve.tensor_tensor(res[:, 0, :], res[:, 0, :], rows[0:P, BO, :], ALU.add))
                dve.wait_ge(s_fy, m)
                norm(res[:, 0, :], m, 0, 16, s_mv1, s_sd1, G1, E1, y[:, :]).then_inc(s_y, 1)

            r2ch = Chain(dve, s_r2ch)

            def second_half(m):
                dve.wait_ge(s_fw, m + 1)
                dve.wait_ge(s_y, m + 1)
                dve.tensor_tensor(res[:, 1, :], bank[6][0:P, 0:D], y[:, :], ALU.add).then_inc(s_r2, 1)
                dve.wait_ge(s_r2, m + 1)
                r2ch.start(m * 2)
                r2ch(dve.tensor_tensor(res[:, 1, :], res[:, 1, :], rows[0:P, B2, :], ALU.add))
                r2ch(norm(res[:, 1, :], m, 1, 24, s_mv2, s_sd2, G2, E2, res[:, 1, :]))
                dve.wait_ge(s_os, m * 16)
                dve.wait_ge(s_res, m + 1)
                dve.tensor_tensor(ob[:, :], res[:, 1, :], xx[:, :], ALU.add).then_inc(s_o, 1)
                dve.wait_ge(s_o, m + 1)

            queries_phi(0)
            attention(0)
            first_half(0)
            with dve.Fori(0, NT - 1) as i:
                edges(i + KV_ROUNDS, 0)
                queries_phi(i + 1)
                edges(i + KV_ROUNDS, 1)
                edges(i + KV_ROUNDS, 2)
                attention(i + 1)
                edges(i + KV_ROUNDS, 3)
                second_half(i)
                first_half(i + 1)
            second_half(NT - 1)
            with dve.Fori(KV_ROUNDS + NT - 1, ROUNDS) as k:
                for bt in range(BODY):
                    edges(k, bt)
            add_sums(ROUNDS * BODY)

            mc = Chain(dve, m_ch)

            def graph_rows(j, s):
                b = j * MT + s
                sums = acc[:, ds(b * ROW, ROW)]
                mc(dve.tensor_scalar(mw[:, s, 9, 0:H], sums[:, D:ROW], 1e-37, None, ALU.max))
                mc(dve.reciprocal(mw[:, s, 9, 0:H], mw[:, s, 9, 0:H]))
                mc(dve.tensor_tensor(mf[:, s, :].rearrange("p (h d) -> p h d", h=H),
                                     sums[:, 0:D].rearrange("p (h d) -> p h d", h=H),
                                     mw[:, s, 9, 0:H].unsqueeze(2).to_broadcast([P, H, HD]), ALU.mult))
                mc(dve.tensor_tensor(mf[:, s, :], mf[:, s, :], rows[0:P, GB, :], ALU.add))
                dve.tensor_scalar(me[:, s, :], mf[:, s, :], 0.0, None, ALU.min).then_inc(m_em, 1)

            def base_rows(j):
                dve.wait_ge(m_b, (j + 1) * 16)
                for s in range(MT):
                    dve.wait_ge(m_ee, j * MT + s + 1)
                    mc(dve.scalar_tensor_tensor(out=mf[:, s, :], in0=mf[:, s, :], scalar=0.0, in1=me[:, s, :],
                                                op0=ALU.max, op1=ALU.add))
                    last = dve.scalar_tensor_tensor(out=mx[:, 0, s, :], in0=mf[:, s, :], scalar=-1.0,
                                                    in1=mb[:, s, :], op0=ALU.add, op1=ALU.add)
                    if s == MT - 1:
                        last.then_inc(m_x, 1)
                        dve.wait_ge(m_x, j + 1)
                    else:
                        mc(last)
                for s in range(MT):
                    mc(dve.bn_stats(mw[:, s, 10, 0:6], mx[:, 0, s, :]))
                settle(dve, "rows", j)
                for s in range(MT):
                    last = dve.bn_aggr(mw[:, s, 0, 0:2], mw[:, s, 10, 0:6])
                last.then_inc(m_mv, 1)

            def norm_rows(j):
                dve.wait_ge(m_sd, j + 1)
                mc(dve.reciprocal(mw[:, :, 1, 1:2], mw[:, :, 1, 0:1]))
                for s in range(MT):
                    last = dve.tensor_scalar(mf[:, s, :], mx[:, 0, s, :], mw[:, s, 0, 0:1], mw[:, s, 1, 1:2],
                                             ALU.subtract, ALU.mult)
                last.then_inc(m_f, 1)

            def route(j):
                dve.wait_ge(m_l, j + 1)
                logits = bank[2][0:P, 0:MT * 8].rearrange("p (s n) -> p s n", s=MT)[:, :, 0:NE]
                mc(dve.tensor_tensor(mw[:, :, 2, 0:NE], logits,
                                     rb2r[0:P, :].unsqueeze(1).to_broadcast([P, MT, NE]), ALU.add))
                mc(dve.tensor_reduce(mw[:, :, 1, 2:3].rearrange("p s n -> p (s n)"), mw[:, :, 2, 0:NE], AX, ALU.max))
                dve.tensor_tensor(mw[:, :, 2, 0:NE], mw[:, :, 2, 0:NE],
                                  mw[:, :, 1, 2:3].to_broadcast([P, MT, NE]), ALU.subtract).then_inc(m_lm, 1)
                dve.wait_ge(m_le, j + 1)
                mc(dve.tensor_reduce(mw[:, :, 1, 3:4].rearrange("p s n -> p (s n)"), mw[:, :, 3, 0:NE], AX, ALU.add))
                mc(dve.reciprocal(mw[:, :, 1, 4:5], mw[:, :, 1, 3:4]))
                mc(dve.tensor_tensor(mw[:, :, 3, 0:NE], mw[:, :, 3, 0:NE],
                                     mw[:, :, 1, 4:5].to_broadcast([P, MT, NE]), ALU.mult))
                for s in range(MT):
                    settle(dve, f"max{s}", j)
                    mc(dve.max(mw[:, s, 4, :], mw[:, s, 3, :]))
                    settle(dve, f"index{s}", j)
                    mc(dve.max_index(mi[:, s, :], mw[:, s, 4, :], mw[:, s, 3, :]))
                dve.tensor_tensor(mw[:, :, 7, 0:1], mw[:, :, 4, 1:2], mw[:, :, 4, 0:1], ALU.subtract
                                  ).then_inc(m_d, 1)
                dve.wait_ge(m_de, j + 1)
                mc(dve.tensor_copy(mw[:, :, 5, :], mi[:, :, :]))
                mc(dve.tensor_scalar(mw[:, :, 8, 1:2], mw[:, :, 8, 0:1], 1.0, None, ALU.add))
                mc(dve.reciprocal(mw[:, :, 8, 2:3], mw[:, :, 8, 1:2]))
                mc(dve.tensor_tensor(mw[:, :, 8, 3:4], mw[:, :, 8, 0:1], mw[:, :, 8, 2:3], ALU.mult))
                for s in range(MT):
                    for r in range(2):
                        mc(dve.tensor_scalar(mw[:, s, 11 + r, 0:NE], iota[0:P, 0:NE], mw[:, s, 5, r:r + 1],
                                             mw[:, s, 8, 2 + r:3 + r], ALU.is_equal, ALU.mult))
                dve.wait_ge(m_s, j)
                dve.tensor_tensor(wt[:, 0, :, :], mw[:, :, 11, 0:NE], mw[:, :, 12, 0:NE], ALU.add).then_inc(m_wt, 1)
                dve.wait_ge(m_wt, j + 1)

            def start_tile(j):
                dve.wait_ge(m_bb, j + 1)
                dve.wait_ge(m_st, j * 16)
                dve.tensor_copy(wt[:, 1, :, :], wt[:, 0, :, :])
                dve.tensor_tensor(mx[:, 1, :, :].rearrange("p s n -> p (s n)"),
                                  mx[:, 0, :, :].rearrange("p s n -> p (s n)"), bank[7][0:P, 0:MT * D], ALU.add
                                  ).then_inc(m_s, 1)
                dve.wait_ge(m_s, j + 1)

            def add_expert(j, e):
                for s in range(MT):
                    dve.wait_ge(m_o, (j * NE + e) * MT + s + 1)
                    if e >= 1:
                        dve.wait_ge(m_oa, (j * NE + e - 1) * MT + s + 1)
                    dve.scalar_tensor_tensor(out=mx[:, 1, s, :], in0=bank[5 + s][0:P, 0:D],
                                             scalar=wt[:, 1, s, e:e + 1], in1=mx[:, 1, s, :],
                                             op0=ALU.mult, op1=ALU.add).then_inc(m_oa, 1)

            def tile_of_experts(j, ahead):
                start_tile(j)
                for e in range(NE):
                    if ahead:
                        if e == 0:
                            for s in range(MT):
                                graph_rows(j + 1, s)
                        if e == 1:
                            base_rows(j + 1)
                            norm_rows(j + 1)
                        if e == 4:
                            route(j + 1)
                    add_expert(j, e)

            mc(dve.memset(mw[:, :, 3, :], -1.0))
            for s in range(MT):
                graph_rows(0, s)
            base_rows(0)
            norm_rows(0)
            route(0)
            pro = mc.n
            with dve.Fori(0, NJ - 1) as j:
                mc.start(pro + j * (pro - 1))
                tile_of_experts(j, True)
                assert mc.n == pro - 1, (mc.n, pro)
            tile_of_experts(NJ - 1, False)

        @block.tensor
        def _(pe):
            pe.wait_ge(s_vconst, 1)
            pe.wait_ge(s_const, 5)
            pe.wait_ge(s_pos, 1)
            for b in range(2):
                last = pe.matmul(bank[b][:, 0:HALF], ones[0:1, :], pos[:, 0, b * HALF:(b + 1) * HALF],
                                 start=True, stop=True)
            last.then_inc(s_tpe, 1)
            for c in range(CH):
                pe.wait_ge(s_tf, c + 1)
                if c >= 2:
                    pe.wait_ge(s_tc, c - 1)
                for n, rows_ in enumerate((sf, df)):
                    for u in range(PAIR):
                        q = n * PAIR + u
                        last = pe.transpose(bank[2 + c % 2][:, q * 128:(q + 1) * 128],
                                            rows_[:, u * TE:(u + 1) * TE], ident[:, :])
                last.then_inc(s_tt, 1)

            pe.wait_ge(s_tab, TAB_LINKS)
            with pe.Fori(0, NT // AU) as i:
                for u in range(AU):
                    t = i * AU + u
                    pe.wait_ge(s_xn, t + 1)
                    if u >= 2:
                        pe.wait_ge(s_xte, t - 1)
                    else:
                        pe.wait_ge(s_xte, i * AU)
                    for c in range(2):
                        last = pe.transpose(bank[4 + u % 2][:, c * P:(c + 1) * P], xn[:, u, c * 128:(c + 1) * 128],
                                            ident[0:P, 0:P])
                    last.then_inc(s_xt, 1)
                    pe.wait_ge(s_xte, t + 1)
                    if u >= 2:
                        pe.wait_ge(s_fe, t - 1)
                    else:
                        pe.wait_ge(s_fe, i * AU)
                    for c in range(2):
                        last = pe.matmul(bank[6 + u % 2][0:P, 0:ROW + H], xT[:, u, c * P:(c + 1) * P], wext[:, c, :],
                                         start=(c == 0), stop=(c == 1))
                    last.then_inc(s_f, 1)

            pe.wait_ge(s_gm, 1)
            pe.transpose(bank[2][0:H, 0:P], gmax[0:P, 0:H], ident[0:P, 0:P]).then_inc(s_gm, 1)
            pe.wait_ge(s_gm, 3)
            pe.matmul(bank[2][0:P, 256:256 + H], ones[0:H, 0:P], gmax[0:H, 8:8 + H], start=True, stop=True
                      ).then_inc(s_gm, 1)

            def transposes(n, par):
                pe.wait_ge(s_S, n + 1)
                for j in range(BATCH):
                    last = pe.transpose(bank[0][0:P, j * TE:(j + 1) * TE], S[:, par, j, :], ident[:, :])
                last.then_inc(s_st, 1)

            def logits(n, par):
                pe.wait_ge(s_ste, n + 1)
                for q in range(SB):
                    b = pe.value_load(blk[0:1, ds((n + 1) * SB + q, 1)], min_val=0, max_val=NT)
                    for j in range(q * PAIR, (q + 1) * PAIR):
                        for part in range(3):
                            last = pe.matmul(bank[1][:, j * 2 * H:(j + 1) * 2 * H],
                                             ST[0:P, par, j * TE:(j + 1) * TE],
                                             nodep[:, part, ds(b * (2 * H), 2 * H)],
                                             start=(part == 0), stop=(part == 2))
                last.then_inc(s_er, 1)

            def edges(k, bt):
                n = k * BODY + bt
                pe.wait_ge(s_ste, n + 1)
                transposes(n + 1, (bt + 1) % 2)
                pe.wait_ge(s_msg, n + 1)
                for q in range(SB):
                    pe.wait_ge(s_acc, n * SB + q + 1)
                    for u in range(PAIR):
                        j = q * PAIR + u
                        last = pe.matmul(bank[2 + q][0:P, 0:ROW], S[:, bt % 2, j, :], G[:, bt * BATCH + j, :],
                                         start=(u == 0), stop=(u == PAIR - 1))
                    last.then_inc(s_sum, 1)
                pe.wait_ge(s_arg, n + 1)
                logits(n + 1, (bt + 1) % 2)

            pe.wait_ge(s_nt, 1)
            transposes(0, 0)
            pe.wait_ge(s_blk, 32)
            logits(0, 0)
            for q in range(SB):
                pe.matmul(bank[2 + q][0:P, 0:ROW], zero[:, 0:P], zero[:, :], start=True, stop=True
                          ).then_inc(s_sum, 1)

            pe.wait_ge(s_wload, 16 * WLOADS)
            for c in range(2):
                pe.matmul(bank[5 + c][:, 0:129], zero[:, 0:128], zero[:, 0:129], start=True, stop=False)

            def keys_values(i, u):
                pe.wait_ge(s_kx[u], (i + 1) * 16)
                pe.wait_ge(s_km, i * 2 + u)
                for c in range(2):
                    last = pe.matmul(bank[4][0:P, :], xm[:, u, c * P:(c + 1) * P], wkv[:, c, :],
                                     start=(c == 0), stop=(c == 1))
                last.then_inc(s_kmm[u], 1)

            def add_kv(i, u):
                pe.wait_ge(s_kp, i * 2 + u + 1)
                for c in range(2):
                    last = pe.matmul(bank[5 + c][:, 0:129], kb[:, u, c * 128:(c + 1) * 128], vb[:, u, c, :],
                                     start=False, stop=False)
                last.then_inc(s_ka[u], 1)

            with pe.Fori(0, KV_ROUNDS) as i:
                edges(i, 0)
                keys_values(i, 0)
                edges(i, 1)
                keys_values(i, 1)
                edges(i, 2)
                add_kv(i, 0)
                edges(i, 3)
                add_kv(i, 1)
            for c in range(2):
                last = pe.matmul(bank[5 + c][:, 0:129], zero[:, 0:128], zero[:, 0:129], start=False, stop=True)
            last.then_inc(s_kv, 1)

            def queries(m):
                pe.wait_ge(s_xm, (m + 1) * 16)
                pe.wait_ge(s_res, m)
                for o in range(2):
                    for c in range(2):
                        last = pe.matmul(bank[5][:, o * P:(o + 1) * P], wq[:, c, o * 128:(o + 1) * 128],
                                         xm[:, 0, c * P:(c + 1) * P], start=(c == 0), stop=(c == 1))
                last.then_inc(s_pq, 1)

            def attend(m):
                pe.wait_ge(s_qp, m + 1)
                for c in range(2):
                    last = pe.matmul(bank[5][0:P, c * (128 + H):(c + 1) * (128 + H)], qb[:, c, :], kvbd[:, c, :],
                                     start=True, stop=True)
                last.then_inc(s_pa, 1)

            def attention_T(m):
                pe.wait_ge(s_at, m + 1)
                for c in range(2):
                    last = pe.transpose(bank[4][:, c * P:(c + 1) * P], at[:, c * 128:(c + 1) * 128],
                                        ident[0:P, 0:P])
                last.then_inc(s_pT, 1)

            def project(m):
                pe.wait_ge(s_aT, m + 1)
                for c in range(2):
                    last = pe.matmul(bank[5][0:P, 0:D], aT[:, c, :], wo[:, c, :], start=(c == 0), stop=(c == 1))
                last.then_inc(s_po, 1)

            def norm_T(m):
                pe.wait_ge(s_y, m + 1)
                for c in range(2):
                    last = pe.transpose(bank[4][:, c * P:(c + 1) * P], y[:, c * 128:(c + 1) * 128], ident[0:P, 0:P])
                last.then_inc(s_fy, 1)

            def hidden(m, half):
                pe.wait_ge(s_yT, m + 1)
                if half == 0:
                    pe.wait_ge(s_r2, m)
                else:
                    pe.wait_ge(s_h, m * 2)
                for c4 in range(4):
                    f = (half * 4 + c4) * 128
                    for c in range(2):
                        last = pe.matmul(bank[6 + half][:, c4 * P:(c4 + 1) * P], w1[:, c, f:f + 128], yT[:, c, :],
                                         start=(c == 0), stop=(c == 1))
                last.then_inc(s_fh, 1)

            def second_layer(m):
                pe.wait_ge(s_h, m * 2 + 2)
                for f in range(8):
                    last = pe.matmul(bank[6][0:P, 0:D], hT[:, f, :], w2[:, f, :], start=(f == 0), stop=(f == 7))
                last.then_inc(s_fw, 1)

            pe.wait_ge(s_kbd, 1)
            queries(0)
            attend(0)
            attention_T(0)
            project(0)
            with pe.Fori(0, NT - 1) as i:
                edges(i + KV_ROUNDS, 0)
                norm_T(i)
                queries(i + 1)
                edges(i + KV_ROUNDS, 1)
                hidden(i, 0)
                attend(i + 1)
                edges(i + KV_ROUNDS, 2)
                hidden(i, 1)
                attention_T(i + 1)
                edges(i + KV_ROUNDS, 3)
                second_layer(i)
                project(i + 1)
            norm_T(NT - 1)
            hidden(NT - 1, 0)
            hidden(NT - 1, 1)
            second_layer(NT - 1)
            with pe.Fori(KV_ROUNDS + NT - 1, ROUNDS) as k:
                for bt in range(BODY):
                    edges(k, bt)

            def rows_T(j):
                pe.wait_ge(m_f, j + 1)
                pe.wait_ge(m_fe, j)
                for s in range(MT):
                    for c in range(2):
                        last = pe.transpose(bank[0][:, c * MT * P + s * P:c * MT * P + (s + 1) * P],
                                            mf[:, s, c * 128:(c + 1) * 128], ident[0:P, 0:P])
                last.then_inc(m_fT, 1)

            def router_1(j):
                pe.wait_ge(m_fe, j + 1)
                for c in range(2):
                    last = pe.matmul(bank[1][:, 0:MT * P], r1[:, c, :], mfT[:, 0, c, :], start=(c == 0), stop=(c == 1))
                last.then_inc(m_r, 1)

            def router_2(j):
                pe.wait_ge(m_rr, j + 1)
                pe.wait_ge(m_we, j)
                for s in range(MT):
                    last = pe.matmul(bank[2][0:P, s * 8:s * 8 + NE], mrh[:, s * P:(s + 1) * P], r2[:, :],
                                     start=True, stop=True)
                last.then_inc(m_l, 1)

            def weights_T(j):
                pe.wait_ge(m_wt, j + 1)
                for s in range(MT):
                    last = pe.transpose(bank[2][0:NE, 128 + s * P:128 + (s + 1) * P], wt[:, 0, s, :],
                                        ident[0:P, 0:P])
                last.then_inc(m_wT, 1)

            def biases(j):
                pe.wait_ge(m_we, j + 1)
                pe.wait_ge(m_s, j)
                for s in range(MT):
                    last = pe.matmul(bank[7][0:P, s * D:(s + 1) * D], wtT[:, s, :], e3b[:, :], start=True, stop=True)
                last.then_inc(m_bb, 1)

            def layer_1(j, e):
                pe.wait_ge(m_c, j + 1)
                pe.wait_ge(m_h1r, j * NE + e)
                for o in range(2):
                    for c in range(2):
                        last = pe.matmul(bank[3][:, o * MT * P:(o + 1) * MT * P], x1[:, e, c, o * 128:(o + 1) * 128],
                                         mfT[:, 1, c, :], start=(c == 0), stop=(c == 1))
                last.then_inc(m_h1, 1)

            def layer_2(j, e):
                pe.wait_ge(m_h1r, j * NE + e + 1)
                pe.wait_ge(m_h2r, j * NE + e)
                for o in range(2):
                    for c in range(2):
                        last = pe.matmul(bank[4][:, o * MT * P:(o + 1) * MT * P], x2[:, e, c, o * 128:(o + 1) * 128],
                                         h1[:, e % 2, c, :], start=(c == 0), stop=(c == 1))
                last.then_inc(m_h2, 1)

            def layer_3(j, e):
                pe.wait_ge(m_h2r, j * NE + e + 1)
                for s in range(MT):
                    if e >= 1:
                        pe.wait_ge(m_oa, (j * NE + e - 1) * MT + s + 1)
                    else:
                        pe.wait_ge(m_oa, j * (NE * MT))
                    for c in range(2):
                        last = pe.matmul(bank[5 + s][0:P, 0:D], h2[:, e % 2, c, s * P:(s + 1) * P], x3[:, e, c, :],
                                         start=(c == 0), stop=(c == 1))
                    last.then_inc(m_o, 1)

            def tile_of_experts(j, ahead):
                layer_1(j, 0)
                for e in range(NE):
                    if e + 1 < NE:
                        layer_1(j, e + 1)
                    layer_2(j, e)
                    if e >= 1:
                        layer_3(j, e - 1)
                    if ahead:
                        if e == 2:
                            rows_T(j + 1)
                        if e == 3:
                            router_1(j + 1)
                        if e == 4:
                            router_2(j + 1)
                        if e == 5:
                            weights_T(j + 1)
                layer_3(j, NE - 1)
                if ahead:
                    biases(j + 1)

            pe.wait_ge(s_os, 16 * NT)
            rows_T(0)
            router_1(0)
            router_2(0)
            weights_T(0)
            biases(0)
            with pe.Fori(0, NJ - 1) as j:
                tile_of_experts(j, True)
            tile_of_experts(NJ - 1, False)


_INS = ['x', 'src', 'dst', 'L0_gnn_W', 'L0_gnn_attn_l', 'L0_gnn_attn_r', 'L0_gnn_bias', 'L0_mix_Wq', 'L0_mix_bq',
        'L0_mix_Wk', 'L0_mix_bk', 'L0_mix_Wv', 'L0_mix_bv', 'L0_mix_Wo', 'L0_mix_bo', 'L0_mix_W1', 'L0_mix_b1',
        'L0_mix_W2', 'L0_mix_b2', 'L0_mix_ln1_g', 'L0_mix_ln1_b', 'L0_mix_ln2_g', 'L0_mix_ln2_b',
        'L0_ffn_router_w1', 'L0_ffn_router_b1', 'L0_ffn_router_w2', 'L0_ffn_router_b2', 'L0_ffn_expert_w1',
        'L0_ffn_expert_b1', 'L0_ffn_expert_w2', 'L0_ffn_expert_b2', 'L0_ffn_expert_w3', 'L0_ffn_expert_b3']


def kernel(**inputs):
    import numpy as np
    import concourse.bacc as bacc
    from concourse import mybir as _mybir
    from concourse.bass_utils import run_bass_kernel_spmd

    nc = bacc.Bacc("TRN2", target_bir_lowering=False, num_devices=1)
    arrays, args = {}, []
    for name in _INS:
        a = np.ascontiguousarray(inputs[name])
        if name in ('src', 'dst'):
            pad = np.full(EPAD - E, 0 if name == 'src' else N, a.dtype)
            a = np.concatenate([a, pad])
        arrays[f"in_{name}"] = a
        args.append(nc.dram_tensor(f"in_{name}", a.shape, _mybir.dt.from_np(a.dtype), kind="ExternalInput").ap())
    args.append(nc.dram_tensor("out_x", (N, D), _mybir.dt.float32, kind="ExternalOutput").ap())
    gps_layer(nc, *args)
    r = run_bass_kernel_spmd(nc, [arrays], core_ids=[0])
    return r.results[0]["out_x"]
```

```python
from contextlib import ExitStack

import concourse.bass as bass
from concourse import mybir

N, D, E, H, HD = 6250, 256, 206250, 4, 64
P = 125
NT = N // P
TE = 128
PAIR = 2
NP = -(-E // (TE * PAIR))
EPAD = NP * PAIR * TE
BATCH = 4
BODY = 4
SLOTS = BATCH * BODY
SB = BATCH // PAIR
ROUNDS = -(-(NP + NT) * PAIR // SLOTS)
CH = -(-(ROUNDS * SLOTS // PAIR + 4) // 128)
ROW = D + H
NCB = NT + 1
MH, MD = 8, 32
FF = 1024
RH = 128
NE = 6
MT = 2
NJ = NT // MT
EPS = 1e-5
AU = 5
HALF = NP // 2
KV_ROUNDS = NT // 2
KLOADS = 4
WLOADS = 23
WEXT_LINKS = 8
PACK = 64
NPACK = (CH * 128 - 2) // 4
BATCHES = ROUNDS * BODY
DEPTH = 4
assert N == NT * P and NP == 2 * HALF and NT % AU == 0 and KV_ROUNDS + NT + DEPTH - 1 < ROUNDS and BODY == 4


class Chain:

    def __init__(self, engine, semaphore):
        self.engine, self.semaphore, self.base, self.n = engine, semaphore, 0, 0

    def start(self, base):
        self.base, self.n = base, 0

    def __call__(self, instruction):
        self.n += 1
        instruction.then_inc(self.semaphore, 1)
        self.engine.wait_ge(self.semaphore, self.base + self.n)


def unpack(packed, digit):
    value = packed // PACK ** digit if digit else packed
    return (value % PACK if digit < 3 else value).with_bounds(min_val=0, max_val=NT)


def past(engine, semaphore, value):
    if not isinstance(value, int) or value > 0:
        engine.wait_ge(semaphore, value)


def gps_layer(nc, x, src, dst, gW, attn_l, attn_r, gbias, Wq, bq, Wk, bk, Wv, bv, Wo, bo, W1, b1, W2, b2,
              g1, be1, g2, be2, rw1, rb1, rw2, rb2, ew1, eb1, ew2, eb2, ew3, eb3, out):
    fp32, bf16, i32, u32 = mybir.dt.float32, mybir.dt.bfloat16, mybir.dt.int32, mybir.dt.uint32
    ALU = mybir.AluOpType
    ACT = mybir.ActivationFunctionType
    AX = mybir.AxisListType.X
    ds = bass.ds

    feat_d = nc.dram_tensor("feat_d", (N, ROW), fp32, kind="Internal").ap()
    xn_d = nc.dram_tensor("xn_d", (N, D), fp32, kind="Internal").ap()
    xT_d = nc.dram_tensor("xT_d", (NT * 128, 2 * P), fp32, kind="Internal").ap()
    xx_d = nc.dram_tensor("xx_d", (N, D), fp32, kind="Internal").ap()
    base_d = nc.dram_tensor("base_d", (N, D), fp32, kind="Internal").ap()
    blk_d = nc.dram_tensor("blk_d", (1, CH * 128), i32, kind="Internal").ap()
    src2 = src.rearrange("(t e) -> t e", e=PAIR * TE)
    dst2 = dst.rearrange("(t e) -> t e", e=PAIR * TE)

    ctx, tables, early, mixer, experts = ExitStack(), ExitStack(), ExitStack(), ExitStack(), ExitStack()
    with ctx:
        def sb(name, shape, dt=fp32, where=ctx):
            return where.enter_context(nc.sbuf_tensor(name, shape, dt))

        def sem(name):
            return ctx.enter_context(nc.semaphore(name))

        ident = sb("ident", [128, 128])
        ones = sb("ones", [128, 128])
        zero = sb("zero", [128, ROW])
        iota = sb("iota", [128, P])
        eps = sb("eps", [128, 1])
        wext = sb("wext", [128, 2, D + 2 * H])
        wkv = sb("wkv", [128, 2, 2 * D])
        wq = sb("wq", [128, 2, D])
        wo = sb("wo", [128, 2, D])
        w1 = sb("w1", [128, 2, FF])
        w2 = sb("w2", [128, 8, D])
        r1 = sb("r1", [128, 2, RH])
        r2 = sb("r2", [128, NE])
        x1 = sb("x1", [128, NE, 2, D])
        x2 = sb("x2", [128, NE, 2, D])
        x3 = sb("x3", [128, NE, 2, D])
        e3b = sb("e3b", [NE, D])
        rows = sb("rows", [128, 9, D])
        BK, BV, BO, B2, G1, E1, G2, E2, GB = range(9)
        rb2r = sb("rb2r", [128, NE])
        bqc = sb("bqc", [128, 2])
        b1c = sb("b1c", [128, 8])
        rb1c = sb("rb1c", [128, 1])
        eb1c = sb("eb1c", [128, NE, 2])
        eb2c = sb("eb2c", [128, NE, 2])
        srct = sb("srct", [128, CH * 128, PAIR], i32)
        dstt = sb("dstt", [128, CH * 128, PAIR])
        blk = sb("blk", [1, CH * 128 + SB], i32)
        pack = sb("pack", [1, 2, NPACK], i32)
        nodes = sb("nodes", [P, NCB, 2 * H])
        nodep = sb("nodep", [P, 3, NCB * 2 * H], bf16)
        acc = sb("acc", [P, NCB * ROW])
        kvbd = sb("kvbd", [128, 2, 128 + H])
        first = sb("first", [1, NP], i32, tables)
        pos = sb("pos", [1, 2, NP], fp32, tables)
        step = sb("step", [128, CH], fp32, tables)
        below = sb("below", [128, HALF], fp32, tables)
        sg = sb("sg", [128, 2, PAIR * TE], i32, tables)
        dg = sb("dg", [128, 2, PAIR * TE], i32, tables)
        sf = sb("sf", [128, PAIR * TE], fp32, tables)
        df = sb("df", [128, PAIR * TE], fp32, tables)
        lr = sb("lr", [128, 2, D], fp32, tables)
        prod = sb("prod", [128, 2, D], fp32, tables)
        ntmp = sb("ntmp", [P, 2, NCB * 2 * H], fp32, tables)
        tables.close()
        G = sb("G", [128, SLOTS, ROW])
        idx = sb("idx", [128, SLOTS], i32)
        S = sb("S", [128, BODY, BATCH, P])
        ST = sb("ST", [128, 2, BATCH * TE], bf16)
        arg = sb("arg", [128, 3, BATCH, H])
        xin = sb("xin", [P, AU, D], fp32, early)
        xn = sb("xn", [P, AU, D], fp32, early)
        xT = sb("xT", [128, AU, 2 * P], fp32, early)
        xs = sb("xs", [P, AU, D], fp32, early)
        fe = sb("fe", [P, AU, ROW], fp32, early)
        stat = sb("stat", [P, AU, 6], fp32, early)
        mv = sb("mv", [P, AU, 2], fp32, early)
        rstd = sb("rstd", [P, 2, AU], fp32, early)
        count = sb("count", [128, 2, CH], fp32, early)
        tpair = sb("tpair", [128, 4, CH], fp32, early)
        tpi = sb("tpi", [128, 2, CH], i32, early)
        packf = sb("packf", [1, 2, NPACK], fp32, early)
        gmax = sb("gmax", [128, 16], fp32, early)
        early.close()
        kb = sb("kb", [P, 2, D], fp32, mixer)
        ke = sb("ke", [P, 2, D], fp32, mixer)
        vb = sb("vb", [P, 2, 2, 128 + 1], fp32, mixer)
        xm = sb("xm", [128, 2, 2 * P], fp32, mixer)
        xr = sb("xr", [P, D], fp32, mixer)
        xo = sb("xo", [P, D], fp32, mixer)
        qb = sb("qb", [128, 2, P], fp32, mixer)
        qe = sb("qe", [128, 2, P], fp32, mixer)
        at = sb("at", [P, D], fp32, mixer)
        aT = sb("aT", [128, 2, P], fp32, mixer)
        res = sb("res", [P, 2, D], fp32, mixer)
        y = sb("y", [P, 2, D], fp32, mixer)
        yT = sb("yT", [128, 2, P], fp32, mixer)
        hT = sb("hT", [128, 8, P], fp32, mixer)
        ob = sb("ob", [P, D], fp32, mixer)
        zs = sb("zs", [P, 64], fp32, mixer)
        mixer.close()
        mb = sb("mb", [P, MT, D], fp32, experts)
        mx = sb("mx", [P, 2, MT, D], fp32, experts)
        mf = sb("mf", [P, MT, D], fp32, experts)
        me = sb("me", [P, MT, D], fp32, experts)
        mfT = sb("mfT", [128, 2, 2, MT * P], fp32, experts)
        mrh = sb("mrh", [128, MT * P], fp32, experts)
        mw = sb("mw", [P, MT, 16, 8], fp32, experts)
        mi = sb("mi", [P, MT, 8], u32, experts)
        wt = sb("wt", [P, 2, MT, NE], fp32, experts)
        wtT = sb("wtT", [NE, MT, P], fp32, experts)
        h1 = sb("h1", [128, 2, 2, MT * P], fp32, experts)
        h2 = sb("h2", [128, 2, 2, MT * P], fp32, experts)
        experts.close()

        bank = [ctx.enter_context(nc.psum_tensor(f"bank{i}", [128, 512], fp32)) for i in range(8)]

        s_turn = sem("s_turn")
        s_const = sem("s_const")
        s_vconst = sem("s_vconst")
        s_kload = sem("s_kload")
        s_wload = sem("s_wload")
        s_gload = sem("s_gload")
        s_first = sem("s_first")
        s_tab = sem("s_tab")
        s_pos = sem("s_pos")
        s_tpe = sem("s_tpe")
        s_pack = sem("s_pack")
        s_tix = sem("s_tix")
        s_tg = [sem(f"s_tg{i}") for i in range(2)]
        s_tf = sem("s_tf")
        s_tt = sem("s_tt")
        s_tc = sem("s_tc")
        s_blk = sem("s_blk")
        s_xin = [sem(f"s_xin{i}") for i in range(AU)]
        s_mv = sem("s_mv")
        s_sd = sem("s_sd")
        s_xn = sem("s_xn")
        s_xns = [sem(f"s_xns{i}") for i in range(AU)]
        s_ach = sem("s_ach")
        s_xt = sem("s_xt")
        s_xte = sem("s_xte")
        s_xts = [sem(f"s_xts{i}") for i in range(AU)]
        s_f = sem("s_f")
        s_fe = sem("s_fe")
        s_xs = sem("s_xs")
        s_xss = [sem(f"s_xss{i}") for i in range(AU)]
        s_nch = sem("s_nch")
        s_gm = sem("s_gm")
        s_nt = sem("s_nt")
        s_idx = [sem(f"s_idx{i}") for i in range(BODY)]
        s_g = [sem(f"s_g{i}") for i in range(BODY)]
        s_S = sem("s_S")
        s_st = sem("s_st")
        s_ste = sem("s_ste")
        s_er = sem("s_er")
        s_zch = sem("s_zch")
        s_arg = sem("s_arg")
        s_w = sem("s_w")
        s_msg = sem("s_msg")
        s_sum = sem("s_sum")
        s_acc = sem("s_acc")
        s_kx = [sem(f"s_kx{i}") for i in range(2)]
        s_kmm = [sem(f"s_kmm{i}") for i in range(2)]
        s_kb = sem("s_kb")
        s_km = sem("s_km")
        s_ke = sem("s_ke")
        s_kp = sem("s_kp")
        s_ka = [sem(f"s_ka{i}") for i in range(2)]
        s_kch = sem("s_kch")
        s_kv = sem("s_kv")
        s_kbd = sem("s_kbd")
        s_xm = sem("s_xm")
        s_xr = sem("s_xr")
        s_xo = sem("s_xo")
        s_pq = sem("s_pq")
        s_qb = sem("s_qb")
        s_qm = sem("s_qm")
        s_qe = sem("s_qe")
        s_qp = sem("s_qp")
        s_pa = sem("s_pa")
        s_at = sem("s_at")
        s_pT = sem("s_pT")
        s_aT = sem("s_aT")
        s_po = sem("s_po")
        s_res = sem("s_res")
        s_mv1 = sem("s_mv1")
        s_y = sem("s_y")
        s_yc = sem("s_yc")
        s_fy = sem("s_fy")
        s_yT = sem("s_yT")
        s_fh = sem("s_fh")
        s_h = sem("s_h")
        s_fa = sem("s_fa")
        s_fw = sem("s_fw")
        s_r2 = sem("s_r2")
        s_mv2 = sem("s_mv2")
        s_sdm = sem("s_sdm")
        s_rs = sem("s_rs")
        s_o = sem("s_o")
        s_os = sem("s_os")
        s_lch = sem("s_lch")
        s_l2ch = sem("s_l2ch")
        s_och = sem("s_och")
        s_rch = sem("s_rch")
        s_r2ch = sem("s_r2ch")
        s_mch = sem("s_mch")
        m_b = sem("m_b")
        m_em = sem("m_em")
        m_ee = sem("m_ee")
        m_x = sem("m_x")
        m_mv = sem("m_mv")
        m_sd = sem("m_sd")
        m_f = sem("m_f")
        m_fT = sem("m_fT")
        m_fe = sem("m_fe")
        m_r = sem("m_r")
        m_rr = sem("m_rr")
        m_l = sem("m_l")
        m_lm = sem("m_lm")
        m_le = sem("m_le")
        m_d = sem("m_d")
        m_de = sem("m_de")
        m_wt = sem("m_wt")
        m_wT = sem("m_wT")
        m_we = sem("m_we")
        m_bb = sem("m_bb")
        m_c = sem("m_c")
        m_s = sem("m_s")
        m_h1 = sem("m_h1")
        m_h1r = sem("m_h1r")
        m_h2 = sem("m_h2")
        m_h2r = sem("m_h2r")
        m_o = sem("m_o")
        m_oa = sem("m_oa")
        m_st = sem("m_st")
        m_ch = sem("m_ch")

        block = ctx.enter_context(nc.Block())

        def settle(engine):
            engine.sem_inc(s_turn, 1)

        @block.sync
        def _(sp):
            with nc.allow_non_contiguous_dma("first destination of each pair, biases by partition"):
                sp.dma_start(first[:, :], dst2[:, 0:1].rearrange("t e -> e t")).then_inc(s_first, 16)
            gl = [(wext[:, :, 0:D], gW.rearrange("(c p) n -> p c n", p=128)),
                  (lr[:, 0, :], attn_l.rearrange("h d -> (h d)").partition_broadcast(128)),
                  (lr[:, 1, :], attn_r.rearrange("h d -> (h d)").partition_broadcast(128))]
            for to, of in gl:
                sp.dma_start(to, of).then_inc(s_gload, 16)

            def load_x(t, u):
                sp.dma_start(xin[:, u, :], x[ds(t * P, P), :]).then_inc(s_xin[u], 16)

            for u in range(AU):
                load_x(u, u)
            sp.wait_ge(s_tix, 1)
            with nc.allow_non_contiguous_dma("steps from partitions to a row"):
                sp.dma_start(blk_d[0, :].rearrange("(c p) -> p c", p=128), tpi[:, 1, :]).then_inc(s_blk, 16)
            sp.wait_ge(s_blk, 16)
            sp.dma_start(blk[:, SB:], blk_d[:, :]).then_inc(s_blk, 16)

            def store_xn(i, u):
                t = i * AU + u
                sp.wait_ge(s_xn, t + 1)
                sp.dma_start(xn_d[ds(t * P, P), :], xn[:, u, :]).then_inc(s_xns[u], 16)
                sp.wait_ge(s_xs, t + 1)
                sp.dma_start(xx_d[ds(t * P, P), :], xs[:, u, :]).then_inc(s_xss[u], 16)

            with sp.Fori(0, NT // AU - 1) as i:
                for u in range(AU):
                    store_xn(i, u)
                    load_x((i + 1) * AU + u, u)
            for u in range(AU):
                store_xn(NT // AU - 1, u)

            vectors = [(rows[:, n, :], v.partition_broadcast(128)) for n, v in
                       enumerate([bk, bv, bo, b2, g1, be1, g2, be2, gbias])]
            kl = [(wkv[:, :, 0:D], Wk.rearrange("(c p) n -> p c n", p=128)),
                  (wkv[:, :, D:2 * D], Wv.rearrange("(c p) n -> p c n", p=128))] + vectors[0:2]
            wl = vectors[2:]
            wl += [(wq[:, :, :], Wq.rearrange("(c p) n -> p c n", p=128)),
                   (wo[:, :, :], Wo.rearrange("(c p) n -> p c n", p=128)),
                   (w1[:, :, :], W1.rearrange("(c p) n -> p c n", p=128)),
                   (w2[:, :, :], W2.rearrange("(c p) n -> p c n", p=128)),
                   (r1[:, :, :], rw1.rearrange("(c p) n -> p c n", p=128)),
                   (r2[:, :], rw2), (e3b[:, :], eb3),
                   (rb2r[:, :], rb2.partition_broadcast(128)),
                   (x1[:, :, :, :], ew1.rearrange("e (c p) n -> p e c n", p=128)),
                   (x2[:, :, :, :], ew2.rearrange("e (c p) n -> p e c n", p=128)),
                   (x3[:, :, :, :], ew3.rearrange("e (c p) n -> p e c n", p=128))]
            nl = [(bqc[:, :], bq.rearrange("(c p) -> p c", p=128)),
                  (b1c[:, :], b1.rearrange("(c p) -> p c", p=128)),
                  (rb1c[:, :], rb1.rearrange("(c p) -> p c", p=128)),
                  (eb1c[:, :, :], eb1.rearrange("e (c p) -> p e c", p=128)),
                  (eb2c[:, :, :], eb2.rearrange("e (c p) -> p e c", p=128))]
            assert len(wl) + len(nl) == WLOADS and len(kl) == KLOADS
            for to, of in kl:
                sp.dma_start(to, of).then_inc(s_kload, 16)
            for to, of in wl:
                sp.dma_start(to, of).then_inc(s_wload, 16)
            with nc.allow_non_contiguous_dma("biases by partition"):
                for to, of in nl:
                    sp.dma_start(to, of).then_inc(s_wload, 16)

            for u in range(AU):
                sp.wait_ge(s_xts[u], 32 * (NT // AU))
                sp.wait_ge(s_xns[u], 16 * (NT // AU))
                sp.wait_ge(s_xss[u], 16 * (NT // AU))
            sp.wait_ge(s_nt, 1)
            with sp.Fori(0, KV_ROUNDS) as i:
                for u in range(2):
                    sp.wait_ge(s_kmm[u], i)
                    sp.dma_start(xm[:, u, :], xT_d[ds((i * 2 + u) * 128, 128), :]).then_inc(s_kx[u], 16)
            sp.wait_ge(s_kmm[0], KV_ROUNDS)

            def load_xm(m):
                past(sp, s_pq, m)
                sp.dma_start(xm[:, 0, :], xT_d[ds(m * 128, 128), :]).then_inc(s_xm, 16)

            def load_xr(m):
                past(sp, s_res, m)
                sp.dma_start(xr[:, :], xn_d[ds(m * P, P), :]).then_inc(s_xr, 16)

            def load_xo(m):
                past(sp, s_o, m)
                sp.dma_start(xo[:, :], xx_d[ds(m * P, P), :]).then_inc(s_xo, 16)

            def store_base(m):
                sp.wait_ge(s_o, m + 1)
                sp.dma_start(base_d[ds(m * P, P), :], ob[:, :]).then_inc(s_os, 16)

            load_xm(0)
            load_xr(0)
            load_xo(0)
            load_xm(1)
            load_xm(2)
            load_xr(1)
            load_xm(3)
            load_xr(2)
            with sp.Fori(0, NT - 4) as i:
                load_xm(i + 4)
                load_xr(i + 3)
                store_base(i)
                load_xo(i + 1)
            load_xr(NT - 1)
            for m in range(NT - 4, NT):
                store_base(m)
                if m + 1 < NT:
                    load_xo(m + 1)
            sp.wait_ge(s_os, 16 * NT)

            def load_base(j):
                sp.wait_ge(m_x, j)
                sp.dma_start(mb[:, :, :], base_d[ds(j * MT * P, MT * P), :].rearrange("(s p) n -> p s n", p=P)
                             ).then_inc(m_b, 16)

            def store_out(j):
                sp.wait_ge(m_oa, MT * NE * (j + 1))
                sp.dma_start(out[ds(j * MT * P, MT * P), :].rearrange("(s p) n -> p s n", p=P), mx[:, 1, :, :]
                             ).then_inc(m_st, 16)

            load_base(0)
            load_base(1)
            with sp.Fori(0, NJ - 2) as j:
                store_out(j)
                load_base(j + 2)
            store_out(NJ - 2)
            store_out(NJ - 1)
            sp.wait_ge(m_st, 16 * NJ)

        @block.gpsimd
        def _(pool):
            pool.memset(ident[:, :], 0.0).then_inc(s_const, 1)
            pool.wait_ge(s_const, 1)
            pool.affine_select(out=ident[:, :], in_=ident[:, :], compare_op=ALU.not_equal, fill=1.0, base=0,
                               pattern=[[-1, 128]], channel_multiplier=1).then_inc(s_const, 1)
            pool.iota(iota[:, :], [[1, P]], base=0, channel_multiplier=0,
                      allow_small_or_imprecise_dtypes=True).then_inc(s_const, 1)
            pool.iota(pos[:, 1, :], [[1, NP]], base=0, channel_multiplier=0,
                      allow_small_or_imprecise_dtypes=True).then_inc(s_const, 1)
            pool.iota(step[:, :], [[128, CH]], base=0, channel_multiplier=1,
                      allow_small_or_imprecise_dtypes=True).then_inc(s_const, 1)
            pool.memset(acc[:, :], 0.0).then_inc(s_const, 1)
            pool.wait_ge(s_tix, 1)
            def edge_rows(c):
                if c >= 2:
                    pool.wait_ge(s_tf, c - 1)
                at_pair = bass.IndirectOffsetOnAxis(ap=tpi[:, 0, c:c + 1], axis=0)
                pool.indirect_dma_start(sg[:, c % 2, :], None, src2, at_pair).then_inc(s_tg[c % 2], 16)
                pool.indirect_dma_start(dg[:, c % 2, :], None, dst2, at_pair).then_inc(s_tg[c % 2], 16)

            for c in range(2):
                edge_rows(c)
            with pool.Fori(0, NT // AU) as i:
                for u in range(AU):
                    pool.wait_ge(s_xn, i * AU + u + 1)
                    pool.wait_ge(s_xss[u], i * 16)
                    pool.tensor_tensor(xs[:, u, :], xin[:, u, :], xn[:, u, :], ALU.add).then_inc(s_xs, 1)
            for c in range(2, CH):
                edge_rows(c)
            for u in range(AU):
                pool.wait_ge(s_xts[u], 32 * (NT // AU))

            def gather(bt, k):
                pool.wait_ge(s_idx[bt], k + 1)
                settle(pool)
                for j in range(bt * BATCH, (bt + 1) * BATCH):
                    pool.indirect_dma_start(G[:, j, :], None, feat_d,
                                            bass.IndirectOffsetOnAxis(ap=idx[:, j:j + 1], axis=0)
                                            ).then_inc(s_g[bt], 16)

            for bt in range(BODY):
                gather(bt, 0)
            with pool.Fori(0, ROUNDS - 1) as k:
                for bt in range(BODY):
                    pool.wait_ge(s_sum, SB * (k * BODY + bt + 2))
                    gather(bt, k + 1)

        @block.scalar
        def _(act):
            def deviations(i):
                act.wait_ge(s_mv, i + 1)
                act.activation(rstd[:, 0, :], mv[:, :, 1], ACT.Sqrt, bias=eps[0:P, :]).then_inc(s_sd, 1)

            def block_T(i, u):
                t = i * AU + u
                act.wait_ge(s_xt, t + 1)
                past(act, s_xts[u], i * 32)
                act.activation(xT[:, u, :], bank[4 + u % 2][:, 0:2 * P], ACT.Copy).then_inc(s_xte, 1)
                act.wait_ge(s_xte, t + 1)
                act.dma_start(xT_d[ds(t * 128, 128), :], xT[:, u, :]).then_inc(s_xts[u], 16)

            def features(i, u):
                t = i * AU + u
                act.wait_ge(s_f, t + 1)
                act.activation(nodes[:, ds(t, 1), :].rearrange("p t h -> p (t h)"),
                               bank[6 + u % 2][0:P, D:ROW + H], ACT.Copy)
                act.activation(fe[:, u, :], bank[6 + u % 2][0:P, 0:ROW], ACT.Copy).then_inc(s_fe, 1)
                act.wait_ge(s_fe, t + 1)
                act.dma_start(feat_d[ds(t * P, P), :], fe[:, u, :]).then_inc(s_xts[u], 16)

            def first_round(i, last):
                block_T(i, 0)
                for u in range(AU):
                    if u + 1 < AU:
                        block_T(i, u + 1)
                    elif not last:
                        deviations(i + 1)
                    features(i, u)

            act.wait_ge(s_vconst, 1)
            deviations(0)
            with act.Fori(0, NT // AU - 1) as i:
                first_round(i, False)
            first_round(NT // AU - 1, True)

            def indices(bt, k):
                act.activation(idx[:, bt * BATCH:(bt + 1) * BATCH],
                               srct[:, ds(k * (SLOTS // PAIR) + bt * SB, SB), :].rearrange("p s u -> p (s u)"),
                               ACT.Copy).then_inc(s_idx[bt], 1)

            def transposes_out(n, par):
                act.wait_ge(s_st, n + 1)
                act.activation(ST[0:P, par, :], bank[0][0:P, :], ACT.Copy).then_inc(s_ste, 1)

            def edge_weights(n, bt):
                act.wait_ge(s_arg, n + 1)
                act.activation(G[:, bt * BATCH:(bt + 1) * BATCH, D:ROW], arg[:, 2, :, :], ACT.Exp
                               ).then_inc(s_w, 1)

            act.wait_ge(s_tc, CH)
            for bt in range(BODY):
                indices(bt, 0)
            transposes_out(0, 0)
            transposes_out(1, 1)
            edge_weights(0, 0)
            indices(0, 1)

            def edges(k, bt, last=False):
                n = k * BODY + bt
                if not last or bt + 2 < BODY:
                    act.wait_ge(s_er, n + 1)
                    transposes_out(n + 2, bt % 2)
                if not last or bt + 1 < BODY:
                    edge_weights(n + 1, (bt + 1) % BODY)
                if not last:
                    indices((bt + 1) % BODY, k + 1 + (bt + 1) // BODY)

            def keys(i, u):
                act.wait_ge(s_km, i * 2 + u + 1)
                act.activation(ke[:, u, :], ke[:, u, :], ACT.Exp).then_inc(s_ke, 1)

            with act.Fori(0, KV_ROUNDS) as i:
                edges(i, 0)
                keys(i, 0)
                edges(i, 1)
                edges(i, 2)
                keys(i, 1)
                edges(i, 3)

            act.wait_ge(s_wload, 16 * WLOADS)
            act.wait_ge(s_rs, 1)

            def queries_in(m):
                act.wait_ge(s_pq, m + 1)
                past(act, s_pa, m)
                for c in range(2):
                    last = act.activation(qb[:, c, :], bank[7][:, c * P:(c + 1) * P], ACT.Identity,
                                          bias=bqc[:, c:c + 1])
                last.then_inc(s_qb, 1)

            def queries_exp(m):
                act.wait_ge(s_qm, m + 1)
                act.activation(qe[:, :, :], qe[:, :, :], ACT.Exp).then_inc(s_qe, 1)

            def attention_T(m):
                act.wait_ge(s_pT, m + 1)
                past(act, s_po, m)
                act.activation(aT[:, :, :].rearrange("p c n -> p (c n)"), bank[4][:, 0:2 * P], ACT.Copy
                               ).then_inc(s_aT, 1)

            def deviation(i, blocks):
                if 1 in blocks:
                    act.wait_ge(s_mv1, i)
                if 3 in blocks:
                    act.wait_ge(s_mv2, i - 2)
                act.activation(zs[:, 20:22], zs[:, 17:20:2], ACT.Sqrt, bias=eps[0:P, :]).then_inc(s_sdm, 1)

            def norm_T(m):
                act.wait_ge(s_fy, m + 1)
                past(act, s_fh, m * 2)
                act.activation(yT[:, :, :].rearrange("p c n -> p (c n)"), bank[4][:, 0:2 * P], ACT.Copy
                               ).then_inc(s_yT, 1)

            def keep_norm(m):
                act.wait_ge(s_y, m + 1)
                past(act, s_r2, m)
                act.activation(y[:, 1, :], y[:, 0, :], ACT.Copy).then_inc(s_yc, 1)

            def hidden(m, half):
                act.wait_ge(s_fh, m * 2 + half + 1)
                past(act, s_fw if half else s_fa, m)
                for c in range(4):
                    ch = half * 4 + c
                    last = act.activation(hT[:, ch, :], bank[6 + half][:, c * P:(c + 1) * P], ACT.Relu,
                                          bias=b1c[:, ch:ch + 1])
                last.then_inc(s_h, 1)

            def mixer_round(i, blocks=range(DEPTH)):
                k = i + KV_ROUNDS
                edges(k, 0)
                if 1 in blocks:
                    attention_T(i - 1)
                if 2 in blocks:
                    keep_norm(i - 2)
                    hidden(i - 2, 0)
                edges(k, 1)
                if 0 in blocks:
                    queries_in(i)
                if 1 in blocks or 3 in blocks:
                    deviation(i, blocks)
                edges(k, 2)
                if 0 in blocks:
                    queries_exp(i)
                if 2 in blocks:
                    hidden(i - 2, 1)
                edges(k, 3)
                if 1 in blocks:
                    norm_T(i - 1)

            for i in range(DEPTH - 1):
                mixer_round(i, range(i + 1))
            with act.Fori(DEPTH - 1, NT) as i:
                mixer_round(i)
            for i in range(NT, NT + DEPTH - 1):
                mixer_round(i, range(i - NT + 1, DEPTH))
            with act.Fori(KV_ROUNDS + NT + DEPTH - 1, ROUNDS - 1) as k:
                for bt in range(BODY):
                    edges(k, bt)
            for bt in range(BODY):
                edges(ROUNDS - 1, bt, last=True)

            def elu_exp(j, s):
                act.wait_ge(m_em, j * MT + s + 1)
                act.activation(me[:, s, :], me[:, s, :], ACT.Exp).then_inc(m_ee, 1)

            def row_deviations(j):
                act.wait_ge(m_mv, j + 1)
                act.activation(mw[:, :, 1, 0:1], mw[:, :, 0, 1:2], ACT.Sqrt, bias=eps[0:P, :]).then_inc(m_sd, 1)

            def rows_T(j):
                act.wait_ge(m_fT, j + 1)
                act.wait_ge(m_c, j)
                act.activation(mfT[:, 0, :, :].rearrange("p c n -> p (c n)"), bank[0][:, 0:2 * MT * P],
                               ACT.Copy).then_inc(m_fe, 1)

            def router_hidden(j):
                act.wait_ge(m_r, j + 1)
                act.activation(mrh[:, :], bank[1][:, 0:MT * P], ACT.Relu, bias=rb1c[:, :]).then_inc(m_rr, 1)

            def router_exps(j):
                act.wait_ge(m_lm, j + 1)
                act.activation(mw[:, :, 3, 0:NE], mw[:, :, 2, 0:NE], ACT.Exp).then_inc(m_le, 1)
                act.wait_ge(m_d, j + 1)
                act.activation(mw[:, :, 8, 0:1], mw[:, :, 7, 0:1], ACT.Exp).then_inc(m_de, 1)

            def weights_T(j):
                act.wait_ge(m_wT, j + 1)
                act.wait_ge(m_bb, j)
                act.activation(wtT[:, :, :], bank[2][0:NE, 128:128 + MT * P].rearrange("p (s n) -> p s n", s=MT),
                               ACT.Copy).then_inc(m_we, 1)

            def place(j):
                act.wait_ge(m_fe, j + 1)
                act.wait_ge(m_h1, j * NE)
                act.activation(mfT[:, 1, :, :], mfT[:, 0, :, :], ACT.Copy).then_inc(m_c, 1)

            def relus(j, e, which):
                done, to, at_bank, bias, done_r, read = (
                    (m_h1, h1, 3, eb1c, m_h1r, m_h2) if which == 1 else (m_h2, h2, 4, eb2c, m_h2r, m_o))
                act.wait_ge(done, j * NE + e + 1)
                for c in range(2):
                    last = act.activation(to[:, e % 2, c, :], bank[at_bank][:, c * MT * P:(c + 1) * MT * P],
                                          ACT.Relu, bias=bias[:, e, c:c + 1])
                last.then_inc(done_r, 1)

            def tile_of_experts(j, ahead):
                place(j)
                relus(j, 0, 1)
                for e in range(NE):
                    if e + 1 < NE:
                        relus(j, e + 1, 1)
                    relus(j, e, 2)
                    if ahead:
                        if e == 0:
                            for s in range(MT):
                                elu_exp(j + 1, s)
                        if e == 1:
                            row_deviations(j + 1)
                        if e == 2:
                            rows_T(j + 1)
                        if e == 3:
                            router_hidden(j + 1)
                        if e == 4:
                            router_exps(j + 1)
                        if e == 5:
                            weights_T(j + 1)

            for s in range(MT):
                elu_exp(0, s)
            row_deviations(0)
            rows_T(0)
            router_hidden(0)
            router_exps(0)
            weights_T(0)
            with act.Fori(0, NJ - 1) as j:
                tile_of_experts(j, True)
            tile_of_experts(NJ - 1, False)

        @block.vector
        def _(dve):
            dve.memset(ones[:, :], 1.0)
            dve.memset(zero[:, :], 0.0)
            dve.memset(eps[:, :], EPS)
            dve.memset(nodes[:, :, :], 0.0)
            dve.memset(blk[:, 0:SB], 0)
            dve.memset(kvbd[:, :, :], 0.0).then_inc(s_vconst, 1)

            tab = Chain(dve, s_tab)
            dve.wait_ge(s_gload, 48)
            for c in range(2):
                for a in range(2):
                    tab(dve.tensor_tensor(prod[:, a, :], wext[:, c, 0:D], lr[:, a, :], ALU.mult))
                    tab(dve.tensor_reduce(wext[:, c, D + a * H:D + (a + 1) * H],
                                          prod[:, a, :].rearrange("p (h d) -> p h d", h=H), AX, ALU.add))
            assert tab.n == WEXT_LINKS
            dve.wait_ge(s_first, 16)
            tab(dve.tensor_copy(pos[:, 0, :], first[:, :]))
            tab(dve.tensor_scalar(pos[:, 0, :], pos[:, 0, :], 0.5, 1.0 / P, ALU.add, ALU.mult))
            tab(dve.tensor_scalar(first[:, :], pos[:, 0, :], -0.5, None, ALU.add))
            dve.wait_ge(s_const, 5)
            dve.tensor_tensor(pos[:, 0, :], first[:, :], pos[:, 1, :], ALU.add).then_inc(s_pos, 1)
            dve.wait_ge(s_tpe, 1)
            for c in range(CH):
                for b in range(2):
                    tab(dve.tensor_scalar(below[:, :], bank[b][:, 0:HALF], step[:, c:c + 1], 0.0,
                                          ALU.is_le, ALU.add, accum_out=count[:, b, c:c + 1]))
            tab(dve.scalar_tensor_tensor(out=tpair[:, 0, :], in0=count[:, 0, :], scalar=-1.0, in1=count[:, 1, :],
                                         op0=ALU.add, op1=ALU.add))
            tab(dve.tensor_scalar(tpair[:, 0, :], tpair[:, 0, :], 0.0, None, ALU.max))
            tab(dve.tensor_tensor(tpair[:, 1, :], step[:, :], tpair[:, 0, :], ALU.subtract))
            tab(dve.tensor_scalar(tpair[:, 1, :], tpair[:, 1, :], float(NT), None, ALU.min))
            tab(dve.tensor_scalar(tpair[:, 2, :], tpair[:, 1, :], float(P), None, ALU.mult))
            tab(dve.tensor_copy(tpi[:, 0, :], tpair[:, 0, :]))
            dve.tensor_copy(tpi[:, 1, :], tpair[:, 1, :]).then_inc(s_tix, 1)
            ch = Chain(dve, s_ach)
            with dve.Fori(0, NT // AU) as i:
                ch.start(i * (AU + 1))
                for u in range(AU):
                    dve.wait_ge(s_xin[u], (i + 1) * 16)
                    last = dve.bn_stats(stat[:, u, :], xin[:, u, :])
                    ch(last)
                settle(dve)
                for u in range(AU):
                    last = dve.bn_aggr(mv[:, u, :], stat[:, u, :])
                last.then_inc(s_mv, 1)
                dve.wait_ge(s_sd, i + 1)
                ch(dve.reciprocal(rstd[:, 1, :], rstd[:, 0, :]))
                for u in range(AU):
                    dve.wait_ge(s_xns[u], i * 16)
                    dve.wait_ge(s_xt, i * AU)
                    dve.wait_ge(s_xs, i * AU)
                    dve.tensor_scalar(xn[:, u, :], xin[:, u, :], mv[:, u, 0:1], rstd[:, 1, u:u + 1],
                                      ALU.subtract, ALU.mult).then_inc(s_xn, 1)

            for c in range(CH):
                dve.wait_ge(s_tg[c % 2], 32 * (c // 2 + 1))
                if c >= 1:
                    dve.wait_ge(s_tt, c)
                dve.tensor_copy(sf[:, :], sg[:, c % 2, :])
                dve.tensor_scalar(df[:, :], dg[:, c % 2, :], tpair[:, 2, c:c + 1], None, ALU.subtract
                                  ).then_inc(s_tf, 1)
                dve.wait_ge(s_tt, c + 1)
                dve.tensor_copy(srct[:, c * 128:(c + 1) * 128, :].rearrange("p s u -> p u s"),
                                bank[2 + c % 2][:, 0:PAIR * 128].rearrange("p (u s) -> p u s", u=PAIR))
                dve.tensor_copy(dstt[:, c * 128:(c + 1) * 128, :].rearrange("p s u -> p u s"),
                                bank[2 + c % 2][:, PAIR * 128:2 * PAIR * 128].rearrange("p (u s) -> p u s", u=PAIR)
                                ).then_inc(s_tc, 1)

            nch = Chain(dve, s_nch)
            dve.wait_ge(s_fe, NT)
            nch(dve.tensor_reduce(gmax[0:P, 0:H], nodes[:, 0:NT, 0:H].rearrange("p t h -> p h t"), AX, ALU.max))
            dve.memset(gmax[0:P, 4:5], 0.0).then_inc(s_gm, 1)
            dve.wait_ge(s_gm, 2)
            nch(dve.tensor_reduce(gmax[0:H, 5:6], bank[2][0:H, 0:P], AX, ALU.max))
            dve.tensor_scalar(gmax[0:H, 8:8 + H], ident[0:H, 0:H], gmax[0:H, 5:6], None, ALU.mult).then_inc(s_gm, 1)
            dve.wait_ge(s_gm, 4)
            nch(dve.tensor_copy(gmax[0:P, 12:16], bank[2][0:P, 256:256 + H]))
            one = ntmp[:, 0, :].rearrange("p (t h) -> p t h", h=2 * H)
            two = ntmp[:, 1, :].rearrange("p (t h) -> p t h", h=2 * H)
            nch(dve.tensor_tensor(one[:, :, 0:H], nodes[:, :, H:2 * H],
                                  gmax[0:P, 12:16].unsqueeze(1).to_broadcast([P, NCB, H]), ALU.add))
            nch(dve.tensor_copy(nodes[:, :, 0:H], nodes[:, :, H:2 * H]))
            nch(dve.scalar_tensor_tensor(out=nodes[:, :, H:2 * H], in0=one[:, :, 0:H], scalar=0.2,
                                         in1=one[:, :, 0:H], op0=ALU.mult, op1=ALU.max))
            flat = nodes[:, :, :].rearrange("p t h -> p (t h)")
            nch(dve.tensor_copy(nodep[:, 0, :], flat))
            nch(dve.tensor_tensor(ntmp[:, 0, :], flat, nodep[:, 0, :], ALU.subtract))
            nch(dve.tensor_copy(nodep[:, 1, :], ntmp[:, 0, :]))
            nch(dve.tensor_tensor(ntmp[:, 1, :], ntmp[:, 0, :], nodep[:, 1, :], ALU.subtract))
            for u in range(AU):
                dve.wait_ge(s_xns[u], 16 * (NT // AU))
                dve.wait_ge(s_xts[u], 32 * (NT // AU))
                dve.wait_ge(s_xss[u], 16 * (NT // AU))
            dve.tensor_copy(nodep[:, 2, :], ntmp[:, 1, :]).then_inc(s_nt, 1)
            dve.wait_ge(s_nt, 1)

            def one_hots(n, ring):
                columns = dstt[:, ds(n * SB, SB), :].rearrange("p s u -> p (s u)")
                dve.tensor_tensor(S[:, ring, :, :], iota[:, :].unsqueeze(1).to_broadcast([128, BATCH, P]),
                                  columns.unsqueeze(2).to_broadcast([128, BATCH, P]), ALU.is_equal
                                  ).then_inc(s_S, 1)

            def packed(pair):
                return dve.value_load(pack[0:1, 0, ds(pair, 1)], min_val=0, max_val=PACK ** 4 - 1)

            def add_sums(n, blocks):
                for q, b in enumerate(blocks):
                    dve.wait_ge(s_sum, n * SB + q + 1)
                    if not isinstance(n, int) or n * SB + q > 0:
                        dve.wait_ge(s_acc, n * SB + q)
                    dve.tensor_tensor(acc[:, ds(b * ROW, ROW)], bank[2 + q][0:P, 0:ROW],
                                      acc[:, ds(b * ROW, ROW)], ALU.add).then_inc(s_acc, 1)

            zch = Chain(dve, s_zch)

            def exponents(n, bt, rounds):
                slots = G[:, bt * BATCH:(bt + 1) * BATCH, :]
                dve.wait_ge(s_g[bt], rounds * (16 * BATCH))
                dve.wait_ge(s_er, n + 1)
                er = bank[1][:, 0:BATCH * 2 * H].rearrange("p (j h) -> p j h", j=BATCH)
                zch.start(n * 2)
                zch(dve.tensor_tensor(arg[:, 0, :, :], slots[:, :, D:ROW], er[:, :, 0:H], ALU.add))
                zch(dve.scalar_tensor_tensor(out=arg[:, 1, :, :], in0=arg[:, 0, :, :], scalar=0.2,
                                             in1=arg[:, 0, :, :], op0=ALU.mult, op1=ALU.max))
                dve.tensor_tensor(arg[:, 2, :, :], arg[:, 1, :, :], er[:, :, H:2 * H], ALU.subtract
                                  ).then_inc(s_arg, 1)

            def messages(n, bt):
                slots = G[:, bt * BATCH:(bt + 1) * BATCH, :]
                dve.wait_ge(s_w, n + 1)
                features = slots[:, :, 0:D].rearrange("p j (h d) -> p j h d", h=H)
                dve.tensor_tensor(features, features,
                                  slots[:, :, D:ROW].unsqueeze(3).to_broadcast([128, BATCH, H, HD]), ALU.mult
                                  ).then_inc(s_msg, 1)

            ahead = {}

            def edges(k, bt, last=False):
                n = k * BODY + bt
                if bt % 2 == 0:
                    ahead[0] = packed(k * 2 + bt // 2)
                add_sums(n, [unpack(ahead[0], bt % 2 * SB + q) for q in range(SB)])
                more = not last or bt + 1 < BODY
                if more:
                    exponents(n + 1, (bt + 1) % BODY, k + 1 + (bt + 1) // BODY)
                if not last or bt + 3 < BODY:
                    dve.wait_ge(s_sum, n * SB + SB)
                    one_hots(n + 3, (bt + 3) % BODY)
                if more:
                    messages(n + 1, (bt + 1) % BODY)

            dve.wait_ge(s_blk, 32)
            pch = Chain(dve, s_pack)
            digits = [blk[:, first_step:first_step + 4 * NPACK].rearrange("p (n q) -> p n q", q=4)
                      for first_step in (0, SB)]
            for digit in (2, 1, 0):
                for which in range(2):
                    more = digits[which][:, :, 3] if digit == 2 else packf[:, which, :]
                    pch(dve.scalar_tensor_tensor(out=packf[:, which, :], in0=more, scalar=float(PACK),
                                                 in1=digits[which][:, :, digit], op0=ALU.mult, op1=ALU.add))
            pch(dve.tensor_copy(pack[:, :, :], packf[:, :, :]))
            dve.wait_ge(s_const, 6)
            dve.wait_ge(s_tc, CH)
            for n in range(BODY - 1):
                one_hots(n, n)
            dve.memset(vb[:, :, :, 128:129], 1.0)
            exponents(0, 0, 1)
            messages(0, 0)

            kch = Chain(dve, s_kch)
            dve.wait_ge(s_kload, 16 * KLOADS)

            def keys_in(i, u):
                m = i * 2 + u
                dve.wait_ge(s_kmm[u], i + 1)
                dve.wait_ge(s_ka[u], i)
                kch.start(m)
                dve.tensor_tensor(vb[:, u, :, 0:128], bank[4][0:P, D:2 * D].rearrange("p (c n) -> p c n", c=2),
                                  rows[0:P, BV, :].rearrange("p (c n) -> p c n", c=2), ALU.add)
                kch(dve.tensor_tensor(kb[:, u, :], bank[4][0:P, 0:D], rows[0:P, BK, :], ALU.add))
                dve.tensor_scalar(ke[:, u, :], kb[:, u, :], 0.0, None, ALU.min).then_inc(s_km, 1)

            def keys_phi(i, u):
                dve.wait_ge(s_ke, i * 2 + u + 1)
                dve.scalar_tensor_tensor(out=kb[:, u, :], in0=kb[:, u, :], scalar=0.0, in1=ke[:, u, :],
                                         op0=ALU.max, op1=ALU.add).then_inc(s_kp, 1)

            with dve.Fori(0, KV_ROUNDS) as i:
                edges(i, 0)
                keys_in(i, 0)
                keys_phi(i, 0)
                edges(i, 1)
                edges(i, 2)
                keys_in(i, 1)
                keys_phi(i, 1)
                edges(i, 3)
            dve.wait_ge(s_kv, 1)
            for c in range(2):
                for h in range(4):
                    hp = slice(32 * h, 32 * h + 32)
                    dve.tensor_copy(kvbd[hp, c, 32 * h:32 * h + 32], bank[5 + c][hp, 32 * h:32 * h + 32])
                    last = dve.tensor_copy(kvbd[hp, c, 128 + h:129 + h], bank[5 + c][hp, 128:129])
            last.then_inc(s_kbd, 1)

            dve.wait_ge(s_wload, 16 * WLOADS)
            dve.memset(zs[:, :], 1.0).then_inc(s_rs, 1)
            mch = Chain(dve, s_mch)

            def queries_low(m):
                dve.wait_ge(s_qb, m + 1)
                dve.tensor_scalar(qe[:, :, :], qb[:, :, :], 0.0, None, ALU.min).then_inc(s_qm, 1)

            def queries_phi(m):
                dve.wait_ge(s_qe, m + 1)
                dve.scalar_tensor_tensor(out=qb[:, :, :], in0=qb[:, :, :], scalar=0.0, in1=qe[:, :, :],
                                         op0=ALU.max, op1=ALU.add).then_inc(s_qp, 1)

            def attention(m):
                dve.wait_ge(s_pa, m + 1)
                past(dve, s_pT, m)
                both = bank[5][0:P, 0:2 * (128 + H)].rearrange("p (c n) -> p c n", c=2)
                z = zs[:, 0:2 * H]
                mch.start(m * 2)
                mch(dve.tensor_scalar(z.rearrange("p (c h) -> p c h", c=2), both[:, :, 128:128 + H], 1e-6, None,
                                      ALU.add))
                mch(dve.reciprocal(z, z))
                dve.tensor_tensor(at[:, :].rearrange("p (c h d) -> p c h d", c=2, h=H),
                                  both[:, :, 0:128].rearrange("p c (h d) -> p c h d", h=H),
                                  z.rearrange("p (c h) -> p c h", c=2).unsqueeze(3).to_broadcast([P, 2, H, MD]),
                                  ALU.mult).then_inc(s_at, 1)

            rch = [Chain(dve, s_rch), Chain(dve, s_r2ch)]

            def moments(k, m, bias, column, mean_var):
                if k == 1:
                    dve.wait_ge(s_r2, m + 1)
                rch[k].start(m * 2)
                rch[k](dve.tensor_tensor(res[:, k, :], res[:, k, :], rows[0:P, bias, :], ALU.add))
                rch[k](dve.bn_stats(zs[:, 32 + 8 * k:38 + 8 * k], res[:, k, :]))
                settle(dve)
                dve.bn_aggr(zs[:, column:column + 2], zs[:, 32 + 8 * k:38 + 8 * k]).then_inc(mean_var, 1)

            nln = [Chain(dve, s_lch), Chain(dve, s_l2ch)]

            def reciprocals(i):
                dve.wait_ge(s_sdm, i)
                dve.reciprocal(zs[:, 22:24], zs[:, 20:22]).then_inc(s_rs, 1)
                dve.wait_ge(s_rs, i + 1)

            def norm(k, m, gain, shift, to):
                mean = 16 + 2 * k
                nln[k].start(m)
                nln[k](dve.scalar_tensor_tensor(out=res[:, k, :], in0=res[:, k, :], scalar=zs[:, mean:mean + 1],
                                                in1=rows[0:P, gain, :], op0=ALU.subtract, op1=ALU.mult))
                return dve.scalar_tensor_tensor(out=to, in0=res[:, k, :], scalar=zs[:, 22 + k:23 + k],
                                                in1=rows[0:P, shift, :], op0=ALU.mult, op1=ALU.add)

            def first_residual(m):
                dve.wait_ge(s_po, m + 1)
                dve.wait_ge(s_xr, (m + 1) * 16)
                dve.tensor_tensor(res[:, 0, :], bank[5][0:P, 0:D], xr[:, :], ALU.add).then_inc(s_res, 1)
                dve.wait_ge(s_res, m + 1)
                moments(0, m, BO, 16, s_mv1)

            def first_norm(m):
                past(dve, s_fy, m)
                past(dve, s_yc, m)
                norm(0, m, G1, E1, y[:, 0, :]).then_inc(s_y, 1)

            def second_residual(m):
                dve.wait_ge(s_fw, m + 1)
                dve.wait_ge(s_yc, m + 1)
                past(dve, s_o, m)
                dve.tensor_tensor(res[:, 1, :], bank[6][0:P, 0:D], y[:, 1, :], ALU.add).then_inc(s_r2, 1)

            och = Chain(dve, s_och)

            def result(m):
                past(dve, s_os, m * 16)
                och.start(m)
                och(norm(1, m, G2, E2, ob[:, :]))
                dve.wait_ge(s_xo, (m + 1) * 16)
                dve.tensor_tensor(ob[:, :], ob[:, :], xo[:, :], ALU.add).then_inc(s_o, 1)

            def mixer_round(i, blocks=range(DEPTH)):
                k = i + KV_ROUNDS
                edges(k, 0)
                if 3 in blocks:
                    moments(1, i - 3, B2, 18, s_mv2)
                edges(k, 1)
                if 0 in blocks:
                    queries_low(i)
                if 1 in blocks:
                    first_residual(i - 1)
                edges(k, 2)
                if 0 in blocks:
                    queries_phi(i)
                if 1 in blocks or 3 in blocks:
                    reciprocals(i)
                if 1 in blocks:
                    first_norm(i - 1)
                edges(k, 3)
                if 0 in blocks:
                    attention(i)
                if 3 in blocks:
                    result(i - 3)
                if 2 in blocks:
                    second_residual(i - 2)

            for i in range(DEPTH - 1):
                mixer_round(i, range(i + 1))
            with dve.Fori(DEPTH - 1, NT) as i:
                mixer_round(i)
            for i in range(NT, NT + DEPTH - 1):
                mixer_round(i, range(i - NT + 1, DEPTH))
            with dve.Fori(KV_ROUNDS + NT + DEPTH - 1, ROUNDS - 1) as k:
                for bt in range(BODY):
                    edges(k, bt)
            for bt in range(BODY):
                edges(ROUNDS - 1, bt, last=True)
            rest = packed(BATCHES // 2)
            add_sums(BATCHES, [unpack(rest, q) for q in range(SB)])

            mc = Chain(dve, m_ch)

            def graph_rows(j, s):
                b = j * MT + s
                sums = acc[:, ds(b * ROW, ROW)]
                mc(dve.tensor_scalar(mw[:, s, 9, 0:H], sums[:, D:ROW], 1e-37, None, ALU.max))
                mc(dve.reciprocal(mw[:, s, 9, 0:H], mw[:, s, 9, 0:H]))
                mc(dve.tensor_tensor(mf[:, s, :].rearrange("p (h d) -> p h d", h=H),
                                     sums[:, 0:D].rearrange("p (h d) -> p h d", h=H),
                                     mw[:, s, 9, 0:H].unsqueeze(2).to_broadcast([P, H, HD]), ALU.mult))
                mc(dve.tensor_tensor(mf[:, s, :], mf[:, s, :], rows[0:P, GB, :], ALU.add))
                dve.tensor_scalar(me[:, s, :], mf[:, s, :], 0.0, None, ALU.min).then_inc(m_em, 1)

            def base_rows(j):
                dve.wait_ge(m_b, (j + 1) * 16)
                for s in range(MT):
                    dve.wait_ge(m_ee, j * MT + s + 1)
                    mc(dve.scalar_tensor_tensor(out=mf[:, s, :], in0=mf[:, s, :], scalar=0.0, in1=me[:, s, :],
                                                op0=ALU.max, op1=ALU.add))
                    last = dve.scalar_tensor_tensor(out=mx[:, 0, s, :], in0=mf[:, s, :], scalar=-1.0,
                                                    in1=mb[:, s, :], op0=ALU.add, op1=ALU.add)
                    if s == MT - 1:
                        last.then_inc(m_x, 1)
                        dve.wait_ge(m_x, j + 1)
                    else:
                        mc(last)
                for s in range(MT):
                    mc(dve.bn_stats(mw[:, s, 10, 0:6], mx[:, 0, s, :]))
                settle(dve)
                for s in range(MT):
                    last = dve.bn_aggr(mw[:, s, 0, 0:2], mw[:, s, 10, 0:6])
                last.then_inc(m_mv, 1)

            def norm_rows(j):
                dve.wait_ge(m_sd, j + 1)
                mc(dve.reciprocal(mw[:, :, 1, 1:2], mw[:, :, 1, 0:1]))
                for s in range(MT):
                    last = dve.tensor_scalar(mf[:, s, :], mx[:, 0, s, :], mw[:, s, 0, 0:1], mw[:, s, 1, 1:2],
                                             ALU.subtract, ALU.mult)
                last.then_inc(m_f, 1)

            def route(j):
                dve.wait_ge(m_l, j + 1)
                logits = bank[2][0:P, 0:MT * 8].rearrange("p (s n) -> p s n", s=MT)[:, :, 0:NE]
                mc(dve.tensor_tensor(mw[:, :, 2, 0:NE], logits,
                                     rb2r[0:P, :].unsqueeze(1).to_broadcast([P, MT, NE]), ALU.add))
                mc(dve.tensor_reduce(mw[:, :, 1, 2:3].rearrange("p s n -> p (s n)"), mw[:, :, 2, 0:NE], AX, ALU.max))
                dve.tensor_tensor(mw[:, :, 2, 0:NE], mw[:, :, 2, 0:NE],
                                  mw[:, :, 1, 2:3].to_broadcast([P, MT, NE]), ALU.subtract).then_inc(m_lm, 1)
                dve.wait_ge(m_le, j + 1)
                mc(dve.tensor_reduce(mw[:, :, 1, 3:4].rearrange("p s n -> p (s n)"), mw[:, :, 3, 0:NE], AX, ALU.add))
                mc(dve.reciprocal(mw[:, :, 1, 4:5], mw[:, :, 1, 3:4]))
                mc(dve.tensor_tensor(mw[:, :, 3, 0:NE], mw[:, :, 3, 0:NE],
                                     mw[:, :, 1, 4:5].to_broadcast([P, MT, NE]), ALU.mult))
                for s in range(MT):
                    settle(dve)
                    mc(dve.max(mw[:, s, 4, :], mw[:, s, 3, :]))
                    settle(dve)
                    mc(dve.max_index(mi[:, s, :], mw[:, s, 4, :], mw[:, s, 3, :]))
                dve.tensor_tensor(mw[:, :, 7, 0:1], mw[:, :, 4, 1:2], mw[:, :, 4, 0:1], ALU.subtract
                                  ).then_inc(m_d, 1)
                dve.wait_ge(m_de, j + 1)
                mc(dve.tensor_copy(mw[:, :, 5, :], mi[:, :, :]))
                mc(dve.tensor_scalar(mw[:, :, 8, 1:2], mw[:, :, 8, 0:1], 1.0, None, ALU.add))
                mc(dve.reciprocal(mw[:, :, 8, 2:3], mw[:, :, 8, 1:2]))
                mc(dve.tensor_tensor(mw[:, :, 8, 3:4], mw[:, :, 8, 0:1], mw[:, :, 8, 2:3], ALU.mult))
                for s in range(MT):
                    for r in range(2):
                        mc(dve.tensor_scalar(mw[:, s, 11 + r, 0:NE], iota[0:P, 0:NE], mw[:, s, 5, r:r + 1],
                                             mw[:, s, 8, 2 + r:3 + r], ALU.is_equal, ALU.mult))
                dve.wait_ge(m_s, j)
                dve.tensor_tensor(wt[:, 0, :, :], mw[:, :, 11, 0:NE], mw[:, :, 12, 0:NE], ALU.add).then_inc(m_wt, 1)
                dve.wait_ge(m_wt, j + 1)

            def start_tile(j):
                dve.wait_ge(m_bb, j + 1)
                dve.wait_ge(m_st, j * 16)
                dve.tensor_copy(wt[:, 1, :, :], wt[:, 0, :, :])
                dve.tensor_tensor(mx[:, 1, :, :].rearrange("p s n -> p (s n)"),
                                  mx[:, 0, :, :].rearrange("p s n -> p (s n)"), bank[7][0:P, 0:MT * D], ALU.add
                                  ).then_inc(m_s, 1)
                dve.wait_ge(m_s, j + 1)

            def add_expert(j, e):
                for s in range(MT):
                    dve.wait_ge(m_o, (j * NE + e) * MT + s + 1)
                    if e >= 1:
                        dve.wait_ge(m_oa, (j * NE + e - 1) * MT + s + 1)
                    dve.scalar_tensor_tensor(out=mx[:, 1, s, :], in0=bank[5 + s][0:P, 0:D],
                                             scalar=wt[:, 1, s, e:e + 1], in1=mx[:, 1, s, :],
                                             op0=ALU.mult, op1=ALU.add).then_inc(m_oa, 1)

            def tile_of_experts(j, ahead):
                start_tile(j)
                for e in range(NE):
                    if ahead:
                        if e == 0:
                            for s in range(MT):
                                graph_rows(j + 1, s)
                        if e == 1:
                            base_rows(j + 1)
                            norm_rows(j + 1)
                        if e == 4:
                            route(j + 1)
                    add_expert(j, e)

            mc(dve.memset(mw[:, :, 3, :], -1.0))
            for s in range(MT):
                graph_rows(0, s)
            base_rows(0)
            norm_rows(0)
            route(0)
            pro = mc.n
            with dve.Fori(0, NJ - 1) as j:
                mc.start(pro + j * (pro - 1))
                tile_of_experts(j, True)
                assert mc.n == pro - 1, (mc.n, pro)
            tile_of_experts(NJ - 1, False)

        @block.tensor
        def _(pe):
            pe.wait_ge(s_vconst, 1)
            pe.wait_ge(s_const, 5)
            pe.wait_ge(s_pos, 1)
            for b in range(2):
                last = pe.matmul(bank[b][:, 0:HALF], ones[0:1, :], pos[:, 0, b * HALF:(b + 1) * HALF],
                                 start=True, stop=True)
            last.then_inc(s_tpe, 1)
            pe.wait_ge(s_tab, WEXT_LINKS)

            def block_T(i, u):
                t = i * AU + u
                pe.wait_ge(s_xn, t + 1)
                pe.wait_ge(s_xte, t - 1 if u >= 2 else i * AU)
                for c in range(2):
                    last = pe.transpose(bank[4 + u % 2][:, c * P:(c + 1) * P], xn[:, u, c * 128:(c + 1) * 128],
                                        ident[0:P, 0:P])
                last.then_inc(s_xt, 1)

            with pe.Fori(0, NT // AU) as i:
                block_T(i, 0)
                for u in range(AU):
                    t = i * AU + u
                    if u + 1 < AU:
                        block_T(i, u + 1)
                    pe.wait_ge(s_xte, t + 1)
                    pe.wait_ge(s_fe, t - 1 if u >= 2 else i * AU)
                    for c in range(2):
                        last = pe.matmul(bank[6 + u % 2][0:P, 0:ROW + H], xT[:, u, c * P:(c + 1) * P], wext[:, c, :],
                                         start=(c == 0), stop=(c == 1))
                    last.then_inc(s_f, 1)

            for c in range(CH):
                pe.wait_ge(s_tf, c + 1)
                if c >= 2:
                    pe.wait_ge(s_tc, c - 1)
                for n, rows_ in enumerate((sf, df)):
                    for u in range(PAIR):
                        q = n * PAIR + u
                        last = pe.transpose(bank[2 + c % 2][:, q * 128:(q + 1) * 128],
                                            rows_[:, u * TE:(u + 1) * TE], ident[:, :])
                last.then_inc(s_tt, 1)

            pe.wait_ge(s_gm, 1)
            pe.transpose(bank[2][0:H, 0:P], gmax[0:P, 0:H], ident[0:P, 0:P]).then_inc(s_gm, 1)
            pe.wait_ge(s_gm, 3)
            pe.matmul(bank[2][0:P, 256:256 + H], ones[0:H, 0:P], gmax[0:H, 8:8 + H], start=True, stop=True
                      ).then_inc(s_gm, 1)

            def transposes(n, ring):
                pe.wait_ge(s_S, n + 1)
                for j in range(BATCH):
                    last = pe.transpose(bank[0][0:P, j * TE:(j + 1) * TE], S[:, ring, j, :], ident[:, :])
                last.then_inc(s_st, 1)

            def packed(pair):
                return pe.value_load(pack[0:1, 1, ds(pair, 1)], min_val=0, max_val=PACK ** 4 - 1)

            def logits(n, par, blocks):
                pe.wait_ge(s_ste, n + 1)
                for q, b in enumerate(blocks):
                    for j in range(q * PAIR, (q + 1) * PAIR):
                        for part in range(3):
                            last = pe.matmul(bank[1][:, j * 2 * H:(j + 1) * 2 * H],
                                             ST[0:P, par, j * TE:(j + 1) * TE],
                                             nodep[:, part, ds(b * (2 * H), 2 * H)],
                                             start=(part == 0), stop=(part == 2))
                last.then_inc(s_er, 1)

            ahead = {}

            def edges(k, bt, last=False, beside=()):
                n = k * BODY + bt
                if not last or bt + 1 < BODY:
                    pe.wait_ge(s_arg, n + 1)
                    if bt == 0:
                        now = packed(k * 2)
                    else:
                        now = ahead[0]
                    logits(n + 1, (bt + 1) % 2, [unpack(now, (bt + 1) % 2 * SB + q) for q in range(SB)])
                if not last or bt + 2 < BODY:
                    pe.wait_ge(s_ste, n + 2)
                    transposes(n + 2, (bt + 2) % BODY)
                for product, *which in beside:
                    product(*which)
                if bt == 0 or (bt == 2 and not last):
                    ahead[0] = packed(k * 2 + bt // 2 + 1)
                pe.wait_ge(s_msg, n + 1)
                for q in range(SB):
                    pe.wait_ge(s_acc, n * SB + q + 1)
                    for u in range(PAIR):
                        j = q * PAIR + u
                        done = pe.matmul(bank[2 + q][0:P, 0:ROW], S[:, bt, j, :], G[:, bt * BATCH + j, :],
                                         start=(u == 0), stop=(u == PAIR - 1))
                    done.then_inc(s_sum, 1)

            pe.wait_ge(s_nt, 1)
            transposes(0, 0)
            pe.wait_ge(s_blk, 32)
            pe.wait_ge(s_pack, 7)
            blocks_0 = packed(0)
            logits(0, 0, [unpack(blocks_0, q) for q in range(SB)])
            pe.wait_ge(s_ste, 1)
            transposes(1, 1)
            for q in range(SB):
                pe.matmul(bank[2 + q][0:P, 0:ROW], zero[:, 0:P], zero[:, :], start=True, stop=True
                          ).then_inc(s_sum, 1)

            pe.wait_ge(s_kload, 16 * KLOADS)
            for c in range(2):
                pe.matmul(bank[5 + c][:, 0:129], zero[:, 0:128], zero[:, 0:129], start=True, stop=False)

            def keys_values(i, u):
                pe.wait_ge(s_kx[u], (i + 1) * 16)
                pe.wait_ge(s_km, i * 2 + u)
                for c in range(2):
                    last = pe.matmul(bank[4][0:P, :], xm[:, u, c * P:(c + 1) * P], wkv[:, c, :],
                                     start=(c == 0), stop=(c == 1))
                last.then_inc(s_kmm[u], 1)

            def add_kv(i, u):
                pe.wait_ge(s_kp, i * 2 + u + 1)
                for c in range(2):
                    last = pe.matmul(bank[5 + c][:, 0:129], kb[:, u, c * 128:(c + 1) * 128], vb[:, u, c, :],
                                     start=False, stop=False)
                last.then_inc(s_ka[u], 1)

            with pe.Fori(0, KV_ROUNDS) as i:
                edges(i, 0, beside=[(keys_values, i, 0)])
                edges(i, 1, beside=[(add_kv, i, 0)])
                edges(i, 2, beside=[(keys_values, i, 1)])
                edges(i, 3, beside=[(add_kv, i, 1)])
            for c in range(2):
                last = pe.matmul(bank[5 + c][:, 0:129], zero[:, 0:128], zero[:, 0:129], start=False, stop=True)
            last.then_inc(s_kv, 1)

            def queries(m):
                pe.wait_ge(s_xm, (m + 1) * 16)
                past(pe, s_h, m * 2 - 4)
                for o in range(2):
                    for c in range(2):
                        last = pe.matmul(bank[7][:, o * P:(o + 1) * P], wq[:, c, o * 128:(o + 1) * 128],
                                         xm[:, 0, c * P:(c + 1) * P], start=(c == 0), stop=(c == 1))
                last.then_inc(s_pq, 1)

            def attend(m):
                pe.wait_ge(s_qp, m + 1)
                past(pe, s_res, m)
                for c in range(2):
                    last = pe.matmul(bank[5][0:P, c * (128 + H):(c + 1) * (128 + H)], qb[:, c, :], kvbd[:, c, :],
                                     start=True, stop=True)
                last.then_inc(s_pa, 1)

            def attention_T(m):
                pe.wait_ge(s_at, m + 1)
                past(pe, s_yT, m)
                for c in range(2):
                    last = pe.transpose(bank[4][:, c * P:(c + 1) * P], at[:, c * 128:(c + 1) * 128],
                                        ident[0:P, 0:P])
                last.then_inc(s_pT, 1)

            def project(m):
                pe.wait_ge(s_aT, m + 1)
                for c in range(2):
                    last = pe.matmul(bank[5][0:P, 0:D], aT[:, c, :], wo[:, c, :], start=(c == 0), stop=(c == 1))
                last.then_inc(s_po, 1)

            def norm_T(m):
                pe.wait_ge(s_y, m + 1)
                for c in range(2):
                    last = pe.transpose(bank[4][:, c * P:(c + 1) * P], y[:, 0, c * 128:(c + 1) * 128],
                                        ident[0:P, 0:P])
                last.then_inc(s_fy, 1)

            def hidden(m, half, newest):
                pe.wait_ge(s_yT, m + 1)
                if half == 0:
                    past(pe, s_r2, m)
                elif newest is not None:
                    pe.wait_ge(s_qb, newest + 1)
                for c4 in range(4):
                    f = (half * 4 + c4) * 128
                    for c in range(2):
                        last = pe.matmul(bank[6 + half][:, c4 * P:(c4 + 1) * P], w1[:, c, f:f + 128], yT[:, c, :],
                                         start=(c == 0), stop=(c == 1))
                last.then_inc(s_fh, 1)

            def second_layer(m, half):
                pe.wait_ge(s_h, m * 2 + half + 1)
                for f in range(half * 4, half * 4 + 4):
                    last = pe.matmul(bank[6][0:P, 0:D], hT[:, f, :], w2[:, f, :], start=(f == 0), stop=(f == 7))
                last.then_inc(s_fw if half else s_fa, 1)

            def mixer_round(i, blocks=range(DEPTH)):
                k = i + KV_ROUNDS
                beside = [[] for _ in range(BODY)]
                if 1 in blocks:
                    beside[0] += [(attention_T, i - 1)]
                    beside[1] += [(project, i - 1)]
                if 2 in blocks:
                    beside[0] += [(hidden, i - 2, 0, None)]
                    beside[1] += [(second_layer, i - 2, 0)]
                    beside[2] += [(hidden, i - 2, 1, i if 0 in blocks else None)]
                if 0 in blocks:
                    beside[1] = [(queries, i)] + beside[1]
                if 2 in blocks:
                    beside[3] += [(second_layer, i - 2, 1)]
                if 0 in blocks:
                    beside[3] += [(attend, i)]
                if 1 in blocks:
                    beside[3] += [(norm_T, i - 1)]
                for bt in range(BODY):
                    edges(k, bt, beside=beside[bt])

            pe.wait_ge(s_kbd, 1)
            pe.wait_ge(s_wload, 16 * WLOADS)
            for i in range(DEPTH - 1):
                mixer_round(i, range(i + 1))
            with pe.Fori(DEPTH - 1, NT) as i:
                mixer_round(i)
            for i in range(NT, NT + DEPTH - 1):
                mixer_round(i, range(i - NT + 1, DEPTH))
            with pe.Fori(KV_ROUNDS + NT + DEPTH - 1, ROUNDS - 1) as k:
                for bt in range(BODY):
                    edges(k, bt)
            for bt in range(BODY):
                edges(ROUNDS - 1, bt, last=True)

            def rows_T(j):
                pe.wait_ge(m_f, j + 1)
                pe.wait_ge(m_fe, j)
                for s in range(MT):
                    for c in range(2):
                        last = pe.transpose(bank[0][:, c * MT * P + s * P:c * MT * P + (s + 1) * P],
                                            mf[:, s, c * 128:(c + 1) * 128], ident[0:P, 0:P])
                last.then_inc(m_fT, 1)

            def router_1(j):
                pe.wait_ge(m_fe, j + 1)
                for c in range(2):
                    last = pe.matmul(bank[1][:, 0:MT * P], r1[:, c, :], mfT[:, 0, c, :], start=(c == 0), stop=(c == 1))
                last.then_inc(m_r, 1)

            def router_2(j):
                pe.wait_ge(m_rr, j + 1)
                pe.wait_ge(m_we, j)
                for s in range(MT):
                    last = pe.matmul(bank[2][0:P, s * 8:s * 8 + NE], mrh[:, s * P:(s + 1) * P], r2[:, :],
                                     start=True, stop=True)
                last.then_inc(m_l, 1)

            def weights_T(j):
                pe.wait_ge(m_wt, j + 1)
                for s in range(MT):
                    last = pe.transpose(bank[2][0:NE, 128 + s * P:128 + (s + 1) * P], wt[:, 0, s, :],
                                        ident[0:P, 0:P])
                last.then_inc(m_wT, 1)

            def biases(j):
                pe.wait_ge(m_we, j + 1)
                pe.wait_ge(m_s, j)
                for s in range(MT):
                    last = pe.matmul(bank[7][0:P, s * D:(s + 1) * D], wtT[:, s, :], e3b[:, :], start=True, stop=True)
                last.then_inc(m_bb, 1)

            def layer_1(j, e):
                pe.wait_ge(m_c, j + 1)
                pe.wait_ge(m_h1r, j * NE + e)
                for o in range(2):
                    for c in range(2):
                        last = pe.matmul(bank[3][:, o * MT * P:(o + 1) * MT * P], x1[:, e, c, o * 128:(o + 1) * 128],
                                         mfT[:, 1, c, :], start=(c == 0), stop=(c == 1))
                last.then_inc(m_h1, 1)

            def layer_2(j, e):
                pe.wait_ge(m_h1r, j * NE + e + 1)
                pe.wait_ge(m_h2r, j * NE + e)
                for o in range(2):
                    for c in range(2):
                        last = pe.matmul(bank[4][:, o * MT * P:(o + 1) * MT * P], x2[:, e, c, o * 128:(o + 1) * 128],
                                         h1[:, e % 2, c, :], start=(c == 0), stop=(c == 1))
                last.then_inc(m_h2, 1)

            def layer_3(j, e):
                pe.wait_ge(m_h2r, j * NE + e + 1)
                for s in range(MT):
                    if e >= 1:
                        pe.wait_ge(m_oa, (j * NE + e - 1) * MT + s + 1)
                    else:
                        pe.wait_ge(m_oa, j * (NE * MT))
                    for c in range(2):
                        last = pe.matmul(bank[5 + s][0:P, 0:D], h2[:, e % 2, c, s * P:(s + 1) * P], x3[:, e, c, :],
                                         start=(c == 0), stop=(c == 1))
                    last.then_inc(m_o, 1)

            def tile_of_experts(j, ahead):
                layer_1(j, 0)
                for e in range(NE):
                    if e + 1 < NE:
                        layer_1(j, e + 1)
                    layer_2(j, e)
                    if e >= 1:
                        layer_3(j, e - 1)
                    if ahead:
                        if e == 2:
                            rows_T(j + 1)
                        if e == 3:
                            router_1(j + 1)
                        if e == 4:
                            router_2(j + 1)
                        if e == 5:
                            weights_T(j + 1)
                layer_3(j, NE - 1)
                if ahead:
                    biases(j + 1)

            pe.wait_ge(s_os, 16 * NT)
            rows_T(0)
            router_1(0)
            router_2(0)
            weights_T(0)
            biases(0)
            with pe.Fori(0, NJ - 1) as j:
                tile_of_experts(j, True)
            tile_of_experts(NJ - 1, False)


_INS = ['x', 'src', 'dst', 'L0_gnn_W', 'L0_gnn_attn_l', 'L0_gnn_attn_r', 'L0_gnn_bias', 'L0_mix_Wq', 'L0_mix_bq',
        'L0_mix_Wk', 'L0_mix_bk', 'L0_mix_Wv', 'L0_mix_bv', 'L0_mix_Wo', 'L0_mix_bo', 'L0_mix_W1', 'L0_mix_b1',
        'L0_mix_W2', 'L0_mix_b2', 'L0_mix_ln1_g', 'L0_mix_ln1_b', 'L0_mix_ln2_g', 'L0_mix_ln2_b',
        'L0_ffn_router_w1', 'L0_ffn_router_b1', 'L0_ffn_router_w2', 'L0_ffn_router_b2', 'L0_ffn_expert_w1',
        'L0_ffn_expert_b1', 'L0_ffn_expert_w2', 'L0_ffn_expert_b2', 'L0_ffn_expert_w3', 'L0_ffn_expert_b3']


def kernel(**inputs):
    import numpy as np
    import concourse.bacc as bacc
    from concourse import mybir as _mybir
    from concourse.bass_utils import run_bass_kernel_spmd

    nc = bacc.Bacc("TRN2", target_bir_lowering=False, num_devices=1)
    arrays, args = {}, []
    for name in _INS:
        a = np.ascontiguousarray(inputs[name])
        if name in ('src', 'dst'):
            pad = np.full(EPAD - E, 0 if name == 'src' else N, a.dtype)
            a = np.concatenate([a, pad])
        arrays[f"in_{name}"] = a
        args.append(nc.dram_tensor(f"in_{name}", a.shape, _mybir.dt.from_np(a.dtype), kind="ExternalInput").ap())
    args.append(nc.dram_tensor("out_x", (N, D), _mybir.dt.float32, kind="ExternalOutput").ap())
    gps_layer(nc, *args)
    r = run_bass_kernel_spmd(nc, [arrays], core_ids=[0])
    return r.results[0]["out_x"]
```

```python
from contextlib import ExitStack

import concourse.bass as bass
from concourse import mybir

N, D, E, H, HD = 6250, 256, 206250, 4, 64
P = 125
NT = N // P
TE = 128
PAIR = 2
NP = -(-E // (TE * PAIR))
EPAD = NP * PAIR * TE
BATCH = 4
BODY = 4
SLOTS = BATCH * BODY
SB = BATCH // PAIR
ROUNDS = -(-(NP + NT) * PAIR // SLOTS)
CH = -(-(ROUNDS * SLOTS // PAIR + 4) // 128)
ROW = D + H
NCB = NT + 1
MH, MD = 8, 32
FF = 1024
RH = 128
NE = 6
MT = 2
NJ = NT // MT
EPS = 1e-5
AU = 5
AR = NT // AU
TABLE_ROUNDS = 4
CHUNK_ROUNDS = 4
HALF = NP // 2
KV_ROUNDS = NT // 2
KLOADS = 4
WLOADS = 31
WSPREAD = 20
WEXT_LINKS = 8
PACK = 64
NPACK = (CH * 128 - 2) // 4
BATCHES = ROUNDS * BODY
DEPTH = 4
PASS = 6
TRIPLES = -(-(NT + DEPTH - 1) // 2)
assert N == NT * P and NP == 2 * HALF and NT == AU * AR and AR % 2 == 0 and 2 * PASS == 3 * BODY and NT % 2 == 0
assert KV_ROUNDS + 3 * TRIPLES == ROUNDS - 1


class Chain:

    def __init__(self, engine, semaphore):
        self.engine, self.semaphore, self.base, self.n = engine, semaphore, 0, 0

    def start(self, base):
        self.base, self.n = base, 0

    def __call__(self, instruction):
        self.issue(instruction)
        self.wait()

    def issue(self, instruction):
        self.n += 1
        instruction.then_inc(self.semaphore, 1)

    def wait(self):
        self.engine.wait_ge(self.semaphore, self.base + self.n)


def unpack(packed, digit):
    value = packed // PACK ** digit if digit else packed
    return (value % PACK if digit < 3 else value).with_bounds(min_val=0, max_val=NT)


def mixer_batch(triple, half, s):
    n = half * PASS + s
    return KV_ROUNDS + triple * 3 + n // BODY, n % BODY


def active(i):
    return [b for b in range(DEPTH) if not isinstance(i, int) or 0 <= i - b < NT]


def parts(*sizes, end):
    at, slices = 0, []
    for size in sizes:
        size = -(-size // 8) * 8
        slices.append(slice(at, at + size))
        at += size
    return slices + [slice(at, end)]


def past(engine, semaphore, value):
    if not isinstance(value, int) or value > 0:
        engine.wait_ge(semaphore, value)


def gps_layer(nc, x, src, dst, gW, attn_l, attn_r, gbias, Wq, bq, Wk, bk, Wv, bv, Wo, bo, W1, b1, W2, b2,
              g1, be1, g2, be2, rw1, rb1, rw2, rb2, ew1, eb1, ew2, eb2, ew3, eb3, out):
    fp32, bf16, i32, u32 = mybir.dt.float32, mybir.dt.bfloat16, mybir.dt.int32, mybir.dt.uint32
    half = mybir.dt.float32r
    ALU = mybir.AluOpType
    ACT = mybir.ActivationFunctionType
    AX = mybir.AxisListType.X
    ds = bass.ds

    feat_d = nc.dram_tensor("feat_d", (N, ROW), fp32, kind="Internal").ap()
    xn_d = nc.dram_tensor("xn_d", (N, D), fp32, kind="Internal").ap()
    xT_d = nc.dram_tensor("xT_d", (NT * 128, 2 * P), fp32, kind="Internal").ap()
    base_d = nc.dram_tensor("base_d", (N, D), fp32, kind="Internal").ap()
    blk_d = nc.dram_tensor("blk_d", (1, CH * 128), i32, kind="Internal").ap()
    src2 = src.rearrange("(t e) -> t e", e=PAIR * TE)
    dst2 = dst.rearrange("(t e) -> t e", e=PAIR * TE)

    ctx, stage, raw, edge, tables, early, mixer, experts = [ExitStack() for _ in range(8)]
    with ctx:
        def sb(name, shape, dt=fp32, where=ctx):
            return where.enter_context(nc.sbuf_tensor(name, shape, dt))

        def sem(name):
            return ctx.enter_context(nc.semaphore(name))

        ident = sb("ident", [128, 128])
        ones = sb("ones", [128, 128])
        zero = sb("zero", [128, ROW])
        iota = sb("iota", [128, P])
        eps = sb("eps", [128, 1])
        r1 = sb("r1", [128, 2, RH])
        r2 = sb("r2", [128, NE])
        e3b = sb("e3b", [NE, D])
        rows = sb("rows", [128, 9, D])
        BK, BV, BO, B2, G1, E1, G2, E2, GB = range(9)
        rb2r = sb("rb2r", [128, NE])
        rb1c = sb("rb1c", [128, 1])
        eb1c = sb("eb1c", [128, NE, 2])
        eb2c = sb("eb2c", [128, NE, 2])
        xin = sb("xin", [P, 2, AU, D], fp32, stage)
        xT = sb("xT", [128, 2, AU, 2 * P], fp32, stage)
        fe = sb("fe", [P, 2, AU, ROW], fp32, stage)
        sg = sb("sg", [128, CH, PAIR * TE], i32, stage)
        dg = sb("dg", [128, CH, PAIR * TE], i32, stage)
        stage.close()
        acc = sb("acc", [P, NCB * ROW])
        x_part, xT_part, fe_part, step_part, rest_part = parts(
            2 * AU * D, 2 * AU * 2 * P, 2 * AU * ROW, 2 * CH * PAIR * TE, end=NCB * ROW)
        x1 = sb("x1", [128, NE, 2, D], fp32, raw)
        x2 = sb("x2", [128, NE, 2, D], fp32, raw)
        x3 = sb("x3", [128, NE, 2, D], fp32, raw)
        raw.close()
        hid = sb("hid", [128, 2, 2, MT * P])
        hs = sb("hs", [128, 2, 2, 2, 2, MT * P], half)
        sb("unused", [128, 3 * NE * 2 * D - (4 + 16) * MT * P])
        wext = sb("wext", [128, 2, D + 2 * H], fp32, edge)
        wkv = sb("wkv", [128, 2, 2 * D], fp32, edge)
        wq = sb("wq", [128, 2, D], fp32, edge)
        wo = sb("wo", [128, 2, D], fp32, edge)
        w1 = sb("w1", [128, 2, FF], fp32, edge)
        w2 = sb("w2", [128, 8, D], fp32, edge)
        bqc = sb("bqc", [128, 2], fp32, edge)
        b1c = sb("b1c", [128, 8], fp32, edge)
        srct = sb("srct", [128, CH * 128, PAIR], i32, edge)
        dstt = sb("dstt", [128, CH * 128, PAIR], fp32, edge)
        blk = sb("blk", [1, CH * 128 + SB], i32, edge)
        pack = sb("pack", [1, 2, NPACK], i32, edge)
        nodes = sb("nodes", [P, NCB, 2 * H], fp32, edge)
        nodep = sb("nodep", [P, 3, NCB * 2 * H], bf16, edge)
        kvbd = sb("kvbd", [128, 2, 128 + H], fp32, edge)
        first = sb("first", [1, NP], i32, tables)
        pos = sb("pos", [1, 2, NP], fp32, tables)
        step = sb("step", [128, CH], fp32, tables)
        below = sb("below", [128, HALF], fp32, tables)
        sf = sb("sf", [128, 2, PAIR * TE], fp32, tables)
        df = sb("df", [128, 2, PAIR * TE], fp32, tables)
        lr = sb("lr", [128, 2, D], fp32, tables)
        prod = sb("prod", [128, 2, D], fp32, tables)
        ntmp = sb("ntmp", [P, 2, NCB * 2 * H], fp32, tables)
        tables.close()
        G = sb("G", [128, SLOTS, ROW], fp32, edge)
        idx = sb("idx", [128, SLOTS], i32, edge)
        S = sb("S", [128, BODY, BATCH, P], fp32, edge)
        ST = sb("ST", [128, 2, BATCH * TE], bf16, edge)
        arg = sb("arg", [128, 3, BATCH, H], fp32, edge)
        xn = sb("xn", [P, 2, AU, D], fp32, early)
        stat = sb("stat", [P, AU, 6], fp32, early)
        mv = sb("mv", [P, AU, 2], fp32, early)
        rstd = sb("rstd", [P, 2, AU], fp32, early)
        count = sb("count", [128, 2, CH], fp32, early)
        tpair = sb("tpair", [128, 4, CH], fp32, early)
        tpi = sb("tpi", [128, 2, CH], i32, early)
        packf = sb("packf", [1, 2, NPACK], fp32, early)
        gmax = sb("gmax", [128, 16], fp32, early)
        early.close()
        kb = sb("kb", [P, 2, D], fp32, mixer)
        ke = sb("ke", [P, 2, D], fp32, mixer)
        vb = sb("vb", [P, 2, 2, 128 + 1], fp32, mixer)
        xm = sb("xm", [128, 2, 2 * P], fp32, mixer)
        xr = sb("xr", [P, D], fp32, mixer)
        qb = sb("qb", [128, 2, P], fp32, mixer)
        qe = sb("qe", [128, 2, P], fp32, mixer)
        at = sb("at", [P, D], fp32, mixer)
        aT = sb("aT", [128, 2, P], fp32, mixer)
        res = sb("res", [P, 2, D], fp32, mixer)
        y = sb("y", [P, 2, D], fp32, mixer)
        yT = sb("yT", [128, 2, P], fp32, mixer)
        hT = sb("hT", [128, 8, P], fp32, mixer)
        ob = sb("ob", [P, D], fp32, mixer)
        zs = sb("zs", [P, 64], fp32, mixer)
        mixer.close()
        edge.close()
        xh = [sb(f"x{n}h", [128, NE, 2, D], half, experts) for n in (1, 2, 3)]
        xl = [sb(f"x{n}l", [128, NE, 2, D], half, experts) for n in (1, 2, 3)]
        mb = sb("mb", [P, MT, D], fp32, experts)
        mx = sb("mx", [P, MT, D], fp32, experts)
        mq = sb("mq", [P, MT, D], fp32, experts)
        mf = sb("mf", [P, MT, D], fp32, experts)
        mn = sb("mn", [P, MT, D], fp32, experts)
        me = sb("me", [P, MT, D], fp32, experts)
        mfT = sb("mfT", [128, 2, MT * P], fp32, experts)
        ms = sb("ms", [128, 2, 2, MT * P], half, experts)
        mrh = sb("mrh", [128, MT * P], fp32, experts)
        mw = sb("mw", [P, MT, 16, 8], fp32, experts)
        mi = sb("mi", [P, MT, 8], u32, experts)
        wt = sb("wt", [P, MT, NE], fp32, experts)
        wtT = sb("wtT", [NE, MT, P], fp32, experts)
        experts.close()

        bank = [ctx.enter_context(nc.psum_tensor(f"bank{i}", [128, 512], fp32)) for i in range(8)]

        s_turn = sem("s_turn")
        s_const = sem("s_const")
        s_vconst = sem("s_vconst")
        s_kload = sem("s_kload")
        s_wload = sem("s_wload")
        s_gload = sem("s_gload")
        s_first = sem("s_first")
        s_tab = sem("s_tab")
        s_pos = sem("s_pos")
        s_tpe = sem("s_tpe")
        s_pack = sem("s_pack")
        s_tix = sem("s_tix")
        s_tg = [sem(f"s_tg{i}") for i in range(CH)]
        s_tf = sem("s_tf")
        s_tt = sem("s_tt")
        s_tc = sem("s_tc")
        s_blk = sem("s_blk")
        s_xin = [sem(f"s_xin{i}") for i in range(2)]
        s_mv = sem("s_mv")
        s_sd = sem("s_sd")
        s_xn = sem("s_xn")
        s_xns = [sem(f"s_xns{i}") for i in range(2)]
        s_ach = sem("s_ach")
        s_xt = [sem(f"s_xt{i}") for i in range(2)]
        s_xte = sem("s_xte")
        s_xts = [sem(f"s_xts{i}") for i in range(2)]
        s_fes = [sem(f"s_fes{i}") for i in range(2)]
        s_f = sem("s_f")
        s_fe = sem("s_fe")
        s_nch = sem("s_nch")
        s_gm = sem("s_gm")
        s_nt = sem("s_nt")
        s_idx = [sem(f"s_idx{i}") for i in range(BODY)]
        s_g = [sem(f"s_g{i}") for i in range(BODY)]
        s_S = sem("s_S")
        s_st = sem("s_st")
        s_ste = sem("s_ste")
        s_az = sem("s_az")
        s_er = sem("s_er")
        s_zch = sem("s_zch")
        s_arg = sem("s_arg")
        s_w = sem("s_w")
        s_msg = sem("s_msg")
        s_sum = sem("s_sum")
        s_acc = sem("s_acc")
        s_kx = [sem(f"s_kx{i}") for i in range(2)]
        s_kmm = [sem(f"s_kmm{i}") for i in range(2)]
        s_kb = sem("s_kb")
        s_km = sem("s_km")
        s_ke = sem("s_ke")
        s_kp = sem("s_kp")
        s_ka = [sem(f"s_ka{i}") for i in range(2)]
        s_kch = sem("s_kch")
        s_kv = sem("s_kv")
        s_kbd = sem("s_kbd")
        s_xm = sem("s_xm")
        s_xr = sem("s_xr")
        s_pq = sem("s_pq")
        s_qb = sem("s_qb")
        s_qm = sem("s_qm")
        s_qe = sem("s_qe")
        s_qp = sem("s_qp")
        s_pa = sem("s_pa")
        s_at = sem("s_at")
        s_pT = sem("s_pT")
        s_aT = sem("s_aT")
        s_po = sem("s_po")
        s_res = sem("s_res")
        s_mv1 = sem("s_mv1")
        s_y = sem("s_y")
        s_yc = sem("s_yc")
        s_fy = sem("s_fy")
        s_yT = sem("s_yT")
        s_fh = sem("s_fh")
        s_h = sem("s_h")
        s_fa = sem("s_fa")
        s_fw = sem("s_fw")
        s_r2 = sem("s_r2")
        s_mv2 = sem("s_mv2")
        s_sdm = sem("s_sdm")
        s_rs = sem("s_rs")
        s_o = sem("s_o")
        s_os = sem("s_os")
        s_lch = sem("s_lch")
        s_rch = sem("s_rch")
        s_r2ch = sem("s_r2ch")
        s_mch = sem("s_mch")
        m_xh = sem("m_xh")
        m_xl = sem("m_xl")
        m_b = sem("m_b")
        m_bs = sem("m_bs")
        m_rc = sem("m_rc")
        m_pch = sem("m_pch")
        m_em = sem("m_em")
        m_ee = sem("m_ee")
        m_x = sem("m_x")
        m_mv = sem("m_mv")
        m_sd = sem("m_sd")
        m_f = sem("m_f")
        m_fT = sem("m_fT")
        m_fe = sem("m_fe")
        m_r = sem("m_r")
        m_rr = sem("m_rr")
        m_l = sem("m_l")
        m_lm = sem("m_lm")
        m_le = sem("m_le")
        m_d = sem("m_d")
        m_de = sem("m_de")
        m_wt = sem("m_wt")
        m_wT = sem("m_wT")
        m_we = sem("m_we")
        m_bb = sem("m_bb")
        m_c = sem("m_c")
        m_cl = sem("m_cl")
        m_s = sem("m_s")
        m_h1 = sem("m_h1")
        m_h1r = sem("m_h1r")
        m_h1l = sem("m_h1l")
        m_h2 = sem("m_h2")
        m_h2r = sem("m_h2r")
        m_h2l = sem("m_h2l")
        m_o = sem("m_o")
        m_oa = sem("m_oa")
        m_st = sem("m_st")
        m_ch = sem("m_ch")

        block = ctx.enter_context(nc.Block())

        def settle(engine):
            engine.sem_inc(s_turn, 1)

        @block.sync
        def _(sp):
            with nc.allow_non_contiguous_dma("first destination of each pair, biases by partition"):
                sp.dma_start(first[:, :], dst2[:, 0:1].rearrange("t e -> e t")).then_inc(s_first, 16)
            gl = [(wext[:, :, 0:D], gW.rearrange("(c p) n -> p c n", p=128)),
                  (lr[:, 0, :], attn_l.rearrange("h d -> (h d)").partition_broadcast(128)),
                  (lr[:, 1, :], attn_r.rearrange("h d -> (h d)").partition_broadcast(128))]
            for to, of in gl:
                sp.dma_start(to, of).then_inc(s_gload, 16)

            def blocks_of(dram, r, p):
                return dram[ds(r * (AU * p), AU * p), :].rearrange("(u p) n -> p u n", p=p)

            def load_x(i, v):
                past(sp, s_xn, (i * 2 + v - 1) * AU)
                sp.dma_start(xin[:, v, :, :], blocks_of(x, i * 2 + v, P)).then_inc(s_xin[v], 16)

            load_x(0, 0)
            load_x(0, 1)

            def store_normed(i, v):
                r = i * 2 + v
                sp.wait_ge(s_xn, (r + 1) * AU)
                sp.dma_start(blocks_of(xn_d, r, P), xn[:, v, :, :]).then_inc(s_xns[v], 16)

            for i in range(TABLE_ROUNDS // 2):
                for v in range(2):
                    load_x(i + 1, v)
                    store_normed(i, v)
            sp.wait_ge(s_tix, 1)
            with nc.allow_non_contiguous_dma("steps from partitions to a row"):
                sp.dma_start(blk_d[0, :].rearrange("(c p) -> p c", p=128), tpi[:, 1, :]).then_inc(s_blk, 16)
            sp.wait_ge(s_blk, 16)
            sp.dma_start(blk[:, SB:], blk_d[:, :]).then_inc(s_blk, 16)
            with sp.Fori(TABLE_ROUNDS // 2, AR // 2 - 1) as i:
                for v in range(2):
                    load_x(i + 1, v)
                    store_normed(i, v)
            for v in range(2):
                store_normed(AR // 2 - 1, v)

            vectors = [(rows[:, n, :], v.partition_broadcast(128)) for n, v in
                       enumerate([bk, bv, bo, b2, g1, be1, g2, be2, gbias])]
            kl = [(wkv[:, :, 0:D], Wk.rearrange("(c p) n -> p c n", p=128)),
                  (wkv[:, :, D:2 * D], Wv.rearrange("(c p) n -> p c n", p=128))] + vectors[0:2]
            wl = vectors[2:]
            wl += [(wq[:, :, :], Wq.rearrange("(c p) n -> p c n", p=128)),
                   (wo[:, :, :], Wo.rearrange("(c p) n -> p c n", p=128)),
                   (r1[:, :, :], rw1.rearrange("(c p) n -> p c n", p=128)),
                   (r2[:, :], rw2), (e3b[:, :], eb3),
                   (rb2r[:, :], rb2.partition_broadcast(128))]
            for c in range(2):
                wl += [(w1[:, c, :], W1[c * 128:(c + 1) * 128, :]),
                       (w2[:, c * 4:(c + 1) * 4, :],
                        W2[c * (FF // 2):(c + 1) * (FF // 2), :].rearrange("(c p) n -> p c n", p=128))]
            for e in range(0, NE, 2):
                wl += [(to[:, e:e + 2, :, :], of[e:e + 2].rearrange("e (c p) n -> p e c n", p=128))
                       for to, of in ((x1, ew1), (x2, ew2), (x3, ew3))]
            nl = [(bqc[:, :], bq.rearrange("(c p) -> p c", p=128)),
                  (b1c[:, :], b1.rearrange("(c p) -> p c", p=128)),
                  (rb1c[:, :], rb1.rearrange("(c p) -> p c", p=128)),
                  (eb1c[:, :, :], eb1.rearrange("e (c p) -> p e c", p=128)),
                  (eb2c[:, :, :], eb2.rearrange("e (c p) -> p e c", p=128))]
            assert len(wl) + len(nl) == WLOADS and len(kl) == KLOADS
            for to, of in kl:
                sp.dma_start(to, of).then_inc(s_kload, 16)

            for v in range(2):
                sp.wait_ge(s_xts[v], 16 * (AR // 2))
                sp.wait_ge(s_xns[v], 16 * (AR // 2))
            sp.wait_ge(s_nt, 1)

            def load_kv(i):
                for u in range(2):
                    past(sp, s_kmm[u], i)
                    sp.dma_start(xm[:, u, :], xT_d[ds((i * 2 + u) * 128, 128), :]).then_inc(s_kx[u], 16)

            for i in range(WSPREAD):
                load_kv(i)
                sp.wait_ge(s_kmm[1], i + 1)
                with nc.allow_non_contiguous_dma("biases by partition"):
                    for to, of in (wl + nl)[i::WSPREAD]:
                        sp.dma_start(to, of).then_inc(s_wload, 16)
            with sp.Fori(WSPREAD, KV_ROUNDS) as i:
                load_kv(i)
            sp.wait_ge(s_kmm[0], KV_ROUNDS)

            def load_xm(m):
                past(sp, s_pq, m)
                sp.dma_start(xm[:, 0, :], xT_d[ds(m * 128, 128), :]).then_inc(s_xm, 16)

            def load_xr(m):
                past(sp, s_res, m)
                sp.dma_start(xr[:, :], xn_d[ds(m * P, P), :]).then_inc(s_xr, 16)

            def store_base(m):
                sp.wait_ge(s_o, m + 1)
                sp.dma_start(base_d[ds(m * P, P), :], ob[:, :]).then_inc(s_os, 16)

            load_xm(0)
            load_xr(0)
            load_xm(1)
            load_xm(2)
            load_xr(1)
            load_xm(3)
            load_xr(2)
            with sp.Fori(0, NT - 4) as i:
                load_xm(i + 4)
                load_xr(i + 3)
                store_base(i)
            load_xr(NT - 1)
            for m in range(NT - 4, NT):
                store_base(m)
            sp.wait_ge(s_os, 16 * NT)

            def load_base(j):
                sp.wait_ge(m_x, j)
                for to, of in ((mx, x), (mq, xn_d), (mb, base_d)):
                    sp.dma_start(to[:, :, :], of[ds(j * MT * P, MT * P), :].rearrange("(s p) n -> p s n", p=P)
                                 ).then_inc(m_b, 16)

            def store_out(j):
                sp.wait_ge(m_oa, MT * NE * (j + 1))
                rows_of_tile = acc[:, ds(j * (MT * ROW), MT * ROW)].rearrange("p (s n) -> p s n", n=ROW)
                sp.dma_start(out[ds(j * MT * P, MT * P), :].rearrange("(s p) n -> p s n", p=P),
                             rows_of_tile[:, :, 0:D]).then_inc(m_st, 16)

            sp.wait_ge(s_acc, SB * (BATCHES + 1))
            load_base(0)
            load_base(1)
            with sp.Fori(0, NJ - 2) as j:
                load_base(j + 2)
                store_out(j)
            store_out(NJ - 2)
            store_out(NJ - 1)
            sp.wait_ge(m_st, 16 * NJ)

        @block.gpsimd
        def _(pool):
            pool.memset(ident[:, :], 0.0).then_inc(s_const, 1)
            pool.wait_ge(s_const, 1)
            pool.affine_select(out=ident[:, :], in_=ident[:, :], compare_op=ALU.not_equal, fill=1.0, base=0,
                               pattern=[[-1, 128]], channel_multiplier=1).then_inc(s_const, 1)
            pool.iota(iota[:, :], [[1, P]], base=0, channel_multiplier=0,
                      allow_small_or_imprecise_dtypes=True).then_inc(s_const, 1)
            pool.iota(pos[:, 1, :], [[1, NP]], base=0, channel_multiplier=0,
                      allow_small_or_imprecise_dtypes=True).then_inc(s_const, 1)
            pool.iota(step[:, :], [[128, CH]], base=0, channel_multiplier=1,
                      allow_small_or_imprecise_dtypes=True).then_inc(s_const, 1)
            pool.memset(acc[:, rest_part], 0.0).then_inc(s_az, 1)

            def edge_rows(c):
                at_pair = bass.IndirectOffsetOnAxis(ap=tpi[:, 0, c:c + 1], axis=0)
                pool.indirect_dma_start(sg[:, c, :], None, src2, at_pair).then_inc(s_tg[c], 16)
                pool.indirect_dma_start(dg[:, c, :], None, dst2, at_pair).then_inc(s_tg[c], 16)

            pool.wait_ge(s_tix, 1)
            for c in range(CH // 2):
                edge_rows(c)
            for c in range(CH // 2, CH):
                pool.wait_ge(s_xn, (c - CH // 2 + 1) * 2 * AU)
                edge_rows(c)
            pool.wait_ge(s_xn, NT)
            pool.memset(acc[:, x_part], 0.0).then_inc(s_az, 1)
            pool.wait_ge(s_f, NT)
            for v in range(2):
                pool.wait_ge(s_xts[v], 16 * (AR // 2))
            pool.memset(acc[:, xT_part], 0.0).then_inc(s_az, 1)
            for v in range(2):
                pool.wait_ge(s_fes[v], 16 * (AR // 2))

            def gather(bt, k):
                pool.wait_ge(s_idx[bt], k + 1)
                settle(pool)
                for j in range(bt * BATCH, (bt + 1) * BATCH):
                    pool.indirect_dma_start(G[:, j, :], None, feat_d,
                                            bass.IndirectOffsetOnAxis(ap=idx[:, j:j + 1], axis=0)
                                            ).then_inc(s_g[bt], 16)

            for bt in range(BODY):
                gather(bt, 0)
            with pool.Fori(0, ROUNDS - 1) as k:
                for bt in range(BODY):
                    pool.wait_ge(s_sum, SB * (k * BODY + bt + 2))
                    gather(bt, k + 1)

            pc = Chain(pool, m_pch)

            def base_rows(j):
                pc.start(j * 8 * MT - 4 * MT)
                pool.wait_ge(m_b, (j + 1) * 48)
                settle(pool)
                for s in range(MT):
                    pc.issue(pool.tensor_tensor(mb[:, s, :], mb[:, s, :], rows[0:P, G2, :], ALU.mult))
                for s in range(MT):
                    pc.issue(pool.tensor_tensor(mx[:, s, :], mx[:, s, :], mq[:, s, :], ALU.add))
                pc.wait()
                for s in range(MT):
                    pc.issue(pool.tensor_tensor(mb[:, s, :], mb[:, s, :], rows[0:P, E2, :], ALU.add))
                pc.wait()
                for s in range(MT):
                    pc.issue(pool.tensor_tensor(mx[:, s, :], mx[:, s, :], mb[:, s, :], ALU.add))

            def graph_rows(j):
                past(pool, m_x, j)
                settle(pool)
                for s in range(MT):
                    sums = acc[:, ds((j * MT + s) * ROW, ROW)]
                    pc.issue(pool.tensor_tensor(mf[:, s, :].rearrange("p (h d) -> p h d", h=H),
                                          sums[:, 0:D].rearrange("p (h d) -> p h d", h=H),
                                          sums[:, D:ROW].unsqueeze(2).to_broadcast([P, H, HD]), ALU.mult))
                pc.wait()
                for s in range(MT):
                    pc(pool.tensor_tensor(mf[:, s, :], mf[:, s, :], rows[0:P, GB, :], ALU.add))
                for s in range(MT):
                    settle(pool)
                    pool.tensor_scalar(me[:, s, :], mf[:, s, :], 0.0, None, ALU.min).then_inc(m_em, 1)

            def rows_before_experts(j):
                settle(pool)
                for s in range(MT):
                    pc.issue(pool.tensor_scalar(mf[:, s, :], mf[:, s, :], 0.0, -1.0, ALU.max, ALU.add))
                pc.wait()
                for s in range(MT):
                    pc.issue(pool.tensor_tensor(mf[:, s, :], mf[:, s, :], mx[:, s, :], ALU.add))
                pc.wait()
                pool.wait_ge(m_ee, (j + 1) * MT)
                settle(pool)
                for s in range(MT):
                    last = pool.tensor_tensor(acc[:, ds((j * MT + s) * ROW, D)], mf[:, s, :], me[:, s, :], ALU.add)
                last.then_inc(m_x, 1)

            pool.wait_ge(m_rc, 1)
            pc.start(0)
            graph_rows(0)
            pool.wait_ge(m_bs, MT)
            rows_before_experts(0)
            with pool.Fori(1, NJ) as j:
                base_rows(j)
                graph_rows(j)
                rows_before_experts(j)

        @block.scalar
        def _(act):
            def deviations(i):
                act.wait_ge(s_mv, i + 1)
                act.activation(rstd[:, 0, :], mv[:, :, 1], ACT.Sqrt, bias=eps[0:P, :]).then_inc(s_sd, 1)

            def block_T(i, v, u):
                act.wait_ge(s_xt[v], i * AU + u + 1)
                if u == 0:
                    past(act, s_xts[v], i * 16)
                act.activation(xT[:, v, u, :], bank[4 + u % 2][:, 0:2 * P], ACT.Copy).then_inc(s_xte, 1)

            def features(i, v, u):
                t = (i * 2 + v) * AU + u
                act.wait_ge(s_f, t + 1)
                if u == 0:
                    past(act, s_fes[v], i * 16)
                act.activation(nodes[:, ds(t, 1), :].rearrange("p t h -> p (t h)"),
                               bank[6 + u % 2][0:P, D:ROW + H], ACT.Copy)
                act.activation(fe[:, v, u, :], bank[6 + u % 2][0:P, 0:ROW], ACT.Copy).then_inc(s_fe, 1)

            def first_round(i, v, last=False):
                r = i * 2 + v
                block_T(i, v, 0)
                for u in range(AU):
                    if u + 1 < AU:
                        block_T(i, v, u + 1)
                    else:
                        act.wait_ge(s_xte, (r + 1) * AU)
                        act.dma_start(xT_d[ds(r * (AU * 128), AU * 128), :].rearrange("(u p) n -> p u n", p=128),
                                      xT[:, v, :, :]).then_inc(s_xts[v], 16)
                    if u == AU // 2 and not last:
                        deviations(r + 1)
                    features(i, v, u)
                act.wait_ge(s_fe, (r + 1) * AU)
                act.dma_start(feat_d[ds(r * (AU * P), AU * P), :].rearrange("(u p) n -> p u n", p=P),
                              fe[:, v, :, :]).then_inc(s_fes[v], 16)

            act.wait_ge(s_vconst, 1)
            deviations(0)
            with act.Fori(0, AR // 2 - 1) as i:
                for v in range(2):
                    first_round(i, v)
            first_round(AR // 2 - 1, 0)
            first_round(AR // 2 - 1, 1, last=True)

            def indices(bt, k):
                act.activation(idx[:, bt * BATCH:(bt + 1) * BATCH],
                               srct[:, ds(k * (SLOTS // PAIR) + bt * SB, SB), :].rearrange("p s u -> p (s u)"),
                               ACT.Copy).then_inc(s_idx[bt], 1)

            def transposes_out(n, par):
                act.wait_ge(s_st, n + 1)
                act.activation(ST[0:P, par, :], bank[0][0:P, :], ACT.Copy).then_inc(s_ste, 1)

            def zero_sums(part):
                n = part.stop - part.start
                act.activation(acc[:, part], zero[0:P, 0:1].to_broadcast([P, n]), ACT.Copy).then_inc(s_az, 1)

            def edge_weights(n, bt):
                act.wait_ge(s_arg, n + 1)
                act.activation(G[:, bt * BATCH:(bt + 1) * BATCH, D:ROW], arg[:, 2, :, :], ACT.Exp
                               ).then_inc(s_w, 1)

            act.wait_ge(s_tf, CH)
            zero_sums(step_part)
            act.wait_ge(s_tc, CH)
            for bt in range(BODY):
                indices(bt, 0)
            for v in range(2):
                act.wait_ge(s_fes[v], 16 * (AR // 2))
            zero_sums(fe_part)
            transposes_out(0, 0)
            transposes_out(1, 1)
            edge_weights(0, 0)
            indices(0, 1)

            def edges(k, bt, last=False):
                n = k * BODY + bt
                if not last or bt + 2 < BODY:
                    act.wait_ge(s_er, n + 1)
                    transposes_out(n + 2, bt % 2)
                if not last or bt + 1 < BODY:
                    edge_weights(n + 1, (bt + 1) % BODY)
                if not last:
                    indices((bt + 1) % BODY, k + 1 + (bt + 1) // BODY)

            def keys(i, u):
                act.wait_ge(s_km, i * 2 + u + 1)
                act.activation(ke[:, u, :], ke[:, u, :], ACT.Exp).then_inc(s_ke, 1)

            with act.Fori(0, KV_ROUNDS) as i:
                edges(i, 0)
                keys(i, 0)
                edges(i, 1)
                edges(i, 2)
                keys(i, 1)
                edges(i, 3)

            act.wait_ge(s_wload, 16 * WLOADS)
            act.wait_ge(s_rs, 1)

            def queries_in(m):
                act.wait_ge(s_pq, m + 1)
                past(act, s_pa, m)
                for c in range(2):
                    last = act.activation(qb[:, c, :], bank[7][:, c * P:(c + 1) * P], ACT.Identity,
                                          bias=bqc[:, c:c + 1])
                last.then_inc(s_qb, 1)

            def queries_exp(m):
                act.wait_ge(s_qm, m + 1)
                act.activation(qe[:, :, :], qe[:, :, :], ACT.Exp).then_inc(s_qe, 1)

            def attention_T(m):
                act.wait_ge(s_pT, m + 1)
                past(act, s_po, m)
                act.activation(aT[:, :, :].rearrange("p c n -> p (c n)"), bank[4][:, 0:2 * P], ACT.Copy
                               ).then_inc(s_aT, 1)

            def deviation(i, blocks):
                if 1 in blocks:
                    act.wait_ge(s_mv1, i)
                if 3 in blocks:
                    act.wait_ge(s_mv2, i - 2)
                act.activation(zs[:, 20:22], zs[:, 17:20:2], ACT.Sqrt, bias=eps[0:P, :]).then_inc(s_sdm, 1)

            def norm_T(m):
                act.wait_ge(s_fy, m + 1)
                past(act, s_fh, m * 2)
                act.activation(yT[:, :, :].rearrange("p c n -> p (c n)"), bank[4][:, 0:2 * P], ACT.Copy
                               ).then_inc(s_yT, 1)

            def keep_norm(m):
                act.wait_ge(s_y, m + 1)
                past(act, s_r2, m)
                act.activation(y[:, 1, :], y[:, 0, :], ACT.Copy).then_inc(s_yc, 1)

            def hidden(m, half):
                act.wait_ge(s_fh, m * 2 + half + 1)
                past(act, s_fw if half else s_fa, m)
                for c in range(4):
                    ch = half * 4 + c
                    last = act.activation(hT[:, ch, :], bank[6 + half][:, c * P:(c + 1) * P], ACT.Relu,
                                          bias=b1c[:, ch:ch + 1])
                last.then_inc(s_h, 1)

            def two_passes(triple):
                for half in range(2):
                    i = triple * 2 + half
                    blocks = active(i)
                    edges(*mixer_batch(triple, half, 0))
                    if 0 in blocks:
                        queries_in(i)
                    if 1 in blocks:
                        attention_T(i - 1)
                    edges(*mixer_batch(triple, half, 1))
                    if 0 in blocks:
                        queries_exp(i)
                    if 2 in blocks:
                        keep_norm(i - 2)
                    edges(*mixer_batch(triple, half, 2))
                    if 2 in blocks:
                        hidden(i - 2, 0)
                    if 1 in blocks or 3 in blocks:
                        deviation(i, blocks)
                    edges(*mixer_batch(triple, half, 3))
                    if 2 in blocks:
                        hidden(i - 2, 1)
                    edges(*mixer_batch(triple, half, 4))
                    if 1 in blocks:
                        norm_T(i - 1)
                    edges(*mixer_batch(triple, half, 5))

            for triple in range(2):
                two_passes(triple)
            with act.Fori(2, NT // 2) as triple:
                two_passes(triple)
            for triple in range(NT // 2, TRIPLES):
                two_passes(triple)
            for bt in range(BODY):
                edges(ROUNDS - 1, bt, last=True)

            def elu_exp(j, s):
                act.wait_ge(m_em, j * MT + s + 1)
                act.activation(me[:, s, :], me[:, s, :], ACT.Exp).then_inc(m_ee, 1)

            def row_deviations(j):
                act.wait_ge(m_mv, j + 1)
                act.activation(mw[:, :, 1, 0:1], mw[:, :, 0, 1:2], ACT.Sqrt, bias=eps[0:P, :]).then_inc(m_sd, 1)

            def rows_T(j):
                act.wait_ge(m_fT, j + 1)
                past(act, m_cl, j)
                act.activation(mfT[:, :, :].rearrange("p c n -> p (c n)"), bank[0][:, 0:2 * MT * P],
                               ACT.Copy).then_inc(m_fe, 1)

            def router_hidden(j):
                act.wait_ge(m_r, j + 1)
                act.activation(mrh[:, :], bank[1][:, 0:MT * P], ACT.Relu, bias=rb1c[:, :]).then_inc(m_rr, 1)

            def router_exps(j):
                act.wait_ge(m_lm, j + 1)
                act.activation(mw[:, :, 3, 0:NE], mw[:, :, 2, 0:NE], ACT.Exp).then_inc(m_le, 1)

            def top_exps(j):
                act.wait_ge(m_d, j + 1)
                act.activation(mw[:, :, 8, 0:1], mw[:, :, 7, 0:1], ACT.Exp).then_inc(m_de, 1)

            def weights_T(j):
                act.wait_ge(m_wT, j + 1)
                past(act, m_bb, j)
                act.activation(wtT[:, :, :], bank[2][0:NE, 128:128 + MT * P].rearrange("p (s n) -> p s n", s=MT),
                               ACT.Copy).then_inc(m_we, 1)

            def place(j):
                act.wait_ge(m_fe, j + 1)
                past(act, m_h1, j * NE)
                act.activation(ms[:, 0, :, :], mfT[:, :, :], ACT.Copy).then_inc(m_c, 1)

            def relus(j, e, layer):
                done, at_bank, bias, done_r, done_l = (
                    (m_h1, 3, eb1c, m_h1r, m_h1l), (m_h2, 4, eb2c, m_h2r, m_h2l))[layer]
                act.wait_ge(done, j * NE + e + 1)
                past(act, done_l, j * NE + e)
                for to in (hid[:, layer, :, :], hs[:, layer, e % 2, 0, :, :]):
                    for c in range(2):
                        last = act.activation(to[:, c, :], bank[at_bank][:, c * MT * P:(c + 1) * MT * P],
                                              ACT.Relu, bias=bias[:, e, c:c + 1])
                last.then_inc(done_r, 1)

            def tile_of_experts(j, ahead):
                for e in range(NE):
                    if e + 1 < NE:
                        relus(j, e + 1, 0)
                    elif ahead:
                        relus(j + 1, 0, 0)
                    if ahead:
                        if e == 3:
                            rows_T(j + 1)
                        if e == 4:
                            place(j + 1)
                    if e == 1:
                        top_exps(j)
                    relus(j, e, 1)
                    if e == 0 and ahead:
                        for s in range(MT):
                            elu_exp(j + 1, s)
                    if e == 2:
                        if ahead:
                            row_deviations(j + 1)
                        weights_T(j)
                    if ahead:
                        if e == 3:
                            router_hidden(j + 1)
                        if e == 5:
                            router_exps(j + 1)

            def weights_high(e):
                for layer, w in enumerate((x1, x2, x3)):
                    act.activation(xh[layer][:, e, :, :], w[:, e, :, :], ACT.Copy).then_inc(m_xh, 1)

            act.wait_ge(s_acc, SB * (BATCHES + 1))
            for e in range(4):
                weights_high(e)
            for s in range(MT):
                elu_exp(0, s)
            for e in range(4, NE):
                weights_high(e)
            row_deviations(0)
            rows_T(0)
            place(0)
            router_hidden(0)
            router_exps(0)
            relus(0, 0, 0)
            tile_of_experts(0, True)
            with act.Fori(1, NJ - 1) as j:
                tile_of_experts(j, True)
            tile_of_experts(NJ - 1, False)

        @block.vector
        def _(dve):
            dve.memset(ones[:, :], 1.0)
            dve.memset(zero[:, :], 0.0)
            dve.memset(eps[:, :], EPS)
            dve.memset(nodes[:, :, :], 0.0)
            dve.memset(blk[:, 0:SB], 0)
            dve.memset(kvbd[:, :, :], 0.0).then_inc(s_vconst, 1)

            tab = Chain(dve, s_tab)
            dve.wait_ge(s_gload, 48)
            for c in range(2):
                for a in range(2):
                    tab(dve.tensor_tensor(prod[:, a, :], wext[:, c, 0:D], lr[:, a, :], ALU.mult))
                    tab(dve.tensor_reduce(wext[:, c, D + a * H:D + (a + 1) * H],
                                          prod[:, a, :].rearrange("p (h d) -> p h d", h=H), AX, ALU.add))
            assert tab.n == WEXT_LINKS

            def pair_positions():
                dve.wait_ge(s_first, 16)
                tab(dve.tensor_copy(pos[:, 0, :], first[:, :]))
                tab(dve.tensor_scalar(pos[:, 0, :], pos[:, 0, :], 0.5, 1.0 / P, ALU.add, ALU.mult))
                tab(dve.tensor_scalar(first[:, :], pos[:, 0, :], -0.5, None, ALU.add))
                dve.wait_ge(s_const, 5)
                dve.tensor_tensor(pos[:, 0, :], first[:, :], pos[:, 1, :], ALU.add).then_inc(s_pos, 1)

            def count_pairs(c):
                dve.wait_ge(s_tpe, 1)
                for b in range(2):
                    tab(dve.tensor_scalar(below[:, :], bank[b][:, 0:HALF], step[:, c:c + 1], 0.0,
                                          ALU.is_le, ALU.add, accum_out=count[:, b, c:c + 1]))

            def steps():
                tab(dve.scalar_tensor_tensor(out=tpair[:, 0, :], in0=count[:, 0, :], scalar=-1.0, in1=count[:, 1, :],
                                             op0=ALU.add, op1=ALU.add))
                tab(dve.tensor_scalar(tpair[:, 0, :], tpair[:, 0, :], 0.0, None, ALU.max))
                tab(dve.tensor_tensor(tpair[:, 1, :], step[:, :], tpair[:, 0, :], ALU.subtract))
                tab(dve.tensor_scalar(tpair[:, 1, :], tpair[:, 1, :], float(NT), None, ALU.min))
                tab(dve.tensor_scalar(tpair[:, 2, :], tpair[:, 1, :], float(P), None, ALU.mult))
                tab(dve.tensor_copy(tpi[:, 0, :], tpair[:, 0, :]))
                dve.tensor_copy(tpi[:, 1, :], tpair[:, 1, :]).then_inc(s_tix, 1)

            ch = Chain(dve, s_ach)

            def first_round(i, v):
                r = i * 2 + v
                ch.start(r * (AU + 1))
                dve.wait_ge(s_xin[v], (i + 1) * 16)
                for u in range(AU):
                    ch.issue(dve.bn_stats(stat[:, u, :], xin[:, v, u, :]))
                ch.wait()
                settle(dve)
                for u in range(AU):
                    last = dve.bn_aggr(mv[:, u, :], stat[:, u, :])
                last.then_inc(s_mv, 1)
                dve.wait_ge(s_sd, r + 1)
                ch(dve.reciprocal(rstd[:, 1, :], rstd[:, 0, :]))
                dve.wait_ge(s_xns[v], i * 16)
                dve.wait_ge(s_xt[v], i * AU)
                for u in range(AU):
                    dve.tensor_scalar(xn[:, v, u, :], xin[:, v, u, :], mv[:, u, 0:1], rstd[:, 1, u:u + 1],
                                      ALU.subtract, ALU.mult).then_inc(s_xn, 1)

            def edges_as_floats(c):
                dve.wait_ge(s_tg[c], 32)
                if c >= 2:
                    dve.wait_ge(s_tt, c - 1)
                dve.tensor_copy(sf[:, c % 2, :], sg[:, c, :])
                dve.tensor_scalar(df[:, c % 2, :], dg[:, c, :], tpair[:, 2, c:c + 1], None, ALU.subtract
                                  ).then_inc(s_tf, 1)

            def edge_columns(c):
                dve.wait_ge(s_tt, c + 1)
                dve.tensor_copy(srct[:, c * 128:(c + 1) * 128, :].rearrange("p s u -> p u s"),
                                bank[2 + c % 2][:, 0:PAIR * 128].rearrange("p (u s) -> p u s", u=PAIR))
                dve.tensor_copy(dstt[:, c * 128:(c + 1) * 128, :].rearrange("p s u -> p u s"),
                                bank[2 + c % 2][:, PAIR * 128:2 * PAIR * 128].rearrange("p (u s) -> p u s", u=PAIR)
                                ).then_inc(s_tc, 1)

            first_round(0, 0)
            pair_positions()
            for r in range(1, TABLE_ROUNDS):
                first_round(r // 2, r % 2)
                for c in range(CH)[r - 1::TABLE_ROUNDS - 1]:
                    count_pairs(c)
            steps()
            with dve.Fori(TABLE_ROUNDS // 2, (AR - CHUNK_ROUNDS) // 2) as i:
                for v in range(2):
                    first_round(i, v)
            pch = Chain(dve, s_pack)
            dve.wait_ge(s_blk, 32)
            digits = [blk[:, first_step:first_step + 4 * NPACK].rearrange("p (n q) -> p n q", q=4)
                      for first_step in (0, SB)]
            for digit in (2, 1, 0):
                for which in range(2):
                    more = digits[which][:, :, 3] if digit == 2 else packf[:, which, :]
                    pch(dve.scalar_tensor_tensor(out=packf[:, which, :], in0=more, scalar=float(PACK),
                                                 in1=digits[which][:, :, digit], op0=ALU.mult, op1=ALU.add))
            pch(dve.tensor_copy(pack[:, :, :], packf[:, :, :]))
            for c in range(CHUNK_ROUNDS):
                r = AR - CHUNK_ROUNDS + c
                first_round(r // 2, r % 2)
                if c:
                    edge_columns(c - 1)
                edges_as_floats(c)
            for c in range(CHUNK_ROUNDS, CH):
                edges_as_floats(c)
                edge_columns(c - 1)
            edge_columns(CH - 1)

            nch = Chain(dve, s_nch)
            dve.wait_ge(s_fe, NT)
            nch(dve.tensor_reduce(gmax[0:P, 0:H], nodes[:, 0:NT, 0:H].rearrange("p t h -> p h t"), AX, ALU.max))
            dve.memset(gmax[0:P, 4:5], 0.0).then_inc(s_gm, 1)
            dve.wait_ge(s_gm, 2)
            nch(dve.tensor_reduce(gmax[0:H, 5:6], bank[2][0:H, 0:P], AX, ALU.max))
            dve.tensor_scalar(gmax[0:H, 8:8 + H], ident[0:H, 0:H], gmax[0:H, 5:6], None, ALU.mult).then_inc(s_gm, 1)
            dve.wait_ge(s_gm, 4)
            nch(dve.tensor_copy(gmax[0:P, 12:16], bank[2][0:P, 256:256 + H]))
            one = ntmp[:, 0, :].rearrange("p (t h) -> p t h", h=2 * H)
            two = ntmp[:, 1, :].rearrange("p (t h) -> p t h", h=2 * H)
            nch(dve.tensor_tensor(one[:, :, 0:H], nodes[:, :, H:2 * H],
                                  gmax[0:P, 12:16].unsqueeze(1).to_broadcast([P, NCB, H]), ALU.add))
            nch(dve.tensor_copy(nodes[:, :, 0:H], nodes[:, :, H:2 * H]))
            nch(dve.scalar_tensor_tensor(out=nodes[:, :, H:2 * H], in0=one[:, :, 0:H], scalar=0.2,
                                         in1=one[:, :, 0:H], op0=ALU.mult, op1=ALU.max))
            flat = nodes[:, :, :].rearrange("p t h -> p (t h)")
            nch(dve.tensor_copy(nodep[:, 0, :], flat))
            nch(dve.tensor_tensor(ntmp[:, 0, :], flat, nodep[:, 0, :], ALU.subtract))
            nch(dve.tensor_copy(nodep[:, 1, :], ntmp[:, 0, :]))
            nch(dve.tensor_tensor(ntmp[:, 1, :], ntmp[:, 0, :], nodep[:, 1, :], ALU.subtract))
            dve.tensor_copy(nodep[:, 2, :], ntmp[:, 1, :]).then_inc(s_nt, 1)
            dve.wait_ge(s_nt, 1)

            def one_hots(n, ring):
                columns = dstt[:, ds(n * SB, SB), :].rearrange("p s u -> p (s u)")
                dve.tensor_tensor(S[:, ring, :, :], iota[:, :].unsqueeze(1).to_broadcast([128, BATCH, P]),
                                  columns.unsqueeze(2).to_broadcast([128, BATCH, P]), ALU.is_equal
                                  ).then_inc(s_S, 1)

            def packed(pair):
                return dve.value_load(pack[0:1, 0, ds(pair, 1)], min_val=0, max_val=PACK ** 4 - 1)

            def add_sum(n, q, at_sum):
                if q == 0:
                    dve.wait_ge(s_sum, n * SB + SB)
                if not isinstance(n, int) or n * SB + q > 0:
                    dve.wait_ge(s_acc, n * SB + q)
                dve.tensor_tensor(acc[:, ds(at_sum, ROW)], bank[2 + q][0:P, 0:ROW],
                                  acc[:, ds(at_sum, ROW)], ALU.add).then_inc(s_acc, 1)

            zch = Chain(dve, s_zch)

            def exponents(n, bt, rounds, sums=((), ())):
                for q_b in sums[0]:
                    add_sum(*q_b)
                slots = G[:, bt * BATCH:(bt + 1) * BATCH, :]
                dve.wait_ge(s_g[bt], rounds * (16 * BATCH))
                dve.wait_ge(s_er, n + 1)
                er = bank[1][:, 0:BATCH * 2 * H].rearrange("p (j h) -> p j h", j=BATCH)
                zch.start(n * 2)
                zch.issue(dve.tensor_tensor(arg[:, 0, :, :], slots[:, :, D:ROW], er[:, :, 0:H], ALU.add))
                for q_b in sums[1]:
                    add_sum(*q_b)
                zch.wait()
                zch(dve.scalar_tensor_tensor(out=arg[:, 1, :, :], in0=arg[:, 0, :, :], scalar=0.2,
                                             in1=arg[:, 0, :, :], op0=ALU.mult, op1=ALU.max))
                dve.tensor_tensor(arg[:, 2, :, :], arg[:, 1, :, :], er[:, :, H:2 * H], ALU.subtract
                                  ).then_inc(s_arg, 1)

            def messages(n, bt):
                slots = G[:, bt * BATCH:(bt + 1) * BATCH, :]
                dve.wait_ge(s_w, n + 1)
                features = slots[:, :, 0:D].rearrange("p j (h d) -> p j h d", h=H)
                dve.tensor_tensor(features, features,
                                  slots[:, :, D:ROW].unsqueeze(3).to_broadcast([128, BATCH, H, HD]), ALU.mult
                                  ).then_inc(s_msg, 1)

            ahead = {}

            def edges(k, bt, last=False, ends=False):
                n = k * BODY + bt
                if bt % 2 == 0 and not ahead:
                    ahead[0] = packed(k * 2 + bt // 2)
                blocks = ahead[0] if bt % 2 == 0 else ahead.pop(0)
                sums = [(n, q, dve.snap(unpack(blocks, bt % 2 * SB + q) * ROW)) for q in range(SB)]
                more = not last or bt + 1 < BODY
                if more:
                    exponents(n + 1, (bt + 1) % BODY, k + 1 + (bt + 1) // BODY, (sums[:1], sums[1:]))
                else:
                    for q_b in sums:
                        add_sum(*q_b)
                if not last or bt + 3 < BODY:
                    one_hots(n + 3, (bt + 3) % BODY)
                if bt % 2 == 1 and not ends:
                    ahead[0] = packed(k * 2 + bt // 2 + 1)
                if more:
                    messages(n + 1, (bt + 1) % BODY)

            dve.wait_ge(s_blk, 32)
            dve.wait_ge(s_tc, CH)
            for n in range(BODY - 1):
                one_hots(n, n)
            for v in range(2):
                dve.wait_ge(s_xns[v], 16 * (AR // 2))
            dve.memset(vb[:, :, :, 128:129], 1.0)
            exponents(0, 0, 1)
            messages(0, 0)
            dve.wait_ge(s_az, 5)

            kch = Chain(dve, s_kch)
            dve.wait_ge(s_kload, 16 * KLOADS)

            def keys_in(i, u):
                m = i * 2 + u
                dve.wait_ge(s_kmm[u], i + 1)
                dve.wait_ge(s_ka[u], i)
                kch.start(m)
                dve.tensor_tensor(vb[:, u, :, 0:128], bank[4][0:P, D:2 * D].rearrange("p (c n) -> p c n", c=2),
                                  rows[0:P, BV, :].rearrange("p (c n) -> p c n", c=2), ALU.add)
                kch(dve.tensor_tensor(kb[:, u, :], bank[4][0:P, 0:D], rows[0:P, BK, :], ALU.add))
                dve.tensor_scalar(ke[:, u, :], kb[:, u, :], 0.0, None, ALU.min).then_inc(s_km, 1)

            def keys_phi(i, u):
                dve.wait_ge(s_ke, i * 2 + u + 1)
                dve.scalar_tensor_tensor(out=kb[:, u, :], in0=kb[:, u, :], scalar=0.0, in1=ke[:, u, :],
                                         op0=ALU.max, op1=ALU.add).then_inc(s_kp, 1)

            with dve.Fori(0, KV_ROUNDS) as i:
                edges(i, 0)
                keys_in(i, 0)
                keys_phi(i, 0)
                edges(i, 1)
                edges(i, 2)
                keys_in(i, 1)
                keys_phi(i, 1)
                edges(i, 3, ends=True)
            dve.wait_ge(s_kv, 1)
            for c in range(2):
                for h in range(4):
                    hp = slice(32 * h, 32 * h + 32)
                    dve.tensor_copy(kvbd[hp, c, 32 * h:32 * h + 32], bank[5 + c][hp, 32 * h:32 * h + 32])
                    last = dve.tensor_copy(kvbd[hp, c, 128 + h:129 + h], bank[5 + c][hp, 128:129])
            last.then_inc(s_kbd, 1)

            dve.wait_ge(s_wload, 16 * WLOADS)
            dve.memset(zs[:, :], 1.0).then_inc(s_rs, 1)
            mch = Chain(dve, s_mch)

            def queries_low(m):
                dve.wait_ge(s_qb, m + 1)
                dve.tensor_scalar(qe[:, :, :], qb[:, :, :], 0.0, None, ALU.min).then_inc(s_qm, 1)

            def queries_phi(m):
                dve.wait_ge(s_qe, m + 1)
                dve.scalar_tensor_tensor(out=qb[:, :, :], in0=qb[:, :, :], scalar=0.0, in1=qe[:, :, :],
                                         op0=ALU.max, op1=ALU.add).then_inc(s_qp, 1)

            def attention(m):
                dve.wait_ge(s_pa, m + 1)
                past(dve, s_pT, m)
                both = bank[5][0:P, 0:2 * (128 + H)].rearrange("p (c n) -> p c n", c=2)
                z = zs[:, 0:2 * H]
                mch.start(m * 2)
                mch(dve.tensor_scalar(z.rearrange("p (c h) -> p c h", c=2), both[:, :, 128:128 + H], 1e-6, None,
                                      ALU.add))
                mch(dve.reciprocal(z, z))
                dve.tensor_tensor(at[:, :].rearrange("p (c h d) -> p c h d", c=2, h=H),
                                  both[:, :, 0:128].rearrange("p c (h d) -> p c h d", h=H),
                                  z.rearrange("p (c h) -> p c h", c=2).unsqueeze(3).to_broadcast([P, 2, H, MD]),
                                  ALU.mult).then_inc(s_at, 1)

            rch = [Chain(dve, s_rch), Chain(dve, s_r2ch)]

            def moments(k, m, column, mean_var):
                dve.wait_ge((s_res, s_r2)[k], m + 1)
                rch[k].start(m)
                rch[k](dve.bn_stats(zs[:, 32 + 8 * k:38 + 8 * k], res[:, k, :]))
                settle(dve)
                dve.bn_aggr(zs[:, column:column + 2], zs[:, 32 + 8 * k:38 + 8 * k]).then_inc(mean_var, 1)

            nln = Chain(dve, s_lch)

            def reciprocals(i):
                dve.wait_ge(s_sdm, i)
                dve.reciprocal(zs[:, 22:24], zs[:, 20:22]).then_inc(s_rs, 1)
                dve.wait_ge(s_rs, i + 1)

            def first_residual(m):
                dve.wait_ge(s_po, m + 1)
                dve.wait_ge(s_xr, (m + 1) * 16)
                dve.tensor_tensor(res[:, 0, :], bank[5][0:P, 0:D], xr[:, :], ALU.add).then_inc(s_res, 1)
                moments(0, m, 16, s_mv1)

            def first_norm(m):
                past(dve, s_fy, m)
                past(dve, s_yc, m)
                nln.start(m)
                nln(dve.scalar_tensor_tensor(out=res[:, 0, :], in0=res[:, 0, :], scalar=zs[:, 16:17],
                                             in1=rows[0:P, G1, :], op0=ALU.subtract, op1=ALU.mult))
                dve.scalar_tensor_tensor(out=y[:, 0, :], in0=res[:, 0, :], scalar=zs[:, 22:23],
                                         in1=rows[0:P, E1, :], op0=ALU.mult, op1=ALU.add).then_inc(s_y, 1)

            def result(m):
                past(dve, s_os, m * 16)
                dve.tensor_scalar(ob[:, :], res[:, 1, :], zs[:, 18:19], zs[:, 23:24],
                                  ALU.subtract, ALU.mult).then_inc(s_o, 1)

            def second_residual(m):
                dve.wait_ge(s_fw, m + 1)
                dve.wait_ge(s_yc, m + 1)
                past(dve, s_o, m)
                dve.tensor_tensor(res[:, 1, :], bank[6][0:P, 0:D], y[:, 1, :], ALU.add).then_inc(s_r2, 1)

            def two_passes(triple):
                for half in range(2):
                    i = triple * 2 + half
                    blocks = active(i)
                    edges(*mixer_batch(triple, half, 0))
                    if 0 in blocks:
                        queries_low(i)
                    if 3 in blocks:
                        moments(1, i - 3, 18, s_mv2)
                    edges(*mixer_batch(triple, half, 1))
                    if 1 in blocks:
                        first_residual(i - 1)
                    edges(*mixer_batch(triple, half, 2))
                    if 0 in blocks:
                        queries_phi(i)
                    edges(*mixer_batch(triple, half, 3))
                    if 1 in blocks or 3 in blocks:
                        reciprocals(i)
                    if 1 in blocks:
                        first_norm(i - 1)
                    edges(*mixer_batch(triple, half, 4))
                    if 0 in blocks:
                        attention(i)
                    if 3 in blocks:
                        result(i - 3)
                    edges(*mixer_batch(triple, half, 5), ends=half == 1)
                    if 2 in blocks:
                        second_residual(i - 2)

            for triple in range(2):
                two_passes(triple)
            with dve.Fori(2, NT // 2) as triple:
                two_passes(triple)
            for triple in range(NT // 2, TRIPLES):
                two_passes(triple)
            for bt in range(BODY):
                edges(ROUNDS - 1, bt, last=True, ends=bt == BODY - 1)
            rest = packed(BATCHES // 2)
            for q in range(SB):
                add_sum(BATCHES, q, unpack(rest, q) * ROW)

            mc = Chain(dve, m_ch)

            def at_rows(j, s):
                return (j * MT + s) * ROW

            def row_moments(j):
                dve.wait_ge(m_x, j + 1)
                settle(dve)
                for s in range(MT):
                    mc.issue(dve.bn_stats(mw[:, s, 10, 0:6], acc[:, ds(at_rows(j, s), D)]))
                mc.wait()
                settle(dve)
                for s in range(MT):
                    last = dve.bn_aggr(mw[:, s, 0, 0:2], mw[:, s, 10, 0:6])
                last.then_inc(m_mv, 1)

            def norm_rows(j):
                dve.wait_ge(m_sd, j + 1)
                mc(dve.reciprocal(mw[:, :, 1, 1:2], mw[:, :, 1, 0:1]))
                past(dve, m_fT, j)
                for s in range(MT):
                    last = dve.tensor_scalar(mn[:, s, :], acc[:, ds(at_rows(j, s), D)], mw[:, s, 0, 0:1],
                                             mw[:, s, 1, 1:2],
                                             ALU.subtract, ALU.mult)
                last.then_inc(m_f, 1)

            def logits_low(j):
                dve.wait_ge(m_l, j + 1)
                logits = bank[2][0:P, 0:MT * 8].rearrange("p (s n) -> p s n", s=MT)[:, :, 0:NE]
                mc(dve.tensor_tensor(mw[:, :, 2, 0:NE], logits,
                                     rb2r[0:P, :].unsqueeze(1).to_broadcast([P, MT, NE]), ALU.add))
                mc(dve.tensor_reduce(mw[:, :, 1, 2:3].rearrange("p s n -> p (s n)"), mw[:, :, 2, 0:NE], AX, ALU.max))
                dve.tensor_tensor(mw[:, :, 2, 0:NE], mw[:, :, 2, 0:NE],
                                  mw[:, :, 1, 2:3].to_broadcast([P, MT, NE]), ALU.subtract).then_inc(m_lm, 1)

            def probabilities(j):
                dve.wait_ge(m_le, j + 1)
                mc(dve.tensor_reduce(mw[:, :, 1, 3:4].rearrange("p s n -> p (s n)"), mw[:, :, 3, 0:NE], AX, ALU.add))
                mc(dve.reciprocal(mw[:, :, 1, 4:5], mw[:, :, 1, 3:4]))
                mc(dve.tensor_tensor(mw[:, :, 3, 0:NE], mw[:, :, 3, 0:NE],
                                     mw[:, :, 1, 4:5].to_broadcast([P, MT, NE]), ALU.mult))

            def top_two(j):
                settle(dve)
                for s in range(MT):
                    mc.issue(dve.max(mw[:, s, 4, :], mw[:, s, 3, :]))
                mc.wait()
                settle(dve)
                for s in range(MT):
                    mc.issue(dve.max_index(mi[:, s, :], mw[:, s, 4, :], mw[:, s, 3, :]))
                dve.tensor_tensor(mw[:, :, 7, 0:1], mw[:, :, 4, 1:2], mw[:, :, 4, 0:1], ALU.subtract
                                  ).then_inc(m_d, 1)
                mc.wait()
                mc(dve.tensor_copy(mw[:, :, 5, :], mi[:, :, :]))

            def routing_weights(j):
                dve.wait_ge(m_de, j + 1)
                mc.issue(dve.tensor_scalar(mw[:, :, 8, 1:2], mw[:, :, 8, 0:1], 1.0, None, ALU.add))
                for r in range(2):
                    is_it = dve.tensor_tensor(mw[:, :, 11 + r, 0:NE],
                                              iota[0:P, 0:NE].unsqueeze(1).to_broadcast([P, MT, NE]),
                                              mw[:, :, 5, r:r + 1].to_broadcast([P, MT, NE]), ALU.is_equal)
                    mc.issue(is_it)
                mc.wait()
                mc(dve.reciprocal(mw[:, :, 8, 2:3], mw[:, :, 8, 1:2]))
                mc(dve.tensor_tensor(mw[:, :, 8, 3:4], mw[:, :, 8, 0:1], mw[:, :, 8, 2:3], ALU.mult))
                for r in range(2):
                    mc.issue(dve.tensor_tensor(mw[:, :, 11 + r, 0:NE], mw[:, :, 11 + r, 0:NE],
                                               mw[:, :, 8, 2 + r:3 + r].to_broadcast([P, MT, NE]), ALU.mult))
                mc.wait()
                past(dve, m_wT, j)
                dve.tensor_tensor(wt[:, :, :], mw[:, :, 11, 0:NE], mw[:, :, 12, 0:NE], ALU.add).then_inc(m_wt, 1)
                dve.wait_ge(m_wt, j + 1)

            def add_biases(j):
                dve.wait_ge(m_bb, j + 1)
                dve.wait_ge(m_oa, (j * NE + 3) * MT)
                tile = acc[:, ds(at_rows(j, 0), MT * ROW)].rearrange("p (s n) -> p s n", n=ROW)[:, :, 0:D]
                dve.tensor_tensor(tile, tile, bank[7][0:P, 0:MT * D].rearrange("p (s n) -> p s n", n=D), ALU.add
                                  ).then_inc(m_s, 1)
                dve.wait_ge(m_s, j + 1)

            def add_expert(j, e):
                dve.wait_ge(m_o, j * NE + e + 1)
                for s in range(MT):
                    if e >= 1:
                        dve.wait_ge(m_oa, (j * NE + e - 1) * MT + s + 1)
                    rows_so_far = acc[:, ds(at_rows(j, s), D)]
                    dve.scalar_tensor_tensor(out=rows_so_far, in0=bank[5 + e % 2][0:P, s * D:(s + 1) * D],
                                             scalar=wt[:, s, e:e + 1], in1=rows_so_far,
                                             op0=ALU.mult, op1=ALU.add).then_inc(m_oa, 1)

            def rows_low(j):
                dve.wait_ge(m_c, j + 1)
                dve.tensor_tensor(ms[:, 1, :, :], mfT[:, :, :], ms[:, 0, :, :], ALU.subtract).then_inc(m_cl, 1)

            def hidden_low(j, e, layer):
                dve.wait_ge((m_h1r, m_h2r)[layer], j * NE + e + 1)
                dve.tensor_tensor(hs[:, layer, e % 2, 1, :, :], hid[:, layer, :, :], hs[:, layer, e % 2, 0, :, :],
                                  ALU.subtract).then_inc((m_h1l, m_h2l)[layer], 1)

            def weights_low(e):
                for layer, w in enumerate((x1, x2, x3)):
                    dve.wait_ge(m_xh, e * 3 + layer + 1)
                    dve.tensor_tensor(xl[layer][:, e, :, :], w[:, e, :, :], xh[layer][:, e, :, :], ALU.subtract
                                      ).then_inc(m_xl, 1)

            def tile_of_experts(j, ahead, first=False):
                for e in range(NE):
                    if e + 1 < NE:
                        hidden_low(j, e + 1, 0)
                    elif ahead:
                        hidden_low(j + 1, 0, 0)
                    if ahead and e == 4:
                        rows_low(j + 1)
                    if e == 0:
                        probabilities(j)
                    if ahead and e == 2:
                        row_moments(j + 1)
                    hidden_low(j, e, 1)
                    if e == 0:
                        top_two(j)
                    if e == 1:
                        routing_weights(j)
                    if e == 0 and not first:
                        add_expert(j - 1, NE - 1)
                    if e == 4:
                        add_biases(j)
                    if ahead:
                        if e == 2:
                            norm_rows(j + 1)
                        if e == 5:
                            logits_low(j + 1)
                    if e >= 1:
                        add_expert(j, e - 1)

            dve.wait_ge(s_acc, SB * (BATCHES + 1))
            sums_of_weights = acc[:, :].rearrange("p (t n) -> p t n", n=ROW)[:, 0:NT, D:ROW]
            mc(dve.tensor_scalar(sums_of_weights, sums_of_weights, 1e-37, None, ALU.max))
            dve.reciprocal(sums_of_weights, sums_of_weights).then_inc(m_rc, 1)
            mc(dve.memset(mw[:, :, 3, :], -1.0))
            weights_low(0)
            dve.wait_ge(m_b, 48)
            for s in range(MT):
                mc.issue(dve.tensor_tensor(mb[:, s, :], mb[:, s, :], rows[0:P, G2, :], ALU.mult))
            for s in range(MT):
                mc.issue(dve.tensor_tensor(mx[:, s, :], mx[:, s, :], mq[:, s, :], ALU.add))
            mc.wait()
            for s in range(MT):
                mc.issue(dve.tensor_tensor(mb[:, s, :], mb[:, s, :], rows[0:P, E2, :], ALU.add))
            mc.wait()
            for s in range(MT):
                dve.tensor_tensor(mx[:, s, :], mx[:, s, :], mb[:, s, :], ALU.add).then_inc(m_bs, 1)
            for e in range(1, 4):
                weights_low(e)
            row_moments(0)
            norm_rows(0)
            weights_low(4)
            rows_low(0)
            logits_low(0)
            weights_low(5)
            hidden_low(0, 0, 0)
            before = mc.n
            tile_of_experts(0, True, first=True)
            links = mc.n - before
            with dve.Fori(1, NJ - 1) as j:
                mc.start(before + j * links)
                tile_of_experts(j, True)
            mc.start(before + (NJ - 1) * links)
            tile_of_experts(NJ - 1, False)
            add_expert(NJ - 1, NE - 1)

        @block.tensor
        def _(pe):
            pe.wait_ge(s_vconst, 1)
            pe.wait_ge(s_const, 5)
            pe.wait_ge(s_tab, WEXT_LINKS)

            def block_T(r, v, u):
                t = r * AU + u
                pe.wait_ge(s_xn, t + 1)
                past(pe, s_xte, t - 1 if u >= 2 else r * AU)
                for c in range(2):
                    last = pe.transpose(bank[4 + u % 2][:, c * P:(c + 1) * P], xn[:, v, u, c * 128:(c + 1) * 128],
                                        ident[0:P, 0:P])
                last.then_inc(s_xt[v], 1)

            def first_round(i, v):
                r = i * 2 + v
                block_T(r, v, 0)
                for u in range(AU):
                    t = r * AU + u
                    if u + 1 < AU:
                        block_T(r, v, u + 1)
                    pe.wait_ge(s_xte, t + 1)
                    past(pe, s_fe, t - 1 if u >= 2 else r * AU)
                    for c in range(2):
                        last = pe.matmul(bank[6 + u % 2][0:P, 0:ROW + H], xT[:, v, u, c * P:(c + 1) * P],
                                         wext[:, c, :], start=(c == 0), stop=(c == 1))
                    last.then_inc(s_f, 1)

            def edges_T(c):
                pe.wait_ge(s_tf, c + 1)
                if c >= 2:
                    pe.wait_ge(s_tc, c - 1)
                for n, rows_ in enumerate((sf, df)):
                    for u in range(PAIR):
                        q = n * PAIR + u
                        last = pe.transpose(bank[2 + c % 2][:, q * 128:(q + 1) * 128],
                                            rows_[:, c % 2, u * TE:(u + 1) * TE], ident[:, :])
                last.then_inc(s_tt, 1)

            first_round(0, 0)
            pe.wait_ge(s_pos, 1)
            for b in range(2):
                last = pe.matmul(bank[b][:, 0:HALF], ones[0:1, :], pos[:, 0, b * HALF:(b + 1) * HALF],
                                 start=True, stop=True)
            last.then_inc(s_tpe, 1)
            first_round(0, 1)
            with pe.Fori(1, (AR - CHUNK_ROUNDS) // 2) as i:
                for v in range(2):
                    first_round(i, v)
            for c in range(CHUNK_ROUNDS):
                r = AR - CHUNK_ROUNDS + c
                first_round(r // 2, r % 2)
                edges_T(c)
            for c in range(CHUNK_ROUNDS, CH):
                edges_T(c)

            pe.wait_ge(s_gm, 1)
            pe.transpose(bank[2][0:H, 0:P], gmax[0:P, 0:H], ident[0:P, 0:P]).then_inc(s_gm, 1)
            pe.wait_ge(s_gm, 3)
            pe.matmul(bank[2][0:P, 256:256 + H], ones[0:H, 0:P], gmax[0:H, 8:8 + H], start=True, stop=True
                      ).then_inc(s_gm, 1)

            def transposes(n, ring):
                pe.wait_ge(s_S, n + 1)
                for j in range(BATCH):
                    last = pe.transpose(bank[0][0:P, j * TE:(j + 1) * TE], S[:, ring, j, :], ident[:, :])
                last.then_inc(s_st, 1)

            def packed(pair):
                return pe.value_load(pack[0:1, 1, ds(pair, 1)], min_val=0, max_val=PACK ** 4 - 1)

            def logits(n, par, blocks):
                pe.wait_ge(s_ste, n + 1)
                for q, at_node in enumerate(blocks):
                    for j in range(q * PAIR, (q + 1) * PAIR):
                        for part in range(3):
                            last = pe.matmul(bank[1][:, j * 2 * H:(j + 1) * 2 * H],
                                             ST[0:P, par, j * TE:(j + 1) * TE],
                                             nodep[:, part, ds(at_node, 2 * H)],
                                             start=(part == 0), stop=(part == 2))
                last.then_inc(s_er, 1)

            ahead = {}

            def edges(k, bt, last=False, beside=()):
                n = k * BODY + bt
                if not last or bt + 1 < BODY:
                    now = packed(k * 2) if bt == 0 else ahead[0]
                    at_nodes = [pe.snap(unpack(now, (bt + 1) % 2 * SB + q) * (2 * H)) for q in range(SB)]
                    pe.wait_ge(s_arg, n + 1)
                    logits(n + 1, (bt + 1) % 2, at_nodes)
                if not last or bt + 2 < BODY:
                    pe.wait_ge(s_ste, n + 2)
                    transposes(n + 2, (bt + 2) % BODY)
                for product, *which in beside:
                    product(*which)
                if bt == 0 or (bt == 2 and not last):
                    ahead[0] = packed(k * 2 + bt // 2 + 1)
                pe.wait_ge(s_msg, n + 1)
                for q in range(SB):
                    pe.wait_ge(s_acc, n * SB + q + 1)
                    for u in range(PAIR):
                        j = q * PAIR + u
                        done = pe.matmul(bank[2 + q][0:P, 0:ROW], S[:, bt, j, :], G[:, bt * BATCH + j, :],
                                         start=(u == 0), stop=(u == PAIR - 1))
                    done.then_inc(s_sum, 1)

            pe.wait_ge(s_nt, 1)
            transposes(0, 0)
            pe.wait_ge(s_blk, 32)
            pe.wait_ge(s_pack, 7)
            blocks_0 = packed(0)
            logits(0, 0, [unpack(blocks_0, q) * (2 * H) for q in range(SB)])
            pe.wait_ge(s_ste, 1)
            transposes(1, 1)
            for q in range(SB):
                pe.matmul(bank[2 + q][0:P, 0:ROW], zero[:, 0:P], zero[:, :], start=True, stop=True
                          ).then_inc(s_sum, 1)

            pe.wait_ge(s_kload, 16 * KLOADS)
            for c in range(2):
                pe.matmul(bank[5 + c][:, 0:129], zero[:, 0:128], zero[:, 0:129], start=True, stop=False)

            def keys_values(i, u):
                pe.wait_ge(s_kx[u], (i + 1) * 16)
                pe.wait_ge(s_km, i * 2 + u)
                for c in range(2):
                    last = pe.matmul(bank[4][0:P, :], xm[:, u, c * P:(c + 1) * P], wkv[:, c, :],
                                     start=(c == 0), stop=(c == 1))
                last.then_inc(s_kmm[u], 1)

            def add_kv(i, u):
                pe.wait_ge(s_kp, i * 2 + u + 1)
                for c in range(2):
                    last = pe.matmul(bank[5 + c][:, 0:129], kb[:, u, c * 128:(c + 1) * 128], vb[:, u, c, :],
                                     start=False, stop=False)
                last.then_inc(s_ka[u], 1)

            with pe.Fori(0, KV_ROUNDS) as i:
                edges(i, 0, beside=[(keys_values, i, 0)])
                edges(i, 1, beside=[(add_kv, i, 0)])
                edges(i, 2, beside=[(keys_values, i, 1)])
                edges(i, 3, beside=[(add_kv, i, 1)])
            for c in range(2):
                last = pe.matmul(bank[5 + c][:, 0:129], zero[:, 0:128], zero[:, 0:129], start=False, stop=True)
            last.then_inc(s_kv, 1)

            def queries(m):
                pe.wait_ge(s_xm, (m + 1) * 16)
                past(pe, s_h, m * 2 - 4)
                for o in range(2):
                    for c in range(2):
                        last = pe.matmul(bank[7][:, o * P:(o + 1) * P], wq[:, c, o * 128:(o + 1) * 128],
                                         xm[:, 0, c * P:(c + 1) * P], start=(c == 0), stop=(c == 1))
                last.then_inc(s_pq, 1)

            def attend(m):
                pe.wait_ge(s_qp, m + 1)
                past(pe, s_res, m)
                for c in range(2):
                    last = pe.matmul(bank[5][0:P, c * (128 + H):(c + 1) * (128 + H)], qb[:, c, :], kvbd[:, c, :],
                                     start=True, stop=True)
                last.then_inc(s_pa, 1)

            def attention_T(m):
                pe.wait_ge(s_at, m + 1)
                past(pe, s_yT, m)
                for c in range(2):
                    last = pe.transpose(bank[4][:, c * P:(c + 1) * P], at[:, c * 128:(c + 1) * 128],
                                        ident[0:P, 0:P])
                last.then_inc(s_pT, 1)

            def project(m):
                pe.wait_ge(s_aT, m + 1)
                for c in range(2):
                    pe.matmul(bank[5][0:P, 0:D], aT[:, c, :], wo[:, c, :], start=(c == 0), stop=False)
                last = pe.matmul(bank[5][0:P, 0:D], ones[0:1, 0:P], rows[0:1, BO, :], start=False, stop=True)
                last.then_inc(s_po, 1)

            def norm_T(m):
                pe.wait_ge(s_y, m + 1)
                for c in range(2):
                    last = pe.transpose(bank[4][:, c * P:(c + 1) * P], y[:, 0, c * 128:(c + 1) * 128],
                                        ident[0:P, 0:P])
                last.then_inc(s_fy, 1)

            def hidden(m, half, newest):
                pe.wait_ge(s_yT, m + 1)
                if half == 0:
                    past(pe, s_r2, m)
                elif newest is not None:
                    pe.wait_ge(s_qb, newest + 1)
                for c4 in range(4):
                    f = (half * 4 + c4) * 128
                    for c in range(2):
                        last = pe.matmul(bank[6 + half][:, c4 * P:(c4 + 1) * P], w1[:, c, f:f + 128], yT[:, c, :],
                                         start=(c == 0), stop=(c == 1))
                last.then_inc(s_fh, 1)

            def second_layer(m, half):
                pe.wait_ge(s_h, m * 2 + half + 1)
                for f in range(half * 4, half * 4 + 4):
                    last = pe.matmul(bank[6][0:P, 0:D], hT[:, f, :], w2[:, f, :], start=(f == 0), stop=False)
                if half:
                    last = pe.matmul(bank[6][0:P, 0:D], ones[0:1, 0:P], rows[0:1, B2, :], start=False, stop=True)
                last.then_inc(s_fw if half else s_fa, 1)

            def two_passes(triple):
                for half in range(2):
                    i = triple * 2 + half
                    blocks = active(i)
                    beside = [[] for _ in range(PASS)]
                    if 0 in blocks:
                        beside[0] += [(queries, i)]
                    if 1 in blocks:
                        beside[0] += [(attention_T, i - 1)]
                        beside[1] += [(project, i - 1)]
                    if 2 in blocks:
                        beside[2] += [(hidden, i - 2, 0, None)]
                        beside[3] += [(hidden, i - 2, 1, i if 0 in blocks else None)]
                    if 0 in blocks:
                        beside[3] += [(attend, i)]
                    if 2 in blocks:
                        beside[4] += [(second_layer, i - 2, 0)]
                    if 1 in blocks:
                        beside[4] += [(norm_T, i - 1)]
                    if 2 in blocks:
                        beside[5] += [(second_layer, i - 2, 1)]
                    for s in range(PASS):
                        edges(*mixer_batch(triple, half, s), beside=beside[s])

            pe.wait_ge(s_kbd, 1)
            pe.wait_ge(s_wload, 16 * WLOADS)
            for triple in range(2):
                two_passes(triple)
            with pe.Fori(2, NT // 2) as triple:
                two_passes(triple)
            for triple in range(NT // 2, TRIPLES):
                two_passes(triple)
            for bt in range(BODY):
                edges(ROUNDS - 1, bt, last=True)

            def rows_T(j):
                pe.wait_ge(m_f, j + 1)
                past(pe, m_c, j)
                for s in range(MT):
                    for c in range(2):
                        last = pe.transpose(bank[0][:, c * MT * P + s * P:c * MT * P + (s + 1) * P],
                                            mn[:, s, c * 128:(c + 1) * 128], ident[0:P, 0:P])
                last.then_inc(m_fT, 1)

            def router_1(j):
                pe.wait_ge(m_fe, j + 1)
                for c in range(2):
                    last = pe.matmul(bank[1][:, 0:MT * P], r1[:, c, :], mfT[:, c, :], start=(c == 0), stop=(c == 1))
                last.then_inc(m_r, 1)

            def router_2(j):
                pe.wait_ge(m_rr, j + 1)
                past(pe, m_we, j)
                for s in range(MT):
                    last = pe.matmul(bank[2][0:P, s * 8:s * 8 + NE], mrh[:, s * P:(s + 1) * P], r2[:, :],
                                     start=True, stop=True)
                last.then_inc(m_l, 1)

            def weights_T(j):
                pe.wait_ge(m_wt, j + 1)
                for s in range(MT):
                    last = pe.transpose(bank[2][0:NE, 128 + s * P:128 + (s + 1) * P], wt[:, s, :],
                                        ident[0:P, 0:P])
                last.then_inc(m_wT, 1)

            def biases(j):
                pe.wait_ge(m_we, j + 1)
                past(pe, m_s, j)
                for s in range(MT):
                    last = pe.matmul(bank[7][0:P, s * D:(s + 1) * D], wtT[:, s, :], e3b[:, :], start=True, stop=True)
                last.then_inc(m_bb, 1)

            def hidden_layer(out_bank, w, e, parts, low, low_count, done):
                pe.wait_ge(low, low_count)
                products = [(p, part, c) for p, part in ((xh[w], 0), (xl[w], 0), (xh[w], 1)) for c in range(2)]
                for o in range(2):
                    for n, (p, part, c) in enumerate(products):
                        last = pe.matmul(bank[out_bank][:, o * MT * P:(o + 1) * MT * P],
                                         p[:, e, c, o * 128:(o + 1) * 128], parts[:, part, c, :],
                                         start=(n == 0), stop=(n == len(products) - 1))
                last.then_inc(done, 1)

            def layer_1(j, e):
                pe.wait_ge(m_c, j + 1)
                past(pe, m_h1r, j * NE + e)
                hidden_layer(3, 0, e, ms, m_cl, j + 1, m_h1)

            def layer_2(j, e):
                pe.wait_ge(m_h1r, j * NE + e + 1)
                past(pe, m_h2r, j * NE + e)
                hidden_layer(4, 1, e, hs[:, 0, e % 2, :, :, :], m_h1l, j * NE + e + 1, m_h2)

            def layer_3(j, e):
                pe.wait_ge(m_h2r, j * NE + e + 1)
                pe.wait_ge(m_h2l, j * NE + e + 1)
                past(pe, m_oa, (j * NE + e - 1) * MT)
                for s in range(MT):
                    products = [(w, part, c) for w, part in ((xh[2], 0), (xl[2], 0), (xh[2], 1)) for c in range(2)]
                    for n, (w, part, c) in enumerate(products):
                        last = pe.matmul(bank[5 + e % 2][0:P, s * D:(s + 1) * D], hs[:, 1, e % 2, part, c, s * P:(s + 1) * P],
                                         w[:, e, c, :], start=(n == 0), stop=(n == len(products) - 1))
                last.then_inc(m_o, 1)

            def tile_of_experts(j, ahead, first=False):
                for e in range(NE):
                    if first and 4 <= e + 1 < NE:
                        pe.wait_ge(m_xl, 3 * (e + 2))
                    if e + 1 < NE:
                        layer_1(j, e + 1)
                    elif ahead:
                        layer_1(j + 1, 0)
                    layer_2(j, e)
                    if ahead and e == 3:
                        rows_T(j + 1)
                    if e == 3:
                        biases(j)
                    if e >= 1:
                        layer_3(j, e - 1)
                    elif not first:
                        layer_3(j - 1, NE - 1)
                    if e == 2:
                        weights_T(j)
                    if ahead:
                        if e == 3:
                            router_1(j + 1)
                        if e == 4:
                            router_2(j + 1)

            pe.wait_ge(s_os, 16 * NT)
            rows_T(0)
            router_1(0)
            router_2(0)
            pe.wait_ge(m_xl, 3 * 4)
            layer_1(0, 0)
            tile_of_experts(0, True, first=True)
            with pe.Fori(1, NJ - 1) as j:
                tile_of_experts(j, True)
            tile_of_experts(NJ - 1, False)
            layer_3(NJ - 1, NE - 1)


_INS = ['x', 'src', 'dst', 'L0_gnn_W', 'L0_gnn_attn_l', 'L0_gnn_attn_r', 'L0_gnn_bias', 'L0_mix_Wq', 'L0_mix_bq',
        'L0_mix_Wk', 'L0_mix_bk', 'L0_mix_Wv', 'L0_mix_bv', 'L0_mix_Wo', 'L0_mix_bo', 'L0_mix_W1', 'L0_mix_b1',
        'L0_mix_W2', 'L0_mix_b2', 'L0_mix_ln1_g', 'L0_mix_ln1_b', 'L0_mix_ln2_g', 'L0_mix_ln2_b',
        'L0_ffn_router_w1', 'L0_ffn_router_b1', 'L0_ffn_router_w2', 'L0_ffn_router_b2', 'L0_ffn_expert_w1',
        'L0_ffn_expert_b1', 'L0_ffn_expert_w2', 'L0_ffn_expert_b2', 'L0_ffn_expert_w3', 'L0_ffn_expert_b3']


def kernel(**inputs):
    import numpy as np
    import concourse.bacc as bacc
    from concourse import mybir as _mybir
    from concourse.bass_utils import run_bass_kernel_spmd

    nc = bacc.Bacc("TRN2", target_bir_lowering=False, num_devices=1)
    arrays, args = {}, []
    for name in _INS:
        a = np.ascontiguousarray(inputs[name])
        if name in ('src', 'dst'):
            pad = np.full(EPAD - E, 0 if name == 'src' else N, a.dtype)
            a = np.concatenate([a, pad])
        arrays[f"in_{name}"] = a
        args.append(nc.dram_tensor(f"in_{name}", a.shape, _mybir.dt.from_np(a.dtype), kind="ExternalInput").ap())
    args.append(nc.dram_tensor("out_x", (N, D), _mybir.dt.float32, kind="ExternalOutput").ap())
    gps_layer(nc, *args)
    r = run_bass_kernel_spmd(nc, [arrays], core_ids=[0])
    return r.results[0]["out_x"]
```
